# Optimizing a Trainium2 kernel written in Bass

```python
import numpy as np
import jax
import jax.numpy as jnp

def _softmax(x, axis=-1):
    return jax.nn.softmax(x, axis=axis)

def _gelu(x):
    return jax.nn.gelu(x, approximate=True)

def _silu(x):
    return jax.nn.silu(x)

def _sigmoid(x):
    return jax.nn.sigmoid(x)

def _layernorm(x, axis=-1, eps=1e-05):
    m = jnp.mean(x, axis=axis, keepdims=True)
    v = jnp.var(x, axis=axis, keepdims=True)
    return (x - m) / jnp.sqrt(v + eps)

def _scatter_add(tgt, idx, src, axis=0):
    return tgt.at[idx].add(src)

def _segment_sum(src, seg, n):
    return jax.ops.segment_sum(src, seg, n)
kernel_name = 'mk_gnn_ffn_d2_gnn_r32_19dfad'

def setup_inputs(seed: int=0):
    np.random.seed(seed)
    _w = jnp.asarray

    def _rec_inputs():
        import jax
        import jax.numpy as jnp
        _gk = jax.random.key(seed)
        x = -8.776e-05 + 1 * jax.random.normal(jax.random.fold_in(_gk, 1), (3125, 256), jnp.float32)
        _s = jax.random.randint(jax.random.fold_in(_gk, 2), (25000,), 0, 3125, jnp.int32)
        _d = jax.random.randint(jax.random.fold_in(_gk, 3), (25000,), 0, 3125, jnp.int32)
        _loop = jnp.arange(3125, dtype=jnp.int32)
        src = jnp.concatenate([_s, _d, _loop])
        dst = jnp.concatenate([_d, _s, _loop])
        _o = jnp.argsort(dst, stable=True)
        src = src[_o]
        dst = dst[_o]
        return (x, src, dst)
    x, src, dst = _rec_inputs()

    def _L0_gnn_setup():
        import jax, jax.numpy as jnp
        import numpy as np
        N, E, HID, H = (625, 10000, 256, 4)
        C = HID // H

        def _layernorm(x, w, b, eps=1e-05):
            mu = jnp.mean(x, axis=-1, keepdims=True)
            var = jnp.mean((x - mu) ** 2, axis=-1, keepdims=True)
            return (x - mu) / jnp.sqrt(var + eps) * w + b

        def _hybrid_block(x, edge_index, ln1_w, ln1_b, wq, bq, wk, bk, wv, bv, wskip, bskip, ln2_w, ln2_b, w1, b1, w2, b2):
            n = x.shape[0]
            src, dst = (edge_index[0], edge_index[1])
            h = _layernorm(x, ln1_w, ln1_b)
            q = (h @ wq + bq).reshape(n, H, C)
            k = (h @ wk + bk).reshape(n, H, C)
            v = (h @ wv + bv).reshape(n, H, C)
            scores = jnp.sum(q[dst] * k[src], axis=-1) / jnp.sqrt(jnp.asarray(C, x.dtype))
            m = jax.ops.segment_max(scores, dst, num_segments=n)
            m = jnp.where(jnp.isfinite(m), m, 0.0)
            e = jnp.exp(scores - m[dst])
            den = jax.ops.segment_sum(e, dst, num_segments=n)
            attn = e / den[dst]
            agg = jax.ops.segment_sum(attn[:, :, None] * v[src], dst, num_segments=n)
            conv = agg.reshape(n, H * C) + (h @ wskip + bskip)
            x = x + conv
            h2 = _layernorm(x, ln2_w, ln2_b)
            ff = jax.nn.gelu(h2 @ w1 + b1, approximate=False) @ w2 + b2
            return x + ff
        key = jax.random.key(seed)
        ks = jax.random.split(key, 12)
        s = 0.02
        inp = {'x': jax.random.normal(ks[0], (N, HID), jnp.float32), 'edge_index': jax.random.randint(ks[1], (2, E), 0, N, jnp.int64), 'ln1_w': jnp.ones((HID,), jnp.float32), 'ln1_b': jnp.zeros((HID,), jnp.float32), 'ln2_w': jnp.ones((HID,), jnp.float32), 'ln2_b': jnp.zeros((HID,), jnp.float32), 'wq': jax.random.normal(ks[2], (HID, H * C), jnp.float32) * s, 'bq': jnp.zeros((H * C,), jnp.float32), 'wk': jax.random.normal(ks[3], (HID, H * C), jnp.float32) * s, 'bk': jnp.zeros((H * C,), jnp.float32), 'wv': jax.random.normal(ks[4], (HID, H * C), jnp.float32) * s, 'bv': jnp.zeros((H * C,), jnp.float32), 'wskip': jax.random.normal(ks[5], (HID, H * C), jnp.float32) * s, 'bskip': jnp.zeros((H * C,), jnp.float32), 'w1': jax.random.normal(ks[6], (HID, 2 * HID), jnp.float32) * s, 'b1': jnp.zeros((2 * HID,), jnp.float32), 'w2': jax.random.normal(ks[7], (2 * HID, HID), jnp.float32) * s, 'b2': jnp.zeros((HID,), jnp.float32)}
        return inp
    _L0_gnn_all = _L0_gnn_setup()
    _L0_gnn_in = {k: v for k, v in _L0_gnn_all.items() if k in ('ln1_w', 'ln1_b', 'ln2_w', 'ln2_b', 'wq', 'bq', 'wk', 'bk', 'wv', 'bv', 'wskip', 'bskip', 'w1', 'b1', 'w2', 'b2')}
    del _L0_gnn_all

    def _L0_ffn_setup():
        import math
        import jax, jax.numpy as jnp
        import numpy as np
        CAPACITY_FACTOR = 1.25
        TOP_K = 2
        LN_EPS = 1e-05

        def _layer_norm(x, gamma, beta):
            mu = jnp.mean(x, axis=-1, keepdims=True)
            var = jnp.var(x, axis=-1, keepdims=True)
            return (x - mu) * jax.lax.rsqrt(var + LN_EPS) * gamma + beta
        key = jax.random.key(seed)
        ks = jax.random.split(key, 4)
        B, S, D, F, E = (8, 128, 256, 512, 8)
        x = jax.random.normal(ks[0], (B, S, D), dtype=jnp.float32)
        Wr = jax.random.normal(ks[1], (D, E), dtype=jnp.float32) / np.sqrt(D)
        br = jnp.zeros((E,), jnp.float32)
        W1 = jax.random.normal(ks[2], (E, D, F), dtype=jnp.float32) / np.sqrt(D)
        b1 = jnp.zeros((E, F), jnp.float32)
        W2 = jax.random.normal(ks[3], (E, F, D), dtype=jnp.float32) / np.sqrt(F)
        b2 = jnp.zeros((E, D), jnp.float32)
        gamma = jnp.ones((D,), jnp.float32)
        beta = jnp.zeros((D,), jnp.float32)
        return {'x': x, 'Wr': Wr, 'br': br, 'W1': W1, 'b1': b1, 'W2': W2, 'b2': b2, 'gamma': gamma, 'beta': beta}
    _L0_ffn_all = _L0_ffn_setup()
    _L0_ffn_in = {k: v for k, v in _L0_ffn_all.items() if k in ('Wr', 'br', 'W1', 'b1', 'W2', 'b2', 'gamma', 'beta')}
    del _L0_ffn_all

    def _L1_gnn_setup():
        import jax, jax.numpy as jnp
        import numpy as np
        N_NODES = 3125
        F_DIM = 256
        NNZ = 50000

        def _prelu(x, a):
            return jnp.where(x >= 0, x, a * x)

        def _hconv(x, W, b, src, dst, n):
            xt = x @ W
            ones = jnp.ones(src.shape, xt.dtype)
            D = jax.ops.segment_sum(ones, src, num_segments=n)
            B = jax.ops.segment_sum(ones, dst, num_segments=n)
            Dinv = jnp.where(D > 0, 1.0 / D, 0.0)
            Binv = jnp.where(B > 0, 1.0 / B, 0.0)
            m = jax.ops.segment_sum(xt[src], dst, num_segments=n) * Binv[:, None]
            out = jax.ops.segment_sum(m[dst], src, num_segments=n) * Dinv[:, None]
            return out + b
        key = jax.random.key(seed)
        k0, k1, k2, k3 = jax.random.split(key, 4)
        x = jax.random.normal(k0, (N_NODES, F_DIM), dtype=jnp.float32)
        edge_index = jax.random.randint(k1, (2, NNZ), 0, N_NODES, dtype=jnp.int32)
        scale = (2.0 / F_DIM) ** 0.5
        W1 = jax.random.normal(k2, (F_DIM, F_DIM), dtype=jnp.float32) * scale
        W2 = jax.random.normal(k3, (F_DIM, F_DIM), dtype=jnp.float32) * scale
        b1 = jnp.zeros((F_DIM,), jnp.float32)
        b2 = jnp.zeros((F_DIM,), jnp.float32)
        a = jnp.full((1,), 0.25, jnp.float32)
        return {'x': x, 'edge_index': edge_index, 'W1': W1, 'b1': b1, 'W2': W2, 'b2': b2, 'a': a}
    _L1_gnn_all = _L1_gnn_setup()
    _L1_gnn_in = {k: v for k, v in _L1_gnn_all.items() if k in ('W1', 'b1', 'W2', 'b2', 'a')}
    del _L1_gnn_all

    def _L1_ffn_setup():
        import jax, jax.numpy as jnp
        import numpy as np
        TOP_K = 2
        LN_EPS = 1e-05
        key = jax.random.key(seed)
        ks = jax.random.split(key, 8)
        B, S, D, E, H = (16, 1024, 256, 8, 1024)
        x = jax.random.normal(ks[0], (B, S, D), dtype=jnp.float32)
        Wr = jax.random.normal(ks[1], (D, E), dtype=jnp.float32) * 0.1
        br = jnp.zeros((E,), dtype=jnp.float32)
        ln_g = jnp.ones((E, D), dtype=jnp.float32)
        ln_b = jnp.zeros((E, D), dtype=jnp.float32)
        W1 = jax.random.normal(ks[2], (E, D, H), dtype=jnp.float32) * (1.0 / np.sqrt(D))
        b1 = jnp.zeros((E, H), dtype=jnp.float32)
        W2 = jax.random.normal(ks[3], (E, H, D), dtype=jnp.float32) * (1.0 / np.sqrt(H))
        b2 = jnp.zeros((E, D), dtype=jnp.float32)
        return {'x': x, 'Wr': Wr, 'br': br, 'ln_g': ln_g, 'ln_b': ln_b, 'W1': W1, 'b1': b1, 'W2': W2, 'b2': b2}
    _L1_ffn_all = _L1_ffn_setup()
    _L1_ffn_in = {k: v for k, v in _L1_ffn_all.items() if k in ('Wr', 'br', 'ln_g', 'ln_b', 'W1', 'b1', 'W2', 'b2')}
    del _L1_ffn_all
    return {'x': x, 'src': src, 'dst': dst, 'L0_gnn_ln1_w': _L0_gnn_in['ln1_w'], 'L0_gnn_ln1_b': _L0_gnn_in['ln1_b'], 'L0_gnn_ln2_w': _L0_gnn_in['ln2_w'], 'L0_gnn_ln2_b': _L0_gnn_in['ln2_b'], 'L0_gnn_wq': _L0_gnn_in['wq'], 'L0_gnn_bq': _L0_gnn_in['bq'], 'L0_gnn_wk': _L0_gnn_in['wk'], 'L0_gnn_bk': _L0_gnn_in['bk'], 'L0_gnn_wv': _L0_gnn_in['wv'], 'L0_gnn_bv': _L0_gnn_in['bv'], 'L0_gnn_wskip': _L0_gnn_in['wskip'], 'L0_gnn_bskip': _L0_gnn_in['bskip'], 'L0_gnn_w1': _L0_gnn_in['w1'], 'L0_gnn_b1': _L0_gnn_in['b1'], 'L0_gnn_w2': _L0_gnn_in['w2'], 'L0_gnn_b2': _L0_gnn_in['b2'], 'L0_ffn_Wr': _L0_ffn_in['Wr'], 'L0_ffn_br': _L0_ffn_in['br'], 'L0_ffn_W1': _L0_ffn_in['W1'], 'L0_ffn_b1': _L0_ffn_in['b1'], 'L0_ffn_W2': _L0_ffn_in['W2'], 'L0_ffn_b2': _L0_ffn_in['b2'], 'L0_ffn_gamma': _L0_ffn_in['gamma'], 'L0_ffn_beta': _L0_ffn_in['beta'], 'L1_gnn_W1': _L1_gnn_in['W1'], 'L1_gnn_b1': _L1_gnn_in['b1'], 'L1_gnn_W2': _L1_gnn_in['W2'], 'L1_gnn_b2': _L1_gnn_in['b2'], 'L1_gnn_a': _L1_gnn_in['a'], 'L1_ffn_Wr': _L1_ffn_in['Wr'], 'L1_ffn_br': _L1_ffn_in['br'], 'L1_ffn_ln_g': _L1_ffn_in['ln_g'], 'L1_ffn_ln_b': _L1_ffn_in['ln_b'], 'L1_ffn_W1': _L1_ffn_in['W1'], 'L1_ffn_b1': _L1_ffn_in['b1'], 'L1_ffn_W2': _L1_ffn_in['W2'], 'L1_ffn_b2': _L1_ffn_in['b2']}

def reference(x, src, dst, L0_gnn_ln1_w, L0_gnn_ln1_b, L0_gnn_ln2_w, L0_gnn_ln2_b, L0_gnn_wq, L0_gnn_bq, L0_gnn_wk, L0_gnn_bk, L0_gnn_wv, L0_gnn_bv, L0_gnn_wskip, L0_gnn_bskip, L0_gnn_w1, L0_gnn_b1, L0_gnn_w2, L0_gnn_b2, L0_ffn_Wr, L0_ffn_br, L0_ffn_W1, L0_ffn_b1, L0_ffn_W2, L0_ffn_b2, L0_ffn_gamma, L0_ffn_beta, L1_gnn_W1, L1_gnn_b1, L1_gnn_W2, L1_gnn_b2, L1_gnn_a, L1_ffn_Wr, L1_ffn_br, L1_ffn_ln_g, L1_ffn_ln_b, L1_ffn_W1, L1_ffn_b1, L1_ffn_W2, L1_ffn_b2):
    import jax
    import jax.numpy as jnp

    def _L0_gnn_ref(x, edge_index, ln1_w, ln1_b, ln2_w, ln2_b, wq, bq, wk, bk, wv, bv, wskip, bskip, w1, b1, w2, b2):
        import jax, jax.numpy as jnp
        import numpy as np
        N, E, HID, H = (625, 10000, 256, 4)
        C = HID // H

        def _layernorm(x, w, b, eps=1e-05):
            mu = jnp.mean(x, axis=-1, keepdims=True)
            var = jnp.mean((x - mu) ** 2, axis=-1, keepdims=True)
            return (x - mu) / jnp.sqrt(var + eps) * w + b

        def _hybrid_block(x, edge_index, ln1_w, ln1_b, wq, bq, wk, bk, wv, bv, wskip, bskip, ln2_w, ln2_b, w1, b1, w2, b2):
            n = x.shape[0]
            src, dst = (edge_index[0], edge_index[1])
            h = _layernorm(x, ln1_w, ln1_b)
            q = (h @ wq + bq).reshape(n, H, C)
            k = (h @ wk + bk).reshape(n, H, C)
            v = (h @ wv + bv).reshape(n, H, C)
            scores = jnp.sum(q[dst] * k[src], axis=-1) / jnp.sqrt(jnp.asarray(C, x.dtype))
            m = jax.ops.segment_max(scores, dst, num_segments=n)
            m = jnp.where(jnp.isfinite(m), m, 0.0)
            e = jnp.exp(scores - m[dst])
            den = jax.ops.segment_sum(e, dst, num_segments=n)
            attn = e / den[dst]
            agg = jax.ops.segment_sum(attn[:, :, None] * v[src], dst, num_segments=n)
            conv = agg.reshape(n, H * C) + (h @ wskip + bskip)
            x = x + conv
            h2 = _layernorm(x, ln2_w, ln2_b)
            ff = jax.nn.gelu(h2 @ w1 + b1, approximate=False) @ w2 + b2
            return x + ff
        return _hybrid_block(x, edge_index, ln1_w, ln1_b, wq, bq, wk, bk, wv, bv, wskip, bskip, ln2_w, ln2_b, w1, b1, w2, b2)

    def _L0_ffn_ref(x, Wr, br, W1, b1, W2, b2, gamma, beta):
        import math
        import jax, jax.numpy as jnp
        import numpy as np
        CAPACITY_FACTOR = 1.25
        TOP_K = 2
        LN_EPS = 1e-05

        def _layer_norm(x, gamma, beta):
            mu = jnp.mean(x, axis=-1, keepdims=True)
            var = jnp.var(x, axis=-1, keepdims=True)
            return (x - mu) * jax.lax.rsqrt(var + LN_EPS) * gamma + beta
        B, S, D = x.shape
        E = Wr.shape[1]
        N = B * S
        K = TOP_K
        logits = jnp.mean(x, axis=1) @ Wr + br
        routing_weights = jax.nn.softmax(logits, axis=-1)
        capacity = float(math.ceil(N * CAPACITY_FACTOR / E))
        expected_loads = routing_weights.sum(axis=0) * (N / B)
        scale = jnp.where(expected_loads > capacity, capacity / expected_loads, 1.0)
        routing_weights = jax.nn.softmax(routing_weights * scale, axis=-1)
        rw_tok = jnp.broadcast_to(routing_weights[:, None, :], (B, S, E)).reshape(N, E)
        top_w, top_i = jax.lax.top_k(rw_tok, K)
        top_w = jax.nn.softmax(top_w, axis=-1)
        xf = x.reshape(N, D)
        h = jax.nn.gelu(jnp.einsum('nd,edf->enf', xf, W1) + b1[:, None, :], approximate=False)
        y = jnp.einsum('enf,efd->end', h, W2) + b2[:, None, :]
        w_dense = jnp.zeros((N, E), x.dtype).at[jnp.arange(N)[:, None], top_i].add(top_w)
        out = jnp.einsum('ne,end->nd', w_dense, y).reshape(B, S, D)
        out = _layer_norm(out + x, gamma, beta)
        return out

    def _L1_gnn_ref(x, edge_index, W1, b1, W2, b2, a):
        import jax, jax.numpy as jnp
        import numpy as np
        N_NODES = 3125
        F_DIM = 256
        NNZ = 50000

        def _prelu(x, a):
            return jnp.where(x >= 0, x, a * x)

        def _hconv(x, W, b, src, dst, n):
            xt = x @ W
            ones = jnp.ones(src.shape, xt.dtype)
            D = jax.ops.segment_sum(ones, src, num_segments=n)
            B = jax.ops.segment_sum(ones, dst, num_segments=n)
            Dinv = jnp.where(D > 0, 1.0 / D, 0.0)
            Binv = jnp.where(B > 0, 1.0 / B, 0.0)
            m = jax.ops.segment_sum(xt[src], dst, num_segments=n) * Binv[:, None]
            out = jax.ops.segment_sum(m[dst], src, num_segments=n) * Dinv[:, None]
            return out + b
        src, dst = (edge_index[0], edge_index[1])
        n = x.shape[0]
        h = _prelu(_hconv(x, W1, b1, src, dst, n), a)
        h = _hconv(h, W2, b2, src, dst, n) + x
        return _prelu(h, a)

    def _L1_ffn_ref(x, Wr, br, ln_g, ln_b, W1, b1, W2, b2):
        import jax, jax.numpy as jnp
        import numpy as np
        TOP_K = 2
        LN_EPS = 1e-05
        B, S, D = x.shape
        N = B * S
        xt = x.reshape(N, D)
        logits = xt @ Wr + br
        probs = jax.nn.softmax(logits, axis=-1)
        top_p, top_idx = jax.lax.top_k(probs, TOP_K)
        weights = top_p / top_p.sum(axis=-1, keepdims=True)
        mu = xt.mean(axis=-1, keepdims=True)
        var = ((xt - mu) ** 2).mean(axis=-1, keepdims=True)
        xn = (xt - mu) * jax.lax.rsqrt(var + LN_EPS)
        xe = xn[None, :, :] * ln_g[:, None, :] + ln_b[:, None, :]
        h = jax.nn.gelu(jnp.einsum('end,edh->enh', xe, W1) + b1[:, None, :], approximate=False)
        y = jnp.einsum('enh,ehd->end', h, W2) + b2[:, None, :]
        y_tok = jnp.transpose(y, (1, 0, 2))
        sel = jnp.take_along_axis(y_tok, top_idx[:, :, None], axis=1)
        out = (weights[:, :, None] * sel).sum(axis=1)
        return out.reshape(B, S, D)
    edge_index = jnp.stack([src, dst])
    x = x + _L0_gnn_ref(_layernorm(x, axis=-1), edge_index, L0_gnn_ln1_w, L0_gnn_ln1_b, L0_gnn_ln2_w, L0_gnn_ln2_b, L0_gnn_wq, L0_gnn_bq, L0_gnn_wk, L0_gnn_bk, L0_gnn_wv, L0_gnn_bv, L0_gnn_wskip, L0_gnn_bskip, L0_gnn_w1, L0_gnn_b1, L0_gnn_w2, L0_gnn_b2)
    x = x + _L0_ffn_ref(_layernorm(x, axis=-1)[None], L0_ffn_Wr, L0_ffn_br, L0_ffn_W1, L0_ffn_b1, L0_ffn_W2, L0_ffn_b2, L0_ffn_gamma, L0_ffn_beta)[0]
    x = x + _L1_gnn_ref(_layernorm(x, axis=-1), edge_index, L1_gnn_W1, L1_gnn_b1, L1_gnn_W2, L1_gnn_b2, L1_gnn_a)
    x = x + _L1_ffn_ref(_layernorm(x, axis=-1)[None], L1_ffn_Wr, L1_ffn_br, L1_ffn_ln_g, L1_ffn_ln_b, L1_ffn_W1, L1_ffn_b1, L1_ffn_W2, L1_ffn_b2)[0]
    return x

_drawn_inputs = setup_inputs


def setup_inputs(seed=0):
    import zlib

    import numpy as np

    out = dict(_drawn_inputs(seed))
    spreads = {'L0_gnn_ln1_w': (1.0, 0.2),
     'L0_gnn_ln1_b': (0.0, 0.287),
     'L0_gnn_ln2_w': (1.0, 0.6),
     'L0_gnn_ln2_b': (0.0, 0.8),
     'L0_gnn_bq': (0.0, 0.8),
     'L0_gnn_bk': (0.0, 2.0),
     'L0_gnn_bv': (0.0, 0.1),
     'L0_gnn_bskip': (0.0, 0.1),
     'L0_gnn_b1': (0.0, 0.432),
     'L0_gnn_b2': (0.0, 0.1),
     'L0_ffn_br': (0.0, 0.8),
     'L0_ffn_b1': (0.0, 0.452),
     'L0_ffn_b2': (0.0, 0.316),
     'L0_ffn_gamma': (1.0, 0.2),
     'L0_ffn_beta': (0.0, 0.1),
     'L1_gnn_b1': (0.0, 0.335),
     'L1_gnn_b2': (0.0, 0.282),
     'L1_ffn_br': (0.0, 0.366),
     'L1_ffn_ln_g': (1.0, 0.2),
     'L1_ffn_ln_b': (0.0, 0.53),
     'L1_ffn_b1': (0.0, 0.553),
     'L1_ffn_b2': (0.0, 0.376)}
    factors = {'L0_gnn_wq': 8.0, 'L0_gnn_wk': 8.0}
    for name, (base, spread) in spreads.items():
        noise = np.random.default_rng([zlib.crc32(name.encode()), seed]).standard_normal(out[name].shape)
        drawn = base * np.exp(spread * noise) if base else spread * noise
        out[name] = jnp.asarray(drawn.astype(out[name].dtype))
    for name, factor in factors.items():
        out[name] = (out[name] * factor).astype(out[name].dtype)
    return out
```

```python
from contextlib import ExitStack
import math
import concourse.bass as bass
from concourse import mybir

F32 = mybir.dt.float32
F16 = mybir.dt.float16
BF16 = mybir.dt.bfloat16
I32 = mybir.dt.int32
ALU = mybir.AluOpType
ACT = mybir.ActivationFunctionType
AX = mybir.AxisListType.X
P = 128
N = 3125
D = 256
KD = D // P
E = 53125
HEADS = 4
C = D // HEADS
NT = (N + P - 1) // P
TAIL = N - (NT - 1) * P
EC = (E + P - 1) // P
RING = 8
ET = ((E + NT * (P - 1)) // P + RING) // RING * RING
EXPERTS = 8
EPS = 1e-5
FAR = 1e30
GT = 5
GROUPS = NT // GT
GW = GT * P
AW = D + HEADS


def at(i, n=1):
    return bass.ds(i, n)


def flat(ap):
    return ap.rearrange("p o d -> p (o d)")


class Scope:
    def __init__(self, nc, ctx, tag):
        self.nc, self.ctx, self.tag = nc, ctx, tag
        self.sems = []
        ctx.callback(self.end)

    def end(self):
        if self.sems:
            self.nc.clear_and_free_semaphores(self.sems)
            self.nc.all_engine_barrier()

    def sb(self, name, shape, dt=F32):
        return self.ctx.enter_context(self.nc.sbuf_tensor(f"{name}_{self.tag}", shape, dt))

    def ps(self, name, shape, dt=F32):
        return self.ctx.enter_context(self.nc.psum_tensor(f"{name}_{self.tag}", shape, dt))

    def sem(self, name):
        self.sems.append(self.nc.alloc_semaphore(f"{name}_{self.tag}"))
        return self.sems[-1]


def chained(dve, sem):
    step = [0]

    def then(ins):
        step[0] += 1
        ins.then_inc(sem, 1)
        dve.wait_ge(sem, step[0])
    return then


def row(dram, n=D):
    return dram.rearrange("(o d) -> o d", o=1).to_broadcast([P, n])


def constants(nc, sc):
    c = {"iota_t": sc.sb("iota_t", [P, ET], F16), "iota_l": sc.sb("iota_l", [P, P], F16),
         "iota_lf": sc.sb("iota_lf", [P, P]), "iota_b": sc.sb("iota_b", [P, NT]), "iota_tf": sc.sb("iota_tf", [1, ET]),
         "iota_e": sc.sb("iota_e", [P, EXPERTS]), "below": sc.sb("below", [P, P]), "ones": sc.sb("ones", [P, P]),
         "real": sc.sb("real", [P, P]), "ident": sc.sb("ident", [P, P]), "ident_b": sc.sb("ident_b", [P, P], BF16),
         "ones_b": sc.sb("ones_b", [P, P], BF16)}
    with ExitStack() as inner:
        filled = Scope(nc, inner, "const").sem("filled")
        block = inner.enter_context(nc.Block())

        @block.gpsimd
        def _(pool):
            for name, n in (("iota_t", ET), ("iota_l", P), ("iota_lf", P), ("iota_b", NT), ("iota_tf", ET)):
                nc.gpsimd.iota(c[name][:, :], [[1, n]], base=0, channel_multiplier=0, allow_small_or_imprecise_dtypes=True)
            nc.gpsimd.iota(c["iota_e"][:, :], [[1, EXPERTS]], base=-EXPERTS, channel_multiplier=0,
                           allow_small_or_imprecise_dtypes=True)
            nc.gpsimd.memset(c["ones_b"][:, :], 1.0).then_inc(filled, 1)
            nc.gpsimd.memset(c["ones"][:, :], 1.0).then_inc(filled, 1)
            pool.wait_ge(filled, 2)
            nc.gpsimd.affine_select(out=c["below"][:, :], in_=c["ones"][:, :], compare_op=ALU.is_gt, fill=0.0, base=0,
                                    pattern=[[1, P]], channel_multiplier=-1)
            nc.gpsimd.affine_select(out=c["real"][:, :], in_=c["ones"][:, :], compare_op=ALU.is_gt, fill=0.0, base=TAIL,
                                    pattern=[[0, P]], channel_multiplier=-1)
            for name, ones in (("ident", "ones"), ("ident_b", "ones_b")):
                nc.gpsimd.affine_select(out=c[name][:, :], in_=c[ones][:, :], compare_op=ALU.is_equal, fill=0.0, base=0,
                                        pattern=[[1, P]], channel_multiplier=-1)
    return c


def load_nodes(nc, x, X):
    with ExitStack() as ctx:
        sc = Scope(nc, ctx, "load")
        cleared, loaded = sc.sem("cleared"), sc.sem("loaded")
        block = ctx.enter_context(nc.Block())

        @block.vector
        def _(dve):
            nc.vector.memset(X[:, NT - 1, :], 0.0).then_inc(cleared, 1)

        @block.sync
        def _(sp):
            sp.dma_start(X[:, 0:NT - 1, :], x[0:(NT - 1) * P, :].rearrange("(b p) d -> p b d", p=P)).then_inc(loaded, 16)
            sp.wait_ge(cleared, 1)
            sp.dma_start(X[0:TAIL, NT - 1, :], x[(NT - 1) * P:N, :]).then_inc(loaded, 16)
            sp.wait_ge(loaded, 32)


def store_nodes(nc, X, out):
    with ExitStack() as ctx:
        stored = Scope(nc, ctx, "store").sem("stored")
        block = ctx.enter_context(nc.Block())

        @block.sync
        def _(sp):
            sp.dma_start(out[0:(NT - 1) * P, :].rearrange("(b p) d -> p b d", p=P), X[:, 0:NT - 1, :]).then_inc(stored, 16)
            sp.dma_start(out[(NT - 1) * P:N, :], X[0:TAIL, NT - 1, :]).then_inc(stored, 16)
            sp.wait_ge(stored, 32)


def sort_edges(nc, tag, key, other, consts, local_of, other_of, bucket_of):
    with ExitStack() as ctx:
        sc = Scope(nc, ctx, tag)
        key_i = sc.sb("key_i", [P, EC], I32)
        oth_i = sc.sb("oth_i", [P, EC], I32)
        tmp_i = sc.sb("tmp_i", [P, EC], I32)
        bucket_f = sc.sb("bucket_f", [P, EC])
        pay = sc.sb("pay", [P, 3, EC])
        member = sc.sb("member", [P, NT, EC])
        running = sc.sb("running", [P, NT, EC])
        zero = sc.sb("zero", [P, 1])
        count = sc.sb("count", [P, NT])
        upto = sc.sb("upto", [P, NT])
        ti = sc.sb("ti", [P, NT], I32)
        tf = sc.sb("tf", [P, NT])
        first = sc.sb("first", [P, NT])
        offset = sc.sb("offset", [P, NT])
        pos_f = sc.sb("pos_f", [P, EC])
        tile_f = sc.sb("tile_f", [P, EC])
        lane_f = sc.sb("lane_f", [P, EC])
        bfl = sc.sb("bfl", [1, ET])
        in_tile = sc.sb("in_tile", [P, 2, ET], F16)
        in_lane = sc.sb("in_lane", [P, 2, 3, P], F16)
        zl = sc.sb("zl", [P, P], F16)
        zr = sc.sb("zr", [P, ET], F16)
        merged = sc.sb("merged", [P, ET])
        begun = running[0:1, :, :].rearrange("p b j -> p (b j)")[:, 0:NT * (ET // 2)].rearrange("p (t b) -> p t b", b=NT)
        ps = [sc.ps(f"sorted{k}", [P, 512]) for k in range(3)]
        ps_before = sc.ps("before", [P, NT])
        ps_total = sc.ps("total", [P, NT])
        loaded, padded, chain = sc.sem("loaded"), sc.sem("padded"), sc.sem("chain")
        counted, summed = sc.sem("counted"), sc.sem("summed")
        onehots, onehots_used = sc.sem("onehots"), sc.sem("onehots_used")
        full = E // EC
        block = ctx.enter_context(nc.Block())

        @block.sync
        def _(sp):
            sp.wait_ge(padded, 2)
            for dram, tile in ((key, key_i), (other, oth_i)):
                sp.dma_start(tile[0:full, :], dram[0:full * EC].rearrange("(p j) -> p j", j=EC)).then_inc(loaded, 16)
                sp.dma_start(tile[full:full + 1, 0:E - full * EC],
                             dram[full * EC:E].rearrange("(p j) -> p j", p=1)).then_inc(loaded, 16)

        @block.vector
        def _(dve):
            then = chained(dve, chain)
            nc.vector.memset(key_i[:, :], NT * P).then_inc(padded, 1)
            nc.vector.memset(oth_i[:, :], 0).then_inc(padded, 1)
            nc.vector.memset(zero[:, :], 0.0)
            nc.vector.memset(other_of[:, ET:], 0)
            nc.vector.memset(zl[:, :], 0.0)
            then(nc.vector.memset(zr[:, :], 0.0))
            dve.wait_ge(loaded, 64)
            then(nc.vector.tensor_scalar(tmp_i[:, :], key_i[:, :], 7, None, ALU.arith_shift_right))
            then(nc.vector.tensor_copy(bucket_f[:, :], tmp_i[:, :]))
            then(nc.vector.tensor_scalar(tmp_i[:, :], key_i[:, :], P - 1, None, ALU.bitwise_and))
            then(nc.vector.tensor_scalar(pay[:, 0, :], tmp_i[:, :], 1.0, None, ALU.add))
            then(nc.vector.tensor_scalar(tmp_i[:, :], oth_i[:, :], 6, None, ALU.arith_shift_right))
            then(nc.vector.tensor_copy(pay[:, 1, :], tmp_i[:, :]))
            then(nc.vector.tensor_scalar(tmp_i[:, :], oth_i[:, :], 63, None, ALU.bitwise_and))
            then(nc.vector.tensor_copy(pay[:, 2, :], tmp_i[:, :]))
            then(nc.vector.tensor_tensor(member[:, :, :], bucket_f[:, None, :].to_broadcast([P, NT, EC]),
                                         consts["iota_b"][:, :, None].to_broadcast([P, NT, EC]), ALU.is_equal))
            then(nc.vector.tensor_tensor_scan(running[:, :, :].rearrange("p b j -> p (b j)"),
                                              member[:, :, :].rearrange("p b j -> p (b j)"),
                                              zero[:, 0:1].to_broadcast([P, NT * EC]), 0.0, ALU.add, ALU.add))
            then(nc.vector.tensor_copy(upto[:, :], running[:, :, EC - 1]))
            then(nc.vector.tensor_copy(count[:, 0:1], upto[:, 0:1]))
            nc.vector.tensor_tensor(count[:, 1:NT], upto[:, 1:NT], upto[:, 0:NT - 1], ALU.subtract).then_inc(counted, 1)
            dve.wait_ge(summed, 1)
            then(nc.vector.tensor_scalar(ti[:, :], ps_total[:, :], float(P - 1), None, ALU.add))
            then(nc.vector.tensor_scalar(ti[:, :], ti[:, :], 7, None, ALU.arith_shift_right))
            then(nc.vector.tensor_copy(tf[:, :], ti[:, :]))
            then(nc.vector.tensor_tensor_scan(first[:, :], tf[:, :], zero[:, 0:1].to_broadcast([P, NT]), 0.0,
                                              ALU.add, ALU.add))
            then(nc.vector.tensor_tensor(first[:, :], first[:, :], tf[:, :], ALU.subtract))
            then(nc.vector.scalar_tensor_tensor(out=offset[:, :], in0=first[:, :], scalar=float(P), in1=ps_before[:, :],
                                                op0=ALU.mult, op1=ALU.add))
            then(nc.vector.tensor_tensor(offset[:, 1:NT], offset[:, 1:NT], upto[:, 0:NT - 1], ALU.subtract))
            then(nc.vector.tensor_tensor(running[:, :, :], running[:, :, :],
                                         offset[:, :, None].to_broadcast([P, NT, EC]), ALU.add))
            then(nc.vector.tensor_tensor(running[:, :, :], running[:, :, :], member[:, :, :], ALU.mult))
            then(nc.vector.tensor_reduce(pos_f[:, :], running[:, :, :].rearrange("p b j -> p j b"), AX, ALU.add))
            then(nc.vector.tensor_scalar(key_i[:, :], pos_f[:, :], -1.0, None, ALU.add))
            then(nc.vector.tensor_scalar(tmp_i[:, :], key_i[:, :], 7, None, ALU.arith_shift_right))
            then(nc.vector.tensor_copy(tile_f[:, :], tmp_i[:, :]))
            then(nc.vector.tensor_scalar(tmp_i[:, :], key_i[:, :], P - 1, None, ALU.bitwise_and))
            then(nc.vector.tensor_copy(lane_f[:, :], tmp_i[:, :]))
            half = ET // 2
            for h in range(2):
                then(nc.vector.tensor_tensor(begun, consts["iota_tf"][0:1, h * half:(h + 1) * half, None].to_broadcast([1, half, NT]),
                                             first[0:1, None, :].to_broadcast([1, half, NT]), ALU.is_ge))
                then(nc.vector.tensor_reduce(bfl[:, h * half:(h + 1) * half], begun, AX, ALU.add))
            then(nc.vector.tensor_scalar(bucket_of[:, :], bfl[:, :], -1.0, None, ALU.add))
            nc.vector.sem_inc(onehots_used, 2)
            with dve.Fori(0, EC // 2) as i:
                for u in range(2):
                    j = i * 2 + u
                    dve.wait_ge(onehots_used, j + 1)
                    nc.vector.tensor_scalar(in_tile[:, u, :], consts["iota_t"][:, :], tile_f[:, at(j)], None,
                                            ALU.is_equal).then_inc(onehots, 1)
                    for k in range(3):
                        nc.vector.tensor_scalar(in_lane[:, u, k, :], consts["iota_l"][:, :], lane_f[:, at(j)],
                                                pay[:, k, at(j)], ALU.is_equal, ALU.mult).then_inc(onehots, 1)
            dve.wait_ge(onehots_used, EC + 2)
            then(nc.vector.tensor_scalar(local_of[:, :], ps[0][:, 0:ET], -1.0, None, ALU.add))
            then(nc.vector.tensor_copy(merged[:, :], ps[2][:, 0:ET]))
            then(nc.vector.scalar_tensor_tensor(out=other_of[:, 0:ET], in0=ps[1][:, 0:ET], scalar=64.0, in1=merged[:, :],
                                                op0=ALU.mult, op1=ALU.add))

        @block.tensor
        def _(pe):
            pe.wait_ge(counted, 1)
            nc.tensor.matmul(ps_before[:, :], consts["below"][:, :], count[:, :], start=True, stop=True)
            nc.tensor.matmul(ps_total[:, :], consts["ones"][:, :], count[:, :], start=True, stop=True).then_inc(summed, 1)
            for k in range(3):
                nc.tensor.matmul(ps[k][:, 0:ET], zl[:, :], zr[:, :], start=True, stop=False, skip_group_check=True)
            with pe.Fori(0, EC // 2) as i:
                for u in range(2):
                    pe.wait_ge(onehots, i * 8 + (4 * u + 4))
                    for k in range(3):
                        mm = nc.tensor.matmul(ps[k][:, 0:ET], in_lane[:, u, k, :], in_tile[:, u, :],
                                              start=False, stop=False, skip_group_check=True)
                    mm.then_inc(onehots_used, 1)


def layer_norm(nc, tag, src, dst, gamma=None, beta=None, add_to=None):
    with ExitStack() as ctx:
        sc = Scope(nc, ctx, tag)
        stats = sc.sb("stats", [P, NT, 6])
        moments = sc.sb("moments", [P, NT, 2])
        rstd = sc.sb("rstd", [P, NT])
        eps = sc.sb("eps", [P, 1])
        g_row = sc.sb("g_row", [P, D])
        b_row = sc.sb("b_row", [P, D])
        loaded, chain, deviated = sc.sem("loaded"), sc.sem("chain"), sc.sem("deviated")
        stats_done, aggregated, scaled = sc.sem("stats_done"), sc.sem("aggregated"), sc.sem("scaled")
        block = ctx.enter_context(nc.Block())

        @block.sync
        def _(sp):
            if gamma is not None:
                sp.dma_start(g_row[:, :], row(gamma)).then_inc(loaded, 16)
                sp.dma_start(b_row[:, :], row(beta)).then_inc(loaded, 16)

        @block.scalar
        def _(act):
            act.wait_ge(aggregated, NT + 1)
            nc.scalar.activation(rstd[:, :], moments[:, :, 1], ACT.Sqrt, bias=eps[:, 0:1]).then_inc(deviated, 1)

        @block.vector
        def _(dve):
            nc.vector.memset(eps[:, :], EPS).then_inc(aggregated, 1)
            with dve.Fori(0, NT) as t:
                nc.vector.bn_stats(flat(stats[:, at(t), :]), flat(src[:, at(t), :])).then_inc(stats_done, 1)
            dve.wait_ge(stats_done, NT)
            for t in range(NT):
                nc.vector.bn_aggr(moments[:, t, :], stats[:, t, :]).then_inc(aggregated, 1)
            then = chained(dve, chain)
            dve.wait_ge(deviated, 1)
            then(nc.vector.reciprocal(rstd[:, :], rstd[:, :]))
            with dve.Fori(0, NT) as t:
                nc.vector.tensor_scalar(flat(dst[:, at(t), :]), flat(src[:, at(t), :]),
                                        flat(moments[:, at(t), 0:1]), rstd[:, at(t)],
                                        ALU.subtract, ALU.mult).then_inc(scaled, 1)
            dve.wait_ge(scaled, NT)
            if gamma is not None:
                dve.wait_ge(loaded, 32)
                then(nc.vector.tensor_tensor(dst[:, :, :], dst[:, :, :], g_row[:, None, :].to_broadcast([P, NT, D]), ALU.mult))
                then(nc.vector.tensor_tensor(dst[:, :, :], dst[:, :, :], b_row[:, None, :].to_broadcast([P, NT, D]), ALU.add))
            if add_to is not None:
                then(nc.vector.tensor_tensor(add_to[:, :, :], add_to[:, :, :], dst[:, :, :], ALU.add))


def in_pairs(eng, body):
    with eng.Fori(0, NT // 2) as i:
        body(i * 2, 2)
    if NT % 2:
        body(NT - 1, 1)


def small_phase(nc, tag, row_dram, work):
    with ExitStack() as ctx:
        sc = Scope(nc, ctx, tag)
        r = sc.sb("r", [P, D])
        loaded, chain = sc.sem("loaded"), sc.sem("chain")
        block = ctx.enter_context(nc.Block())

        @block.sync
        def _(sp):
            if row_dram is not None:
                sp.dma_start(r[:, :], row(row_dram)).then_inc(loaded, 16)

        @block.vector
        def _(dve):
            if row_dram is not None:
                dve.wait_ge(loaded, 16)
            work(r, chained(dve, chain))


def add_row(nc, tag, X, dram):
    small_phase(nc, tag, dram, lambda r, then: then(
        nc.vector.tensor_tensor(X[:, :, :], X[:, :, :], r[:, None, :].to_broadcast([P, NT, D]), ALU.add)))


def scale_all(nc, tag, X, factor):
    small_phase(nc, tag, None, lambda r, then: then(
        nc.vector.tensor_scalar(X[:, :, :], X[:, :, :], factor, None, ALU.mult)))


def project(nc, tag, consts, source, weights, bias_rows, width, steps, handle, stores):
    with ExitStack() as ctx:
        sc = Scope(nc, ctx, tag)
        placed = sc.sb("placed", [P, 2, D])
        turned = sc.sb("turned", [P, 2, D])
        W = sc.sb("W", [P, KD, width])
        biases = sc.sb("biases", [P, width])
        ps_turn = [sc.ps(f"turn{u}", [P, D]) for u in range(2)]
        out = [sc.ps(f"out{u}", [P, max(width, 512) if width > 256 else width]) for u in range(2)]
        loaded, stored = sc.sem("loaded"), sc.sem("stored")
        pool_placed, pe_turned, act_turned = sc.sem("pool_placed"), sc.sem("pe_turned"), sc.sem("act_turned")
        pe_projected, dve_handled = sc.sem("pe_projected"), sc.sem("dve_handled")
        block = ctx.enter_context(nc.Block())

        @block.sync
        def _(sp):
            for dram, c0 in weights:
                sp.dma_start(W[:, :, c0:c0 + dram.shape[1]], dram.rearrange("(k p) n -> p k n", p=P)).then_inc(loaded, 16)
            for dram, c0 in bias_rows:
                sp.dma_start(biases[:, c0:c0 + dram.shape[0]], row(dram, dram.shape[0])).then_inc(loaded, 16)
            if stores:
                sp.wait_ge(dve_handled, (NT + 2) * steps)
                for table, buf in stores:
                    sp.dma_start(table.rearrange("(b p) d -> p b d", p=P), buf[:, :, :]).then_inc(stored, 16)
                sp.wait_ge(stored, 16 * len(stores))

        @block.gpsimd
        def _(pool):
            def body(t0, n):
                for u in range(n):
                    pool.wait_ge(pe_turned, t0 * 2 + (u + 1) * 2)
                    nc.gpsimd.tensor_copy(placed[:, u, :], flat(source[:, at(t0 + u), :])).then_inc(pool_placed, 1)
            in_pairs(pool, body)

        @block.tensor
        def _(pe):
            nc.tensor.sem_inc(pe_turned, 4)
            nc.tensor.sem_inc(pe_projected, 2)
            pe.wait_ge(loaded, 16 * (len(weights) + len(bias_rows)))

            def body(t0, n):
                for u in range(n):
                    pe.wait_ge(pool_placed, t0 + (u + 1))
                    pe.wait_ge(act_turned, t0 + (u + 1))
                    for k in range(KD):
                        nc.tensor.transpose(ps_turn[u][:, k * P:(k + 1) * P], placed[:, u, k * P:(k + 1) * P],
                                            consts["ident"][:, :]).then_inc(pe_turned, 1)
                for u in range(n):
                    pe.wait_ge(act_turned, t0 + (u + 3))
                    pe.wait_ge(dve_handled, t0 * steps + (u + 1) * steps)
                    for c0 in range(0, width, 512):
                        w = min(512, width - c0)
                        for k in range(KD):
                            mm = nc.tensor.matmul(out[u][:, c0:c0 + w], turned[:, u, k * P:(k + 1) * P],
                                                  W[:, k, c0:c0 + w], start=(k == 0), stop=(k == KD - 1))
                    mm.then_inc(pe_projected, 1)
            in_pairs(pe, body)

        @block.scalar
        def _(act):
            nc.scalar.sem_inc(act_turned, 2)

            def body(t0, n):
                for u in range(n):
                    act.wait_ge(pe_turned, t0 * 2 + (u + 3) * 2)
                    act.wait_ge(pe_projected, t0 + (u + 1))
                    nc.scalar.activation(turned[:, u, :], ps_turn[u][:, :], ACT.Copy).then_inc(act_turned, 1)
            in_pairs(act, body)

        @block.vector
        def _(dve):
            nc.vector.sem_inc(dve_handled, 2 * steps)

            def body(t0, n):
                for u in range(n):
                    dve.wait_ge(pe_projected, t0 + (u + 3))
                    handle(t0 + u, out[u], biases, dve_handled)
            in_pairs(dve, body)


def turn_nodes(nc, tag, consts, source, dest):
    with ExitStack() as ctx:
        sc = Scope(nc, ctx, tag)
        placed = sc.sb("placed", [P, 2, D])
        ps_turn = [sc.ps(f"turn{u}", [P, D]) for u in range(2)]
        pool_placed, pe_turned, act_turned = sc.sem("pool_placed"), sc.sem("pe_turned"), sc.sem("act_turned")
        block = ctx.enter_context(nc.Block())

        @block.gpsimd
        def _(pool):
            def body(t0, n):
                for u in range(n):
                    pool.wait_ge(pe_turned, t0 * 2 + (u + 1) * 2)
                    nc.gpsimd.tensor_copy(placed[:, u, :], flat(source[:, at(t0 + u), :])).then_inc(pool_placed, 1)
            in_pairs(pool, body)

        @block.tensor
        def _(pe):
            nc.tensor.sem_inc(pe_turned, 4)

            def body(t0, n):
                for u in range(n):
                    pe.wait_ge(pool_placed, t0 + (u + 1))
                    pe.wait_ge(act_turned, t0 + (u + 1))
                    for k in range(KD):
                        nc.tensor.transpose(ps_turn[u][:, k * P:(k + 1) * P], placed[:, u, k * P:(k + 1) * P],
                                            consts["ident"][:, :]).then_inc(pe_turned, 1)
            in_pairs(pe, body)

        @block.scalar
        def _(act):
            nc.scalar.sem_inc(act_turned, 2)

            def body(t0, n):
                for u in range(n):
                    act.wait_ge(pe_turned, t0 * 2 + (u + 3) * 2)
                    nc.scalar.activation(dest[:, :, at((t0 + u) * P, P)], ps_turn[u][:, :].rearrange("p (k n) -> p k n", k=KD),
                                         ACT.Copy).then_inc(act_turned, 1)
            in_pairs(act, body)


def attention_scores(nc, consts, k_table, Q, edges, scores, most):
    local_of, other_of, bucket_of = edges
    with ExitStack() as ctx:
        sc = Scope(nc, ctx, "score")
        rows = sc.sb("rows", [P, RING, D])
        index = sc.sb("index", [P, RING], I32)
        onehot = sc.sb("onehot", [P, 2, P])
        turned = sc.sb("turned", [P, 2, P])
        away = sc.sb("away", [P, 2, P], BF16)
        product = sc.sb("product", [P, 2, D])
        score = sc.sb("score", [P, 2, HEADS])
        tile_most = sc.sb("tile_most", [P, 2, HEADS])
        ps_turn = [sc.ps(f"turn{u}", [P, P]) for u in range(2)]
        ps_q = [sc.ps(f"q{u}", [P, D]) for u in range(2)]
        ps_all = [sc.ps(f"all{u}", [P, HEADS * P]) for u in range(2)]
        gathered = [sc.sem(f"gathered{r}") for r in range(RING)]
        indexed, begun, cleared = sc.sem("indexed"), sc.sem("begun"), sc.sem("cleared")
        dve_onehot, pe_turned, act_turned, act_away = (sc.sem(s) for s in ("dve_onehot", "pe_turned", "act_turned", "act_away"))
        pe_q, dve_product, dve_score, act_kept = (sc.sem(s) for s in ("pe_q", "dve_product", "dve_score", "act_kept"))
        pe_all, dve_most, dve_merged = (sc.sem(s) for s in ("pe_all", "dve_most", "dve_merged"))
        block = ctx.enter_context(nc.Block())
        ahead = 2

        @block.gpsimd
        def _(pool):
            with pool.Fori(0, ET // RING) as i:
                for r in range(RING):
                    pool.wait_ge(indexed, i * RING + (r + 1))
                    nc.gpsimd.sem_inc(begun, 1)
                    pool.indirect_dma_start(rows[:, r, :], None, k_table,
                                            bass.IndirectOffsetOnAxis(ap=index[:, r:r + 1], axis=0)).then_inc(gathered[r], 16)

        @block.scalar
        def _(act):
            for s in (act_turned, act_away, act_kept):
                nc.scalar.sem_inc(s, ahead)
            for r in range(RING):
                nc.scalar.activation(index[:, r:r + 1], other_of[:, r:r + 1], ACT.Copy).then_inc(indexed, 1)
            with act.Fori(0, ET // RING) as i:
                for r in range(RING):
                    t, u = i * RING, r % 2
                    act.wait_ge(pe_turned, t + (r + 1 + ahead))
                    act.wait_ge(pe_q, t + (r + 1))
                    nc.scalar.activation(turned[:, u, :], ps_turn[u][:, :], ACT.Copy).then_inc(act_turned, 1)
                    act.wait_ge(pe_all, t + (r + 1))
                    nc.scalar.activation(away[:, u, :], ps_turn[u][:, :], ACT.Copy, bias=-FAR, scale=FAR).then_inc(act_away, 1)
                    act.wait_ge(dve_score, t + (r + 1 + ahead))
                    nc.scalar.activation(flat(scores[:, at(t + r), :]), score[:, u, :], ACT.Copy).then_inc(act_kept, 1)
                    nc.scalar.activation(index[:, r:r + 1], other_of[:, at(t + (r + RING))], ACT.Copy).then_inc(indexed, 1)

        @block.tensor
        def _(pe):
            for s in (pe_turned, pe_q, pe_all):
                nc.tensor.sem_inc(s, ahead)
            with pe.Fori(0, ET // RING) as i:
                t = i * RING
                for r in range(RING):
                    u = r % 2
                    b = pe.value_load(bucket_of[0:1, at(t + r)], min_val=0, max_val=NT - 1)
                    pe.wait_ge(dve_onehot, t + (r + 1 + ahead))
                    pe.wait_ge(act_away, t + (r + 1))
                    nc.tensor.transpose(ps_turn[u][:, :], onehot[:, u, :], consts["ident"][:, :]).then_inc(pe_turned, 1)
                    pe.wait_ge(act_turned, t + (r + 1 + ahead))
                    pe.wait_ge(dve_product, t + (r + 1))
                    nc.tensor.matmul(ps_q[u][:, :], turned[:, u, :], flat(Q[:, at(b), :]), start=True, stop=True).then_inc(pe_q, 1)
                    pe.wait_ge(act_away, t + (r + 1 + ahead))
                    pe.wait_ge(dve_score, t + (r + 1 + ahead))
                    pe.wait_ge(dve_most, t + (r + 1))
                    nc.tensor.matmul(ps_all[u][:, :].rearrange("p (h e) -> p h e", h=HEADS), consts["ident_b"][:, :],
                                     away[:, u, None, :].to_broadcast([P, HEADS, P]), start=True, stop=False,
                                     skip_group_check=True)
                    for h in range(HEADS):
                        mm = nc.tensor.matmul(ps_all[u][:, h * P:(h + 1) * P], score[:, u, h:h + 1].to_broadcast([P, P]),
                                              consts["ident"][:, :], start=False, stop=(h == HEADS - 1), skip_group_check=True)
                    mm.then_inc(pe_all, 1)

        @block.vector
        def _(dve):
            for s in (dve_onehot, dve_product, dve_score, dve_most, dve_merged):
                nc.vector.sem_inc(s, ahead)
            nc.vector.memset(most[:, :, :], -FAR).then_inc(cleared, 1)
            dve.wait_ge(cleared, 1)

            def find_most(t, r):
                u = r % 2
                dve.wait_ge(pe_all, t + (r + 1 + ahead))
                nc.vector.tensor_reduce(tile_most[:, u, :], ps_all[u][:, :].rearrange("p (h e) -> p h e", h=HEADS), AX,
                                        ALU.max).then_inc(dve_most, 1)
                b = dve.value_load(bucket_of[0:1, at(t + r)], min_val=0, max_val=NT - 1)
                dve.wait_ge(dve_most, t + (r + 1 + ahead))
                dve.wait_ge(dve_merged, t + (r + ahead))
                cur = flat(most[:, at(b), :])
                nc.vector.tensor_tensor(cur, cur, tile_most[:, u, :], ALU.max).then_inc(dve_merged, 1)

            with dve.Fori(0, ET // RING) as i:
                t = i * RING
                for r in range(RING):
                    u = r % 2
                    dve.wait_ge(pe_turned, t + (r + 1))
                    nc.vector.tensor_scalar(onehot[:, u, :], consts["iota_lf"][:, :], local_of[:, at(t + r)], None,
                                            ALU.is_equal).then_inc(dve_onehot, 1)
                    if r > 0:
                        find_most(t, r - 1)
                    dve.wait_ge(pe_q, t + (r + 1 + ahead))
                    dve.wait_ge(gathered[r], i * 16 + 16)
                    nc.vector.tensor_tensor(product[:, u, :], ps_q[u][:, :], rows[:, r, :], ALU.mult).then_inc(dve_product, 1)
                    dve.wait_ge(dve_product, t + (r + 1 + ahead))
                    dve.wait_ge(pe_all, t + (r + 1))
                    dve.wait_ge(act_kept, t + (r + 1))
                    nc.vector.tensor_reduce(score[:, u, :], product[:, u, :].rearrange("p (h c) -> p h c", h=HEADS), AX,
                                            ALU.add).then_inc(dve_score, 1)
                find_most(t, RING - 1)


def edge_sums(nc, tag, consts, table, edges, total, attention=None):
    local_of, other_of, bucket_of = edges
    width = D + (HEADS if attention else 1)
    with ExitStack() as ctx:
        sc = Scope(nc, ctx, tag)
        rows = sc.sb("rows", [P, RING, D + 1])
        index = sc.sb("index", [P, RING], I32)
        onehot = sc.sb("onehot", [P, 2, P])
        ps_sum = [sc.ps(f"sum{u}", [P, 512]) for u in range(2)]
        gathered = [sc.sem(f"gathered{r}") for r in range(RING)]
        indexed, begun, cleared = sc.sem("indexed"), sc.sem("begun"), sc.sem("cleared")
        dve_onehot, pe_summed, dve_added = (sc.sem(s) for s in ("dve_onehot", "pe_summed", "dve_added"))
        if attention:
            scores, most = attention
            turned = sc.sb("turned", [P, 2, P])
            less = sc.sb("less", [P, 2, HEADS])
            message = sc.sb("message", [P, 2, AW])
            ps_turn = [sc.ps(f"turn{u}", [P, P]) for u in range(2)]
            ps_most = [sc.ps(f"most{u}", [P, HEADS]) for u in range(2)]
            pe_turned, act_turned, pe_most = (sc.sem(s) for s in ("pe_turned", "act_turned", "pe_most"))
            dve_less, act_exp, dve_message = (sc.sem(s) for s in ("dve_less", "act_exp", "dve_message"))
        block = ctx.enter_context(nc.Block())
        ahead = 2

        @block.gpsimd
        def _(pool):
            with pool.Fori(0, ET // RING) as i:
                for r in range(RING):
                    pool.wait_ge(indexed, i * RING + (r + 1))
                    nc.gpsimd.sem_inc(begun, 1)
                    pool.indirect_dma_start(rows[:, r, 0:D], None, table,
                                            bass.IndirectOffsetOnAxis(ap=index[:, r:r + 1], axis=0)).then_inc(gathered[r], 16)

        @block.scalar
        def _(act):
            if attention:
                for s in (act_turned, act_exp):
                    nc.scalar.sem_inc(s, ahead)
            for r in range(RING):
                nc.scalar.activation(index[:, r:r + 1], other_of[:, r:r + 1], ACT.Copy).then_inc(indexed, 1)
            with act.Fori(0, ET // RING) as i:
                t = i * RING
                for r in range(RING):
                    u = r % 2
                    if attention:
                        act.wait_ge(pe_turned, t + (r + 1 + ahead))
                        act.wait_ge(pe_most, t + (r + 1))
                        nc.scalar.activation(turned[:, u, :], ps_turn[u][:, :], ACT.Copy).then_inc(act_turned, 1)
                        act.wait_ge(dve_less, t + (r + 1 + ahead))
                        act.wait_ge(pe_summed, t + (r + 1))
                        nc.scalar.activation(message[:, u, D:AW], less[:, u, :], ACT.Exp).then_inc(act_exp, 1)
                        act.wait_ge(dve_message, t + (r + 1 + ahead))
                    else:
                        act.wait_ge(pe_summed, t + (r + 1 + ahead))
                    nc.scalar.activation(index[:, r:r + 1], other_of[:, at(t + (r + RING))], ACT.Copy).then_inc(indexed, 1)

        @block.tensor
        def _(pe):
            nc.tensor.sem_inc(pe_summed, ahead)
            if attention:
                nc.tensor.sem_inc(pe_turned, ahead)
                nc.tensor.sem_inc(pe_most, ahead)
            pe.wait_ge(cleared, 2)
            with pe.Fori(0, ET // RING) as i:
                t = i * RING
                for r in range(RING):
                    u = r % 2
                    pe.wait_ge(dve_onehot, t + (r + 1 + ahead))
                    if attention:
                        b = pe.value_load(bucket_of[0:1, at(t + r)], min_val=0, max_val=NT - 1)
                        pe.wait_ge(act_turned, t + (r + 1))
                        nc.tensor.transpose(ps_turn[u][:, :], onehot[:, u, :], consts["ident"][:, :]).then_inc(pe_turned, 1)
                        pe.wait_ge(act_turned, t + (r + 1 + ahead))
                        pe.wait_ge(dve_less, t + (r + 1))
                        nc.tensor.matmul(ps_most[u][:, :], turned[:, u, :], flat(most[:, at(b), :]), start=True,
                                         stop=True).then_inc(pe_most, 1)
                        pe.wait_ge(dve_message, t + (r + 1 + ahead))
                        values = message[:, u, :]
                    else:
                        pe.wait_ge(gathered[r], i * 16 + 16)
                        values = rows[:, r, :]
                    pe.wait_ge(dve_added, t + (r + 1))
                    nc.tensor.matmul(ps_sum[u][:, 0:width], onehot[:, u, :], values, start=True, stop=True).then_inc(pe_summed, 1)

        @block.vector
        def _(dve):
            nc.vector.sem_inc(dve_onehot, ahead)
            nc.vector.sem_inc(dve_added, ahead)
            if attention:
                nc.vector.sem_inc(dve_less, ahead)
                nc.vector.sem_inc(dve_message, ahead)
            nc.vector.memset(total[:, :, :], 0.0).then_inc(cleared, 1)
            nc.vector.memset(rows[:, :, D:D + 1], 1.0).then_inc(cleared, 1)
            dve.wait_ge(cleared, 2)

            def add(t, r):
                u = r % 2
                b = dve.value_load(bucket_of[0:1, at(t + r)], min_val=0, max_val=NT - 1)
                dve.wait_ge(pe_summed, t + (r + 1 + ahead))
                dve.wait_ge(dve_added, t + (r + ahead))
                cur = flat(total[:, at(b), 0:width])
                nc.vector.tensor_tensor(cur, cur, ps_sum[u][:, 0:width], ALU.add).then_inc(dve_added, 1)

            with dve.Fori(0, ET // RING) as i:
                t = i * RING
                for r in range(RING):
                    u = r % 2
                    dve.wait_ge(pe_summed, t + (r + 1))
                    nc.vector.tensor_scalar(onehot[:, u, :], consts["iota_lf"][:, :], local_of[:, at(t + r)], None,
                                            ALU.is_equal).then_inc(dve_onehot, 1)
                    if r > 0:
                        add(t, r - 1)
                    if attention:
                        dve.wait_ge(pe_most, t + (r + 1 + ahead))
                        dve.wait_ge(act_exp, t + (r + 1))
                        nc.vector.tensor_tensor(less[:, u, :], flat(scores[:, at(t + r), :]), ps_most[u][:, :],
                                                ALU.subtract).then_inc(dve_less, 1)
                        dve.wait_ge(act_exp, t + (r + 1 + ahead))
                        dve.wait_ge(gathered[r], i * 16 + 16)
                        nc.vector.tensor_tensor(message[:, u, 0:D].rearrange("p (h c) -> p h c", h=HEADS),
                                                rows[:, r, 0:D].rearrange("p (h c) -> p h c", h=HEADS),
                                                message[:, u, D:AW, None].to_broadcast([P, HEADS, C]),
                                                ALU.mult).then_inc(dve_message, 1)
                add(t, RING - 1)


def join_attention(nc, total, skip, X):
    with ExitStack() as ctx:
        sc = Scope(nc, ctx, "join")
        none = sc.sb("none", [P, NT, HEADS])
        chain = sc.sem("chain")
        block = ctx.enter_context(nc.Block())

        @block.vector
        def _(dve):
            then = chained(dve, chain)
            den = total[:, :, D:AW]
            then(nc.vector.tensor_scalar(none[:, :, :], den, 0.0, None, ALU.is_equal))
            then(nc.vector.tensor_tensor(none[:, :, :], none[:, :, :], den, ALU.add))
            then(nc.vector.reciprocal(none[:, :, :], none[:, :, :]))
            for h in range(HEADS):
                part = total[:, :, h * C:(h + 1) * C]
                then(nc.vector.tensor_tensor(part, part, none[:, :, h:h + 1].to_broadcast([P, NT, C]), ALU.mult))
            then(nc.vector.tensor_tensor(skip[:, :, :], skip[:, :, :], total[:, :, 0:D], ALU.add))
            then(nc.vector.tensor_tensor(X[:, :, :], X[:, :, :], skip[:, :, :], ALU.add))


def divide_by_count(nc, tag, total, table=None, bias=None, slope=None, residual=None, dest=None, add_to=None):
    with ExitStack() as ctx:
        sc = Scope(nc, ctx, tag)
        inv = sc.sb("inv", [P, NT])
        some = sc.sb("some", [P, NT])
        b_row = sc.sb("b_row", [P, D])
        a = sc.sb("a", [P, 1])
        low = sc.sb("low", [P, NT, D]) if dest is not None or add_to is not None else None
        loaded, chain, divided, stored = sc.sem("loaded"), sc.sem("chain"), sc.sem("divided"), sc.sem("stored")
        block = ctx.enter_context(nc.Block())

        @block.sync
        def _(sp):
            if table is not None:
                sp.wait_ge(divided, 1)
                sp.dma_start(table.rearrange("(b p) d -> p b d", p=P), total[:, :, 0:D]).then_inc(stored, 16)
                sp.wait_ge(stored, 16)
            else:
                sp.dma_start(b_row[:, :], row(bias)).then_inc(loaded, 16)
                sp.dma_start(a[:, :], row(slope, 1)).then_inc(loaded, 16)

        @block.vector
        def _(dve):
            then = chained(dve, chain)
            count = total[:, :, D]
            then(nc.vector.tensor_scalar(inv[:, :], count, 1.0, None, ALU.max))
            then(nc.vector.reciprocal(inv[:, :], inv[:, :]))
            then(nc.vector.tensor_scalar(some[:, :], count, 1.0, None, ALU.min))
            then(nc.vector.tensor_tensor(inv[:, :], inv[:, :], some[:, :], ALU.mult))
            body = total[:, :, 0:D]
            then(nc.vector.tensor_tensor(body, body, inv[:, :, None].to_broadcast([P, NT, D]), ALU.mult))
            if table is not None:
                nc.vector.sem_inc(divided, 1)
                return
            dve.wait_ge(loaded, 32)
            then(nc.vector.tensor_tensor(body, body, b_row[:, None, :].to_broadcast([P, NT, D]), ALU.add))
            if residual is not None:
                then(nc.vector.tensor_tensor(body, body, residual[:, :, :], ALU.add))
            then(nc.vector.tensor_scalar(low[:, :, :], body, 0.0, a[:, 0:1], ALU.min, ALU.mult))
            if dest is not None:
                then(nc.vector.scalar_tensor_tensor(out=dest[:, :, :], in0=body, scalar=0.0, in1=low[:, :, :],
                                                    op0=ALU.max, op1=ALU.add))
            else:
                then(nc.vector.scalar_tensor_tensor(out=body, in0=body, scalar=0.0, in1=low[:, :, :],
                                                    op0=ALU.max, op1=ALU.add))
                then(nc.vector.tensor_tensor(add_to[:, :, :], add_to[:, :, :], body, ALU.add))


def top_two(nc, sc, then, consts, probs, T):
    found = []
    left = probs
    for n in range(2):
        best = sc[f"best{n}"]
        first = sc[f"first{n}"]
        one = sc[f"one{n}"]
        wide = [P, T, EXPERTS]
        names = consts["iota_e"][:, None, :].to_broadcast(wide)
        then(nc.vector.tensor_reduce(best[:, :], left[:, :, :], AX, ALU.max))
        then(nc.vector.tensor_tensor(one[:, :, :], left[:, :, :], best[:, :, None].to_broadcast(wide), ALU.is_equal))
        then(nc.vector.tensor_tensor(one[:, :, :], one[:, :, :], names, ALU.mult))
        then(nc.vector.tensor_reduce(first[:, :], one[:, :, :], AX, ALU.min))
        then(nc.vector.tensor_tensor(one[:, :, :], first[:, :, None].to_broadcast(wide), names, ALU.is_equal))
        if n == 0:
            then(nc.vector.scalar_tensor_tensor(out=sc["left"][:, :, :], in0=one[:, :, :], scalar=-4.0, in1=probs[:, :, :],
                                                op0=ALU.mult, op1=ALU.add))
            left = sc["left"]
        found.append((best, first, one))
    return found


def top_buffers(sc, T):
    out = {"left": sc.sb("left", [P, T, EXPERTS])}
    for n in range(2):
        out[f"best{n}"] = sc.sb(f"best{n}", [P, T])
        out[f"first{n}"] = sc.sb(f"first{n}", [P, T])
        out[f"one{n}"] = sc.sb(f"one{n}", [P, T, EXPERTS])
    return out


def softmax_steps(nc, dve, then, peak, sums, x, T, exp_asked, exp_done, n):
    shape = [P, T, x.shape[2]]
    then(nc.vector.tensor_reduce(peak[:, :], x[:, :, :], AX, ALU.max))
    nc.vector.tensor_tensor(x[:, :, :], x[:, :, :], peak[:, :, None].to_broadcast(shape), ALU.subtract).then_inc(exp_asked, 1)
    dve.wait_ge(exp_done, n)
    then(nc.vector.tensor_reduce(sums[:, :], x[:, :, :], AX, ALU.add))
    then(nc.vector.reciprocal(sums[:, :], sums[:, :]))
    then(nc.vector.tensor_tensor(x[:, :, :], x[:, :, :], sums[:, :, None].to_broadcast(shape), ALU.mult))


def route_all(nc, consts, U, Wr, br, chosen, gate):
    capacity = float(math.ceil(N * 1.25 / EXPERTS))
    with ExitStack() as ctx:
        sc = Scope(nc, ctx, "route")
        wr = sc.sb("wr", [P, D, EXPERTS])
        wide = sc.sb("wide", [P, D, EXPERTS])
        br_row = sc.sb("br_row", [P, 1, EXPERTS])
        mean = sc.sb("mean", [P, D])
        rw = sc.sb("rw", [P, 1, EXPERTS])
        load = sc.sb("load", [P, 1, EXPERTS])
        over = sc.sb("over", [P, 1, EXPERTS])
        two = sc.sb("two", [P, 1, 2])
        peak, sums = sc.sb("peak", [P, 1]), sc.sb("sums", [P, 1])
        tops = top_buffers(sc, 1)
        total = sc.ps("total", [P, D])
        loaded, chain, summed = sc.sem("loaded"), sc.sem("chain"), sc.sem("summed")
        exp_asked, exp_done = sc.sem("exp_asked"), sc.sem("exp_done")
        block = ctx.enter_context(nc.Block())

        @block.sync
        def _(sp):
            sp.dma_start(wr[:, :, :].rearrange("p d e -> p (d e)"), row(Wr.rearrange("d e -> (d e)"), D * EXPERTS)).then_inc(loaded, 16)
            sp.dma_start(br_row[:, 0, :], row(br, EXPERTS)).then_inc(loaded, 16)

        @block.tensor
        def _(pe):
            nc.tensor.matmul(total[:, :], consts["real"][:, :], U[:, NT - 1, :], start=True, stop=False)
            for t in range(NT - 1):
                mm = nc.tensor.matmul(total[:, :], consts["ones"][:, :], U[:, t, :], start=False, stop=(t == NT - 2))
            mm.then_inc(summed, 1)

        @block.scalar
        def _(act):
            for n, x in enumerate((rw, rw, two)):
                act.wait_ge(exp_asked, n + 1)
                nc.scalar.activation(x[:, :, :], x[:, :, :], ACT.Exp).then_inc(exp_done, 1)

        @block.vector
        def _(dve):
            then = chained(dve, chain)
            dve.wait_ge(loaded, 32)
            dve.wait_ge(summed, 1)
            then(nc.vector.tensor_scalar(mean[:, :], total[:, :], 1.0 / N, None, ALU.mult))
            then(nc.vector.tensor_tensor(wide[:, :, :], wr[:, :, :], mean[:, :, None].to_broadcast([P, D, EXPERTS]), ALU.mult))
            then(nc.vector.tensor_reduce(rw[:, 0, :], wide[:, :, :].rearrange("p d e -> p e d"), AX, ALU.add))
            then(nc.vector.tensor_tensor(rw[:, :, :], rw[:, :, :], br_row[:, :, :], ALU.add))
            softmax_steps(nc, dve, then, peak, sums, rw, 1, exp_asked, exp_done, 1)
            then(nc.vector.tensor_scalar(load[:, :, :], rw[:, :, :], float(N), None, ALU.mult))
            then(nc.vector.tensor_scalar(over[:, :, :], load[:, :, :], capacity, None, ALU.max))
            then(nc.vector.reciprocal(over[:, :, :], over[:, :, :]))
            then(nc.vector.scalar_tensor_tensor(out=rw[:, :, :], in0=over[:, :, :], scalar=capacity, in1=rw[:, :, :],
                                                op0=ALU.mult, op1=ALU.mult))
            softmax_steps(nc, dve, then, peak, sums, rw, 1, exp_asked, exp_done, 2)
            found = top_two(nc, tops, then, consts, rw, 1)
            for n, (best, first, one) in enumerate(found):
                then(nc.vector.tensor_copy(two[:, 0, n:n + 1], best[:, :]))
                then(nc.vector.tensor_scalar(chosen[:, n:n + 1], first[0:1, :], float(EXPERTS), None, ALU.add))
            softmax_steps(nc, dve, then, peak, sums, two, 1, exp_asked, exp_done, 3)
            then(nc.vector.tensor_copy(gate[:, :], two[:, 0, :]))


def route_each(nc, consts, logits, br, gate):
    with ExitStack() as ctx:
        sc = Scope(nc, ctx, "each")
        br_row = sc.sb("br_row", [P, EXPERTS])
        peak, sums = sc.sb("peak", [P, NT]), sc.sb("sums", [P, NT])
        tops = top_buffers(sc, NT)
        loaded, chain, exp_asked, exp_done = sc.sem("loaded"), sc.sem("chain"), sc.sem("exp_asked"), sc.sem("exp_done")
        block = ctx.enter_context(nc.Block())
        wide = [P, NT, EXPERTS]

        @block.sync
        def _(sp):
            sp.dma_start(br_row[:, :], row(br, EXPERTS)).then_inc(loaded, 16)

        @block.scalar
        def _(act):
            act.wait_ge(exp_asked, 1)
            nc.scalar.activation(logits[:, :, :], logits[:, :, :], ACT.Exp).then_inc(exp_done, 1)

        @block.vector
        def _(dve):
            then = chained(dve, chain)
            dve.wait_ge(loaded, 16)
            then(nc.vector.tensor_tensor(logits[:, :, :], logits[:, :, :], br_row[:, None, :].to_broadcast(wide), ALU.add))
            softmax_steps(nc, dve, then, peak, sums, logits, NT, exp_asked, exp_done, 1)
            (p1, _, one1), (p2, _, one2) = top_two(nc, tops, then, consts, logits, NT)
            then(nc.vector.tensor_tensor(sums[:, :], p1[:, :], p2[:, :], ALU.add))
            then(nc.vector.reciprocal(sums[:, :], sums[:, :]))
            for p, one in ((p1, one1), (p2, one2)):
                then(nc.vector.tensor_tensor(p[:, :], p[:, :], sums[:, :], ALU.mult))
                then(nc.vector.tensor_tensor(one[:, :, :], one[:, :, :], p[:, :, None].to_broadcast(wide), ALU.mult))
            then(nc.vector.tensor_tensor(gate[:, :, :], one1[:, :, :], one2[:, :, :], ALU.add))


def feed_forward(nc, tag, uT, acc, F, experts, params, gate, chosen=None, affine=None):
    W1, b1, W2, b2 = params
    J = F // P
    slots = min(2, experts)
    half = GW // 2
    with ExitStack() as ctx:
        sc = Scope(nc, ctx, tag)
        w1 = [sc.sb(f"w1_{s}", [P, KD, F]) for s in range(slots)]
        w2 = [sc.sb(f"w2_{s}", [P, J, D]) for s in range(slots)]
        b1c = [sc.sb(f"b1_{s}", [P, J]) for s in range(slots)]
        b2r = [sc.sb(f"b2_{s}", [P, D]) for s in range(slots)]
        gc = [sc.sb(f"gc_{s}", [P, KD]) for s in range(slots)]
        bc = [sc.sb(f"bc_{s}", [P, KD]) for s in range(slots)]
        xe = sc.sb("xe", [P, KD, GW])
        hid = sc.sb("hid", [P, J, GW])
        part = sc.sb("part", [P, 2, D])
        ps_h = [sc.ps(f"h{u}", [P, 2, 512]) for u in range(2)]
        ps_y = [sc.ps(f"y{u}", [P, D]) for u in range(2)]
        loaded = [sc.sem(f"loaded{s}") for s in range(slots)]
        weights_used, pool_x, pe_h, act_h = (sc.sem(s) for s in ("weights_used", "pool_x", "pe_h", "act_h"))
        pe_y, dve_part, dve_acc = (sc.sem(s) for s in ("pe_y", "dve_part", "dve_acc"))
        loads = 4 + (2 if affine else 0)
        xs = KD * (2 if affine else 1)
        started = sc.sem("started")
        block = ctx.enter_context(nc.Block())

        def each(eng, body, before=None, after=None):
            def pair(ep):
                for s in range(slots):
                    if before:
                        before(s, ep)
                    with eng.Fori(0, GROUPS) as g:
                        body(s, ep * slots + s, g, (ep * slots + s) * GROUPS + g)
                    if after:
                        after(s, ep)
            if experts > slots:
                with eng.Fori(0, experts // slots) as ep:
                    pair(ep)
            else:
                pair(0)

        @block.sync
        def _(sp):
            def load(s, ep):
                e = ep * slots + s
                if chosen is not None:
                    e = sp.value_load(chosen[0:1, s:s + 1], min_val=0, max_val=EXPERTS - 1)
                sp.wait_ge(weights_used, e + 1) if chosen is None else None
                lot = [(w1[s][:, :, :], W1[at(e), :, :].rearrange("o (k p) f -> p (o k) f", p=P)),
                       (w2[s][:, :, :], W2[at(e), :, :].rearrange("o (j p) d -> p (o j) d", p=P)),
                       (b1c[s][:, :], b1[at(e), :].rearrange("o (j p) -> p (o j)", p=P)),
                       (b2r[s][:, :], b2[at(e), :].to_broadcast([P, D]))]
                if affine:
                    lot += [(gc[s][:, :], affine[0][at(e), :].rearrange("o (k p) -> p (o k)", p=P)),
                            (bc[s][:, :], affine[1][at(e), :].rearrange("o (k p) -> p (o k)", p=P))]
                for tile, dram in lot:
                    sp.dma_start(tile, dram, allow_slow_non_contiguous=True).then_inc(loaded[s], 16)

            if experts > slots:
                with sp.Fori(0, experts // slots) as ep:
                    for s in range(slots):
                        load(s, ep)
            else:
                for s in range(slots):
                    load(s, 0)

        @block.gpsimd
        def _(pool):
            def body(s, e, g, step):
                pool.wait_ge(pe_h, step * J + 2)
                for k in range(KD):
                    u = uT[:, k, at(g * GW, GW)]
                    nc.gpsimd.tensor_copy(xe[:, k, :], u).then_inc(pool_x, 1)
                if affine:
                    pool.wait_ge(pool_x, step * xs + KD)
                    nc.gpsimd.sem_inc(started, 1)
                    for k in range(KD):
                        nc.gpsimd.tensor_scalar(xe[:, k, :], xe[:, k, :], gc[s][:, k:k + 1], bc[s][:, k:k + 1], ALU.mult,
                                                ALU.add).then_inc(pool_x, 1)

            def before(s, ep):
                pool.wait_ge(loaded[s], ep * (16 * loads) + 16 * loads)
                nc.gpsimd.sem_inc(started, 1)
            each(pool, body, before)

        @block.tensor
        def _(pe):
            nc.tensor.sem_inc(pe_h, 2)

            def before(s, ep):
                pe.wait_ge(loaded[s], ep * (16 * loads) + 16 * loads)
                nc.tensor.sem_inc(started, 1)

            def body(s, e, g, step):
                pe.wait_ge(pool_x, step * xs + xs)
                for j in range(J):
                    pe.wait_ge(act_h, step * J + (j + 1))
                    for a in range(2):
                        for k in range(KD):
                            mm = nc.tensor.matmul(ps_h[j % 2][:, a, 0:half], w1[s][:, k, j * P:(j + 1) * P],
                                                  xe[:, k, a * half:(a + 1) * half], start=(k == 0), stop=(k == KD - 1))
                    mm.then_inc(pe_h, 1)
                pe.wait_ge(act_h, step * J + (J + 2))
                for v in range(GT):
                    pe.wait_ge(dve_part, step * GT + (v + 1 if v == 0 else v))
                    for j in range(J):
                        mm = nc.tensor.matmul(ps_y[v % 2][:, :], hid[:, j, v * P:(v + 1) * P], w2[s][:, j, :],
                                              start=(j == 0), stop=(j == J - 1))
                    mm.then_inc(pe_y, 1)

            each(pe, body, before)

        @block.scalar
        def _(act):
            nc.scalar.sem_inc(act_h, 2)

            def before(s, ep):
                act.wait_ge(loaded[s], ep * (16 * loads) + 16 * loads)
                nc.scalar.sem_inc(started, 1)

            def body(s, e, g, step):
                for j in range(J):
                    act.wait_ge(pe_h, step * J + (j + 3))
                    nc.scalar.activation(hid[:, j, :].rearrange("p (a n) -> p a n", a=2), ps_h[j % 2][:, :, 0:half], ACT.Gelu,
                                         bias=b1c[s][:, j:j + 1]).then_inc(act_h, 1)
            each(act, body, before)

        @block.vector
        def _(dve):
            nc.vector.sem_inc(dve_part, 1)
            nc.vector.sem_inc(dve_acc, 2)
            nc.vector.sem_inc(weights_used, slots)

            def before(s, ep):
                dve.wait_ge(loaded[s], ep * (16 * loads) + 16 * loads)
                nc.vector.sem_inc(started, 1)

            def body(s, e, g, step):
                for v in range(GT):
                    dve.wait_ge(pe_y, step * GT + (v + 1))
                    dve.wait_ge(dve_acc, step * GT + (v + 2))
                    nc.vector.tensor_tensor(part[:, v % 2, :], ps_y[v % 2][:, :], b2r[s][:, :], ALU.add).then_inc(dve_part, 1)
                    dve.wait_ge(dve_part, step * GT + (v + 2))
                    cur = flat(acc[:, at(g * GT + v), :])
                    nc.vector.scalar_tensor_tensor(out=cur, in0=part[:, v % 2, :], scalar=gate(g * GT + v, e, s), in1=cur,
                                                   op0=ALU.mult, op1=ALU.add).then_inc(dve_acc, 1)

            def after(s, ep):
                dve.wait_ge(dve_acc, (ep * slots + (s + 1)) * (GROUPS * GT) + 2)
                nc.vector.sem_inc(weights_used, 1)
            each(dve, body, before, after)


def program(nc, x, src, dst, ln1_w, ln1_b, ln2_w, ln2_b, wq, bq, wk, bk, wv, bv, wskip, bskip, w1, b1, w2, b2,
            fWr, fbr, fW1, fb1, fW2, fb2, gamma, beta, hW1, hb1, hW2, hb2, slope,
            mWr, mbr, ln_g, ln_b, mW1, mb1, mW2, mb2, out):
    tables = [nc.dram_tensor(f"table{n}", (NT * P, D), F32, kind="Internal").ap() for n in range(6)]
    with ExitStack() as ctx:
        keep = Scope(nc, ctx, "keep")
        c = constants(nc, keep)

        def edge_lists(name):
            return keep.sb(f"{name}_local", [P, ET]), keep.sb(f"{name}_other", [P, ET + RING], I32), keep.sb(f"{name}_bucket", [1, ET], I32)
        by_dst, by_src = edge_lists("dst"), edge_lists("src")
        sort_edges(nc, "sort_dst", dst, src, c, by_dst[0], by_dst[1], by_dst[2])
        sort_edges(nc, "sort_src", src, dst, c, by_src[0], by_src[1], by_src[2])

        X = keep.sb("X", [P, NT, D])
        U = keep.sb("U", [P, NT, D])
        load_nodes(nc, x, X)

        layer_norm(nc, "ln_x0", X, U)
        with ExitStack() as part:
            loc = Scope(nc, part, "att")
            Q = loc.sb("Q", [P, NT, D])
            with ExitStack() as inner:
                kv = Scope(nc, inner, "kv")
                H, K, V = kv.sb("H", [P, NT, D]), kv.sb("K", [P, NT, D]), kv.sb("V", [P, NT, D])
                layer_norm(nc, "ln_1", U, H, ln1_w, ln1_b)

                def handle(t, ps, biases, done):
                    for n, dest in enumerate((Q, K, V)):
                        nc.vector.tensor_tensor(flat(dest[:, at(t), :]), ps[:, n * D:(n + 1) * D], biases[:, n * D:(n + 1) * D],
                                                ALU.add).then_inc(done, 1)
                    cur = flat(U[:, at(t), :])
                    nc.vector.tensor_tensor(cur, cur, ps[:, 3 * D:4 * D], ALU.add).then_inc(done, 1)
                add_row(nc, "skip_bias", U, bskip)
                project(nc, "qkv", c, H, [(wq, 0), (wk, D), (wv, 2 * D), (wskip, 3 * D)], [(bq, 0), (bk, D), (bv, 2 * D)],
                        4 * D, 4, handle, [(tables[0], K), (tables[1], V)])
            scores = loc.sb("scores", [P, ET, HEADS])
            most = loc.sb("most", [P, NT, HEADS])
            scale_all(nc, "scale_q", Q, C ** -0.5)
            attention_scores(nc, c, tables[0], Q, by_dst, scores, most)
            total = loc.sb("total", [P, NT, AW])
            edge_sums(nc, "attend", c, tables[1], by_dst, total, (scores, most))
            join_attention(nc, total, U, X)
        one_expert = (w1.rearrange("(o d) f -> o d f", o=1), b1.rearrange("(o f) -> o f", o=1),
                      w2.rearrange("(o f) d -> o f d", o=1), b2.rearrange("(o d) -> o d", o=1))
        with ExitStack() as part:
            loc = Scope(nc, part, "ff1")
            H, uT = loc.sb("H", [P, NT, D]), loc.sb("uT", [P, KD, NT * P])
            layer_norm(nc, "ln_2", U, H, ln2_w, ln2_b)
            turn_nodes(nc, "turn_1", c, H, uT)
            feed_forward(nc, "ffn_1", uT, X, 2 * D, 1, one_expert, lambda t, e, s: c["ones"][:, 0:1])

        with ExitStack() as part:
            loc = Scope(nc, part, "ff2")
            uT = loc.sb("uT", [P, KD, NT * P])
            chosen, gate = loc.sb("chosen", [1, 2], I32), loc.sb("gate", [P, 2])
            layer_norm(nc, "ln_x1", X, U)
            route_all(nc, c, U, fWr, fbr, chosen, gate)
            turn_nodes(nc, "turn_2", c, U, uT)
            feed_forward(nc, "ffn_2", uT, U, 2 * D, 2, (fW1, fb1, fW2, fb2), lambda t, e, s: gate[:, s:s + 1], chosen=chosen)
            layer_norm(nc, "ln_3", U, U, gamma, beta, add_to=X)

        with ExitStack() as part:
            loc = Scope(nc, part, "hyper")
            H, total = loc.sb("H", [P, NT, D]), loc.sb("total", [P, NT, AW])
            layer_norm(nc, "ln_x2", X, U)

            def handle(t, ps, biases, done):
                nc.vector.tensor_copy(flat(H[:, at(t), :]), ps[:, :]).then_inc(done, 1)
            project(nc, "conv_1", c, U, [(hW1, 0)], [], D, 1, handle, [(tables[2], H)])
            edge_sums(nc, "to_dst_1", c, tables[2], by_dst, total)
            divide_by_count(nc, "mean_1", total, table=tables[3])
            edge_sums(nc, "to_src_1", c, tables[3], by_src, total)
            divide_by_count(nc, "act_1", total, bias=hb1, slope=slope, dest=H)
            project(nc, "conv_2", c, H, [(hW2, 0)], [], D, 1, handle, [(tables[4], H)])
            edge_sums(nc, "to_dst_2", c, tables[4], by_dst, total)
            divide_by_count(nc, "mean_2", total, table=tables[5])
            edge_sums(nc, "to_src_2", c, tables[5], by_src, total)
            divide_by_count(nc, "act_2", total, bias=hb2, slope=slope, residual=U, add_to=X)

        with ExitStack() as part:
            loc = Scope(nc, part, "moe")
            uT = loc.sb("uT", [P, KD, NT * P])
            gate = loc.sb("gate", [P, NT, EXPERTS])
            logits = loc.sb("logits", [P, NT, EXPERTS])
            layer_norm(nc, "ln_x3", X, U)

            def handle(t, ps, biases, done):
                nc.vector.tensor_copy(flat(logits[:, at(t), :]), ps[:, :]).then_inc(done, 1)
            project(nc, "logits", c, U, [(mWr, 0)], [], EXPERTS, 1, handle, [])
            route_each(nc, c, logits, mbr, gate)
            layer_norm(nc, "ln_4", U, U)
            turn_nodes(nc, "turn_3", c, U, uT)
            gates = gate[:, :, :].rearrange("p t e -> p (t e)")
            feed_forward(nc, "ffn_3", uT, X, 4 * D, EXPERTS, (mW1, mb1, mW2, mb2),
                         lambda t, e, s: gates[:, at(t * EXPERTS + e)], affine=(ln_g, ln_b))
        store_nodes(nc, X, out)


_INS = ["x", "src", "dst", "L0_gnn_ln1_w", "L0_gnn_ln1_b", "L0_gnn_ln2_w", "L0_gnn_ln2_b", "L0_gnn_wq", "L0_gnn_bq",
        "L0_gnn_wk", "L0_gnn_bk", "L0_gnn_wv", "L0_gnn_bv", "L0_gnn_wskip", "L0_gnn_bskip", "L0_gnn_w1", "L0_gnn_b1",
        "L0_gnn_w2", "L0_gnn_b2", "L0_ffn_Wr", "L0_ffn_br", "L0_ffn_W1", "L0_ffn_b1", "L0_ffn_W2", "L0_ffn_b2",
        "L0_ffn_gamma", "L0_ffn_beta", "L1_gnn_W1", "L1_gnn_b1", "L1_gnn_W2", "L1_gnn_b2", "L1_gnn_a", "L1_ffn_Wr",
        "L1_ffn_br", "L1_ffn_ln_g", "L1_ffn_ln_b", "L1_ffn_W1", "L1_ffn_b1", "L1_ffn_W2", "L1_ffn_b2"]


def kernel(**inputs):
    import numpy as _np
    import concourse.bacc as _bacc
    from concourse import mybir as _mybir
    from concourse.bass_utils import run_bass_kernel_spmd as _run

    nc = _bacc.Bacc("TRN2", target_bir_lowering=False, num_devices=1)
    arrays, args = {}, []
    for name in _INS:
        a = _np.ascontiguousarray(inputs[name])
        arrays[f"in_{name}_dram"] = a
        args.append(nc.dram_tensor(f"in_{name}_dram", a.shape, _mybir.dt.from_np(a.dtype), kind="ExternalInput").ap())
    args.append(nc.dram_tensor("out_0_dram", (N, D), F32, kind="ExternalOutput").ap())
    program(nc, *args)
    r = _run(nc, [arrays], core_ids=[0])
    return r.results[0]["out_0_dram"]
```

```python
from contextlib import ExitStack
import math
import concourse.bass as bass
from concourse import mybir

F32 = mybir.dt.float32
F16 = mybir.dt.float16
BF16 = mybir.dt.bfloat16
I32 = mybir.dt.int32
ALU = mybir.AluOpType
ACT = mybir.ActivationFunctionType
AX = mybir.AxisListType.X
P = 128
N = 3125
D = 256
KD = D // P
E = 53125
HEADS = 4
C = D // HEADS
NT = (N + P - 1) // P
TAIL = N - (NT - 1) * P
EC = (E + P - 1) // P
RING = 8
ET = ((E + NT * (P - 1)) // P + RING) // RING * RING
EXPERTS = 8
EPS = 1e-5
FAR = 1e30
GT = 5
GROUPS = NT // GT
GW = GT * P
ETX = ET + RING
BANK = 512
AW = D + HEADS


def at(i, n=1):
    return bass.ds(i, n)


def flat(ap):
    return ap.rearrange("p o d -> p (o d)")


class Scope:
    def __init__(self, nc, ctx, tag):
        self.nc, self.ctx, self.tag = nc, ctx, tag
        self.sems = []
        ctx.callback(self.end)

    def end(self):
        if self.sems:
            self.nc.clear_and_free_semaphores(self.sems)
            self.nc.all_engine_barrier()

    def sb(self, name, shape, dt=F32):
        return self.ctx.enter_context(self.nc.sbuf_tensor(f"{name}_{self.tag}", shape, dt))

    def ps(self, name, shape, dt=F32):
        return self.ctx.enter_context(self.nc.psum_tensor(f"{name}_{self.tag}", shape, dt))

    def sem(self, name):
        self.sems.append(self.nc.alloc_semaphore(f"{name}_{self.tag}"))
        return self.sems[-1]


def chained(dve, sem):
    step = [0]

    def then(ins):
        step[0] += 1
        ins.then_inc(sem, 1)
        dve.wait_ge(sem, step[0])
    return then


def row(dram, n=D):
    return dram.rearrange("(o d) -> o d", o=1).to_broadcast([P, n])


def constants(nc, sc):
    c = {"iota_t": sc.sb("iota_t", [P, ET], F16), "iota_l": sc.sb("iota_l", [P, P], F16),
         "iota_lf": sc.sb("iota_lf", [P, P]), "iota_b": sc.sb("iota_b", [P, NT]), "iota_tf": sc.sb("iota_tf", [1, ETX]),
         "iota_e": sc.sb("iota_e", [P, EXPERTS]), "below": sc.sb("below", [P, P]), "ones": sc.sb("ones", [P, P]),
         "real": sc.sb("real", [P, P]), "ident": sc.sb("ident", [P, P]), "ident_b": sc.sb("ident_b", [P, P], BF16),
         "ones_b": sc.sb("ones_b", [P, P], BF16)}
    with ExitStack() as inner:
        filled = Scope(nc, inner, "const").sem("filled")
        block = inner.enter_context(nc.Block())

        @block.gpsimd
        def _(pool):
            for name, n in (("iota_t", ET), ("iota_l", P), ("iota_lf", P), ("iota_b", NT), ("iota_tf", ETX)):
                nc.gpsimd.iota(c[name][:, :], [[1, n]], base=0, channel_multiplier=0, allow_small_or_imprecise_dtypes=True)
            nc.gpsimd.iota(c["iota_e"][:, :], [[1, EXPERTS]], base=-EXPERTS, channel_multiplier=0,
                           allow_small_or_imprecise_dtypes=True)
            nc.gpsimd.memset(c["ones_b"][:, :], 1.0).then_inc(filled, 1)
            nc.gpsimd.memset(c["ones"][:, :], 1.0).then_inc(filled, 1)
            pool.wait_ge(filled, 2)
            nc.gpsimd.affine_select(out=c["below"][:, :], in_=c["ones"][:, :], compare_op=ALU.is_gt, fill=0.0, base=0,
                                    pattern=[[1, P]], channel_multiplier=-1)
            nc.gpsimd.affine_select(out=c["real"][:, :], in_=c["ones"][:, :], compare_op=ALU.is_gt, fill=0.0, base=TAIL,
                                    pattern=[[0, P]], channel_multiplier=-1)
            for name, ones in (("ident", "ones"), ("ident_b", "ones_b")):
                nc.gpsimd.affine_select(out=c[name][:, :], in_=c[ones][:, :], compare_op=ALU.is_equal, fill=0.0, base=0,
                                        pattern=[[1, P]], channel_multiplier=-1)
    return c


def load_nodes(nc, x, X):
    with ExitStack() as ctx:
        sc = Scope(nc, ctx, "load")
        cleared, loaded = sc.sem("cleared"), sc.sem("loaded")
        block = ctx.enter_context(nc.Block())

        @block.vector
        def _(dve):
            nc.vector.memset(X[:, NT - 1, :], 0.0).then_inc(cleared, 1)

        @block.sync
        def _(sp):
            sp.dma_start(X[:, 0:NT - 1, :], x[0:(NT - 1) * P, :].rearrange("(b p) d -> p b d", p=P)).then_inc(loaded, 16)
            sp.wait_ge(cleared, 1)
            sp.dma_start(X[0:TAIL, NT - 1, :], x[(NT - 1) * P:N, :]).then_inc(loaded, 16)
            sp.wait_ge(loaded, 32)


def store_nodes(nc, X, out):
    with ExitStack() as ctx:
        stored = Scope(nc, ctx, "store").sem("stored")
        block = ctx.enter_context(nc.Block())

        @block.sync
        def _(sp):
            sp.dma_start(out[0:(NT - 1) * P, :].rearrange("(b p) d -> p b d", p=P), X[:, 0:NT - 1, :]).then_inc(stored, 16)
            sp.dma_start(out[(NT - 1) * P:N, :], X[0:TAIL, NT - 1, :]).then_inc(stored, 16)
            sp.wait_ge(stored, 32)


def sort_edges(nc, tag, key, other, consts, local_of, other_of, bucket_of):
    with ExitStack() as ctx:
        sc = Scope(nc, ctx, tag)
        key_i = sc.sb("key_i", [P, EC], I32)
        oth_i = sc.sb("oth_i", [P, EC], I32)
        tmp_i = sc.sb("tmp_i", [P, EC], I32)
        bucket_f = sc.sb("bucket_f", [P, EC])
        pay = sc.sb("pay", [P, 3, EC])
        member = sc.sb("member", [P, NT, EC])
        running = sc.sb("running", [P, NT, EC])
        zero = sc.sb("zero", [P, 1])
        count = sc.sb("count", [P, NT])
        upto = sc.sb("upto", [P, NT])
        ti = sc.sb("ti", [P, NT], I32)
        tf = sc.sb("tf", [P, NT])
        first = sc.sb("first", [P, NT])
        offset = sc.sb("offset", [P, NT])
        pos_f = sc.sb("pos_f", [P, EC])
        tile_f = sc.sb("tile_f", [P, EC])
        lane_f = sc.sb("lane_f", [P, EC])
        bfl = sc.sb("bfl", [1, ETX])
        in_tile = sc.sb("in_tile", [P, 2, ET], F16)
        in_lane = sc.sb("in_lane", [P, 2, 3, P], F16)
        zl = sc.sb("zl", [P, P], F16)
        zr = sc.sb("zr", [P, ET], F16)
        merged = sc.sb("merged", [P, ET])
        begun = running[0:1, :, :].rearrange("p b j -> p (b j)")[:, 0:NT * (ETX // 2)].rearrange("p (t b) -> p t b", b=NT)
        ps = [sc.ps(f"sorted{k}", [P, 512]) for k in range(3)]
        ps_before = sc.ps("before", [P, NT])
        ps_total = sc.ps("total", [P, NT])
        loaded, padded, chain = sc.sem("loaded"), sc.sem("padded"), sc.sem("chain")
        counted, summed = sc.sem("counted"), sc.sem("summed")
        onehots, onehots_used = sc.sem("onehots"), sc.sem("onehots_used")
        full = E // EC
        block = ctx.enter_context(nc.Block())

        @block.sync
        def _(sp):
            sp.wait_ge(padded, 2)
            for dram, tile in ((key, key_i), (other, oth_i)):
                sp.dma_start(tile[0:full, :], dram[0:full * EC].rearrange("(p j) -> p j", j=EC)).then_inc(loaded, 16)
                sp.dma_start(tile[full:full + 1, 0:E - full * EC],
                             dram[full * EC:E].rearrange("(p j) -> p j", p=1)).then_inc(loaded, 16)

        @block.vector
        def _(dve):
            then = chained(dve, chain)
            nc.vector.memset(key_i[:, :], NT * P).then_inc(padded, 1)
            nc.vector.memset(oth_i[:, :], 0).then_inc(padded, 1)
            nc.vector.memset(zero[:, :], 0.0)
            nc.vector.memset(other_of[:, ET:ETX], 0)
            nc.vector.memset(local_of[:, ET:ETX], -1.0)
            nc.vector.memset(bucket_of[:, :], 0)
            nc.vector.memset(zl[:, :], 0.0)
            then(nc.vector.memset(zr[:, :], 0.0))
            dve.wait_ge(loaded, 64)
            then(nc.vector.tensor_scalar(tmp_i[:, :], key_i[:, :], 7, None, ALU.arith_shift_right))
            then(nc.vector.tensor_copy(bucket_f[:, :], tmp_i[:, :]))
            then(nc.vector.tensor_scalar(tmp_i[:, :], key_i[:, :], P - 1, None, ALU.bitwise_and))
            then(nc.vector.tensor_scalar(pay[:, 0, :], tmp_i[:, :], 1.0, None, ALU.add))
            then(nc.vector.tensor_scalar(tmp_i[:, :], oth_i[:, :], 6, None, ALU.arith_shift_right))
            then(nc.vector.tensor_copy(pay[:, 1, :], tmp_i[:, :]))
            then(nc.vector.tensor_scalar(tmp_i[:, :], oth_i[:, :], 63, None, ALU.bitwise_and))
            then(nc.vector.tensor_copy(pay[:, 2, :], tmp_i[:, :]))
            then(nc.vector.tensor_tensor(member[:, :, :], bucket_f[:, None, :].to_broadcast([P, NT, EC]),
                                         consts["iota_b"][:, :, None].to_broadcast([P, NT, EC]), ALU.is_equal))
            then(nc.vector.tensor_tensor_scan(running[:, :, :].rearrange("p b j -> p (b j)"),
                                              member[:, :, :].rearrange("p b j -> p (b j)"),
                                              zero[:, 0:1].to_broadcast([P, NT * EC]), 0.0, ALU.add, ALU.add))
            then(nc.vector.tensor_copy(upto[:, :], running[:, :, EC - 1]))
            then(nc.vector.tensor_copy(count[:, 0:1], upto[:, 0:1]))
            nc.vector.tensor_tensor(count[:, 1:NT], upto[:, 1:NT], upto[:, 0:NT - 1], ALU.subtract).then_inc(counted, 1)
            dve.wait_ge(summed, 1)
            then(nc.vector.tensor_scalar(ti[:, :], ps_total[:, :], float(P - 1), None, ALU.add))
            then(nc.vector.tensor_scalar(ti[:, :], ti[:, :], 7, None, ALU.arith_shift_right))
            then(nc.vector.tensor_copy(tf[:, :], ti[:, :]))
            then(nc.vector.tensor_tensor_scan(first[:, :], tf[:, :], zero[:, 0:1].to_broadcast([P, NT]), 0.0,
                                              ALU.add, ALU.add))
            then(nc.vector.tensor_tensor(first[:, :], first[:, :], tf[:, :], ALU.subtract))
            then(nc.vector.scalar_tensor_tensor(out=offset[:, :], in0=first[:, :], scalar=float(P), in1=ps_before[:, :],
                                                op0=ALU.mult, op1=ALU.add))
            then(nc.vector.tensor_tensor(offset[:, 1:NT], offset[:, 1:NT], upto[:, 0:NT - 1], ALU.subtract))
            then(nc.vector.tensor_tensor(running[:, :, :], running[:, :, :],
                                         offset[:, :, None].to_broadcast([P, NT, EC]), ALU.add))
            then(nc.vector.tensor_tensor(running[:, :, :], running[:, :, :], member[:, :, :], ALU.mult))
            then(nc.vector.tensor_reduce(pos_f[:, :], running[:, :, :].rearrange("p b j -> p j b"), AX, ALU.add))
            then(nc.vector.tensor_scalar(key_i[:, :], pos_f[:, :], -1.0, None, ALU.add))
            then(nc.vector.tensor_scalar(tmp_i[:, :], key_i[:, :], 7, None, ALU.arith_shift_right))
            then(nc.vector.tensor_copy(tile_f[:, :], tmp_i[:, :]))
            then(nc.vector.tensor_scalar(tmp_i[:, :], key_i[:, :], P - 1, None, ALU.bitwise_and))
            then(nc.vector.tensor_copy(lane_f[:, :], tmp_i[:, :]))
            half = ETX // 2
            for h in range(2):
                then(nc.vector.tensor_tensor(begun, consts["iota_tf"][0:1, h * half:(h + 1) * half, None].to_broadcast([1, half, NT]),
                                             first[0:1, None, :].to_broadcast([1, half, NT]), ALU.is_ge))
                then(nc.vector.tensor_reduce(bfl[:, h * half:(h + 1) * half], begun, AX, ALU.add))
            then(nc.vector.tensor_scalar(bucket_of[:, LEAD:LEAD + ETX], bfl[:, :], -1.0, None, ALU.add))
            nc.vector.sem_inc(onehots_used, 2)
            with dve.Fori(0, EC // 2) as i:
                for u in range(2):
                    j = i * 2 + u
                    dve.wait_ge(onehots_used, j + 1)
                    nc.vector.tensor_scalar(in_tile[:, u, :], consts["iota_t"][:, :], tile_f[:, at(j)], None,
                                            ALU.is_equal).then_inc(onehots, 1)
                    for k in range(3):
                        nc.vector.tensor_scalar(in_lane[:, u, k, :], consts["iota_l"][:, :], lane_f[:, at(j)],
                                                pay[:, k, at(j)], ALU.is_equal, ALU.mult).then_inc(onehots, 1)
            dve.wait_ge(onehots_used, EC + 2)
            then(nc.vector.tensor_scalar(local_of[:, 0:ET], ps[0][:, 0:ET], -1.0, None, ALU.add))
            then(nc.vector.tensor_copy(merged[:, :], ps[2][:, 0:ET]))
            then(nc.vector.scalar_tensor_tensor(out=other_of[:, 0:ET], in0=ps[1][:, 0:ET], scalar=64.0, in1=merged[:, :],
                                                op0=ALU.mult, op1=ALU.add))

        @block.tensor
        def _(pe):
            pe.wait_ge(counted, 1)
            nc.tensor.matmul(ps_before[:, :], consts["below"][:, :], count[:, :], start=True, stop=True)
            nc.tensor.matmul(ps_total[:, :], consts["ones"][:, :], count[:, :], start=True, stop=True).then_inc(summed, 1)
            for k in range(3):
                nc.tensor.matmul(ps[k][:, 0:ET], zl[:, :], zr[:, :], start=True, stop=False, skip_group_check=True)
            with pe.Fori(0, EC // 2) as i:
                for u in range(2):
                    pe.wait_ge(onehots, i * 8 + (4 * u + 4))
                    for k in range(3):
                        mm = nc.tensor.matmul(ps[k][:, 0:ET], in_lane[:, u, k, :], in_tile[:, u, :],
                                              start=False, stop=False, skip_group_check=True)
                    mm.then_inc(onehots_used, 1)


def layer_norm(nc, tag, src, dst, gamma=None, beta=None, add_to=None):
    with ExitStack() as ctx:
        sc = Scope(nc, ctx, tag)
        stats = sc.sb("stats", [P, NT, 6])
        moments = sc.sb("moments", [P, NT, 2])
        rstd = sc.sb("rstd", [P, NT])
        eps = sc.sb("eps", [P, 1])
        g_row = sc.sb("g_row", [P, D])
        b_row = sc.sb("b_row", [P, D])
        loaded, chain, deviated = sc.sem("loaded"), sc.sem("chain"), sc.sem("deviated")
        stats_done, aggregated, scaled = sc.sem("stats_done"), sc.sem("aggregated"), sc.sem("scaled")
        block = ctx.enter_context(nc.Block())

        @block.sync
        def _(sp):
            if gamma is not None:
                sp.dma_start(g_row[:, :], row(gamma)).then_inc(loaded, 16)
                sp.dma_start(b_row[:, :], row(beta)).then_inc(loaded, 16)

        @block.scalar
        def _(act):
            act.wait_ge(aggregated, NT + 1)
            nc.scalar.activation(rstd[:, :], moments[:, :, 1], ACT.Sqrt, bias=eps[:, 0:1]).then_inc(deviated, 1)

        @block.vector
        def _(dve):
            nc.vector.memset(eps[:, :], EPS).then_inc(aggregated, 1)
            with dve.Fori(0, NT) as t:
                nc.vector.bn_stats(flat(stats[:, at(t), :]), flat(src[:, at(t), :])).then_inc(stats_done, 1)
            dve.wait_ge(stats_done, NT)
            for t in range(NT):
                nc.vector.bn_aggr(moments[:, t, :], stats[:, t, :]).then_inc(aggregated, 1)
            then = chained(dve, chain)
            dve.wait_ge(deviated, 1)
            then(nc.vector.reciprocal(rstd[:, :], rstd[:, :]))
            with dve.Fori(0, NT) as t:
                nc.vector.tensor_scalar(flat(dst[:, at(t), :]), flat(src[:, at(t), :]),
                                        flat(moments[:, at(t), 0:1]), rstd[:, at(t)],
                                        ALU.subtract, ALU.mult).then_inc(scaled, 1)
            dve.wait_ge(scaled, NT)
            if gamma is not None:
                dve.wait_ge(loaded, 32)
                then(nc.vector.tensor_tensor(dst[:, :, :], dst[:, :, :], g_row[:, None, :].to_broadcast([P, NT, D]), ALU.mult))
                then(nc.vector.tensor_tensor(dst[:, :, :], dst[:, :, :], b_row[:, None, :].to_broadcast([P, NT, D]), ALU.add))
            if add_to is not None:
                then(nc.vector.tensor_tensor(add_to[:, :, :], add_to[:, :, :], dst[:, :, :], ALU.add))


def in_pairs(eng, body):
    with eng.Fori(0, NT // 2) as i:
        body(i * 2, 2)
    if NT % 2:
        body(NT - 1, 1)


def small_phase(nc, tag, row_dram, work):
    with ExitStack() as ctx:
        sc = Scope(nc, ctx, tag)
        r = sc.sb("r", [P, D])
        loaded, chain = sc.sem("loaded"), sc.sem("chain")
        block = ctx.enter_context(nc.Block())

        @block.sync
        def _(sp):
            if row_dram is not None:
                sp.dma_start(r[:, :], row(row_dram)).then_inc(loaded, 16)

        @block.vector
        def _(dve):
            if row_dram is not None:
                dve.wait_ge(loaded, 16)
            work(r, chained(dve, chain))


def add_row(nc, tag, X, dram):
    small_phase(nc, tag, dram, lambda r, then: then(
        nc.vector.tensor_tensor(X[:, :, :], X[:, :, :], r[:, None, :].to_broadcast([P, NT, D]), ALU.add)))


def project(nc, tag, consts, source, weights, bias_rows, width, steps, handle, stores):
    with ExitStack() as ctx:
        sc = Scope(nc, ctx, tag)
        placed = sc.sb("placed", [P, 2, D])
        turned = sc.sb("turned", [P, 2, D])
        W = sc.sb("W", [P, KD, width])
        biases = sc.sb("biases", [P, width])
        ps_turn = [sc.ps(f"turn{u}", [P, D]) for u in range(2)]
        out = [sc.ps(f"out{u}", [P, max(width, 512) if width > 256 else width]) for u in range(2)]
        loaded, stored = sc.sem("loaded"), sc.sem("stored")
        pool_placed, pe_turned, act_turned = sc.sem("pool_placed"), sc.sem("pe_turned"), sc.sem("act_turned")
        pe_projected, dve_handled = sc.sem("pe_projected"), sc.sem("dve_handled")
        block = ctx.enter_context(nc.Block())

        @block.sync
        def _(sp):
            for dram, c0 in weights:
                sp.dma_start(W[:, :, c0:c0 + dram.shape[1]], dram.rearrange("(k p) n -> p k n", p=P)).then_inc(loaded, 16)
            for dram, c0 in bias_rows:
                sp.dma_start(biases[:, c0:c0 + dram.shape[0]], row(dram, dram.shape[0])).then_inc(loaded, 16)
            if stores:
                sp.wait_ge(dve_handled, (NT + 2) * steps)
                for table, buf in stores:
                    sp.dma_start(table.rearrange("(b p) d -> p b d", p=P), buf[:, :, :]).then_inc(stored, 16)
                sp.wait_ge(stored, 16 * len(stores))

        @block.gpsimd
        def _(pool):
            def body(t0, n):
                for u in range(n):
                    pool.wait_ge(pe_turned, t0 * 2 + (u + 1) * 2)
                    nc.gpsimd.tensor_copy(placed[:, u, :], flat(source[:, at(t0 + u), :])).then_inc(pool_placed, 1)
            in_pairs(pool, body)

        @block.tensor
        def _(pe):
            nc.tensor.sem_inc(pe_turned, 4)
            nc.tensor.sem_inc(pe_projected, 2)
            pe.wait_ge(loaded, 16 * (len(weights) + len(bias_rows)))

            def body(t0, n):
                for u in range(n):
                    pe.wait_ge(pool_placed, t0 + (u + 1))
                    pe.wait_ge(act_turned, t0 + (u + 1))
                    for k in range(KD):
                        nc.tensor.transpose(ps_turn[u][:, k * P:(k + 1) * P], placed[:, u, k * P:(k + 1) * P],
                                            consts["ident"][:, :]).then_inc(pe_turned, 1)
                for u in range(n):
                    pe.wait_ge(act_turned, t0 + (u + 3))
                    pe.wait_ge(dve_handled, t0 * steps + (u + 1) * steps)
                    for c0 in range(0, width, 512):
                        w = min(512, width - c0)
                        for k in range(KD):
                            mm = nc.tensor.matmul(out[u][:, c0:c0 + w], turned[:, u, k * P:(k + 1) * P],
                                                  W[:, k, c0:c0 + w], start=(k == 0), stop=(k == KD - 1))
                    mm.then_inc(pe_projected, 1)
            in_pairs(pe, body)

        @block.scalar
        def _(act):
            nc.scalar.sem_inc(act_turned, 2)

            def body(t0, n):
                for u in range(n):
                    act.wait_ge(pe_turned, t0 * 2 + (u + 3) * 2)
                    act.wait_ge(pe_projected, t0 + (u + 1))
                    nc.scalar.activation(turned[:, u, :], ps_turn[u][:, :], ACT.Copy).then_inc(act_turned, 1)
            in_pairs(act, body)

        @block.vector
        def _(dve):
            nc.vector.sem_inc(dve_handled, 2 * steps)

            def body(t0, n):
                for u in range(n):
                    dve.wait_ge(pe_projected, t0 + (u + 3))
                    made = [0]

                    def then(ins):
                        made[0] += 1
                        ins.then_inc(dve_handled, 1)

                    def settle():
                        dve.wait_ge(dve_handled, t0 * steps + ((u + 2) * steps + made[0]))
                    handle(u, t0 + u, out[u], biases, then, settle)
            in_pairs(dve, body)


def turn_nodes(nc, tag, consts, source, dest):
    with ExitStack() as ctx:
        sc = Scope(nc, ctx, tag)
        placed = sc.sb("placed", [P, 2, D])
        ps_turn = [sc.ps(f"turn{u}", [P, D]) for u in range(2)]
        pool_placed, pe_turned, act_turned = sc.sem("pool_placed"), sc.sem("pe_turned"), sc.sem("act_turned")
        block = ctx.enter_context(nc.Block())

        @block.gpsimd
        def _(pool):
            def body(t0, n):
                for u in range(n):
                    pool.wait_ge(pe_turned, t0 * 2 + (u + 1) * 2)
                    nc.gpsimd.tensor_copy(placed[:, u, :], flat(source[:, at(t0 + u), :])).then_inc(pool_placed, 1)
            in_pairs(pool, body)

        @block.tensor
        def _(pe):
            nc.tensor.sem_inc(pe_turned, 4)

            def body(t0, n):
                for u in range(n):
                    pe.wait_ge(pool_placed, t0 + (u + 1))
                    pe.wait_ge(act_turned, t0 + (u + 1))
                    for k in range(KD):
                        nc.tensor.transpose(ps_turn[u][:, k * P:(k + 1) * P], placed[:, u, k * P:(k + 1) * P],
                                            consts["ident"][:, :]).then_inc(pe_turned, 1)
            in_pairs(pe, body)

        @block.scalar
        def _(act):
            nc.scalar.sem_inc(act_turned, 2)

            def body(t0, n):
                for u in range(n):
                    act.wait_ge(pe_turned, t0 * 2 + (u + 3) * 2)
                    nc.scalar.activation(dest[:, :, at((t0 + u) * P, P)], ps_turn[u][:, :].rearrange("p (k n) -> p k n", k=KD),
                                         ACT.Copy).then_inc(act_turned, 1)
            in_pairs(act, body)


STEP = 2
STEPS = RING // STEP
AHEAD = 4
EARLY = 3
SLOTS = 4


LEAD = 4
BATCH = 12


def bucket_registers(eng, name):
    return [eng.alloc_register(f"{name}{n}") for n in range(BATCH)]


def load_buckets(eng, regs, bucket_of, start):
    eng.load(regs, bucket_of[0:1, at(start, BATCH)])
    return [eng.snap(r, min_val=0, max_val=NT - 1) for r in regs]


def done(eng, sem, i, s, lag=0):
    eng.wait_ge(sem, i * STEPS + (s + 1 + AHEAD - lag))


def gather_rows(nc, pool, table, rows, index, indexed, begun, gathered):
    with pool.Fori(0, ET // RING) as i:
        for r in range(RING):
            if r % STEP == 0:
                pool.wait_ge(indexed, i * STEPS + (r // STEP + 1))
                nc.gpsimd.sem_inc(begun, 1)
            pool.indirect_dma_start(rows[:, r, 0:D], None, table,
                                    bass.IndirectOffsetOnAxis(ap=index[:, r:r + 1], axis=0)).then_inc(gathered[r], 16)


def copy_index(nc, index, other_of, t, s, indexed):
    nc.scalar.activation(index[:, s * STEP:(s + 1) * STEP], other_of[:, at(t, STEP)], ACT.Copy).then_inc(indexed, 1)


def make_onehot(nc, consts, onehot, local_of, t, n, made):
    shape = [P, n, P]
    nc.vector.tensor_tensor(onehot, consts["iota_lf"][:, None, :].to_broadcast(shape),
                            local_of[:, at(t, n), None].to_broadcast(shape), ALU.is_equal).then_inc(made, 1)


def attention_scores(nc, consts, k_table, Q3, edges, scores, most):
    local_of, other_of, bucket_of = edges
    with ExitStack() as ctx:
        sc = Scope(nc, ctx, "score")
        rows = sc.sb("rows", [P, RING, D])
        index = sc.sb("index", [P, RING], I32)
        onehot = sc.sb("onehot", [P, 2, STEP, P])
        turned = sc.sb("turned", [P, SLOTS, STEP, P], BF16)
        away = sc.sb("away", [P, SLOTS, STEP, P], BF16)
        product = sc.sb("product", [P, STEP, D])
        score = sc.sb("score", [P, 2, STEP, HEADS])
        halves = sc.sb("halves", [P, 2, 2, STEP * HEADS], BF16)
        tile_most = sc.sb("tile_most", [P, 2, STEP, HEADS])
        ps_turn = [sc.ps(f"turn{u}", [P, STEP * P]) for u in range(2)]
        ps_q = [sc.ps(f"q{u}", [P, STEP * D]) for u in range(2)]
        ps_all = [sc.ps(f"all{u}", [P, STEP, HEADS * P]) for u in range(2)]
        gathered = [sc.sem(f"gathered{r}") for r in range(RING)]
        indexed, begun, cleared = sc.sem("indexed"), sc.sem("begun"), sc.sem("cleared")
        dve_onehot, pe_turned, act_turned, act_away = (sc.sem(s) for s in ("dve_onehot", "pe_turned", "act_turned", "act_away"))
        pe_q, dve_product, dve_score, act_kept = (sc.sem(s) for s in ("pe_q", "dve_product", "dve_score", "act_kept"))
        dve_upper, dve_halves, pe_all, dve_most, dve_merged = (sc.sem(s) for s in (
            "dve_upper", "dve_halves", "pe_all", "dve_most", "dve_merged"))
        block = ctx.enter_context(nc.Block())

        @block.gpsimd
        def _(pool):
            gather_rows(nc, pool, k_table, rows, index, indexed, begun, gathered)

        @block.scalar
        def _(act):
            for s in (act_turned, act_away, act_kept):
                nc.scalar.sem_inc(s, AHEAD)
            for s in range(STEPS):
                copy_index(nc, index, other_of, s * STEP, s, indexed)

            def turn(i, s):
                u, v = s % 2, s % SLOTS
                done(act, pe_turned, i, s)
                done(act, pe_q, i, s, SLOTS)
                nc.scalar.activation(turned[:, v, :, :].rearrange("p g e -> p (g e)"), ps_turn[u][:, :],
                                     ACT.Copy).then_inc(act_turned, 1)
                done(act, pe_all, i, s, SLOTS)
                nc.scalar.activation(away[:, v, :, :].rearrange("p g e -> p (g e)"), ps_turn[u][:, :], ACT.Copy, bias=-FAR,
                                     scale=FAR).then_inc(act_away, 1)
            for s in range(EARLY):
                turn(0, s)
            with act.Fori(0, ET // RING) as i:
                for s in range(STEPS):
                    done(act, dve_product, i, s)
                    copy_index(nc, index, other_of, i * RING + (s * STEP + RING), s, indexed)
                    done(act, dve_score, i, s)
                    nc.scalar.activation(scores[:, at(i * RING + s * STEP, STEP), :], score[:, s % 2, :, :],
                                         ACT.Copy).then_inc(act_kept, 1)
                    turn(i, s + EARLY)

        @block.tensor
        def _(pe):
            for s in (pe_turned, pe_q, pe_all):
                nc.tensor.sem_inc(s, AHEAD)

            def turn(i, s):
                u = s % 2
                done(pe, dve_onehot, i, s)
                done(pe, act_away, i, s, 2)
                for g in range(STEP):
                    tr = nc.tensor.transpose(ps_turn[u][:, g * P:(g + 1) * P], onehot[:, u, g, :], consts["ident"][:, :])
                tr.then_inc(pe_turned, 1)

            regs = bucket_registers(pe, "pe_score")

            def take_q(i, s, buckets):
                u = s % 2
                done(pe, act_turned, i, s)
                done(pe, dve_product, i, s, 2)
                for g in range(STEP):
                    b = buckets[s * STEP + g]
                    for part in range(3):
                        mm = nc.tensor.matmul(ps_q[u][:, g * D:(g + 1) * D], turned[:, s % SLOTS, g, :],
                                              Q3[:, at(b), part * D:(part + 1) * D].rearrange("p o d -> p (o d)"),
                                              start=(part == 0), stop=(part == 2))
                mm.then_inc(pe_q, 1)

            def spread(i, s):
                u = s % 2
                done(pe, act_away, i, s)
                done(pe, dve_halves, i, s)
                done(pe, dve_most, i, s, 2)
                for g in range(STEP):
                    nc.tensor.matmul(ps_all[u][:, g, :].rearrange("p (h e) -> p h e", h=HEADS), consts["ident_b"][:, :],
                                     away[:, s % SLOTS, g, None, :].to_broadcast([P, HEADS, P]), start=True, stop=False,
                                     skip_group_check=True)
                    for h in range(HEADS):
                        for part in range(2):
                            c = g * HEADS + h
                            mm = nc.tensor.matmul(ps_all[u][:, g, h * P:(h + 1) * P],
                                                  halves[:, u, part, c:c + 1].to_broadcast([P, P]), consts["ident_b"][:, :],
                                                  start=False, stop=(h == HEADS - 1 and part == 1), skip_group_check=True)
                mm.then_inc(pe_all, 1)
            for s in range(EARLY):
                turn(0, s)
            take_q(0, 0, load_buckets(pe, regs, bucket_of, LEAD))
            with pe.Fori(0, ET // RING) as i:
                buckets = load_buckets(pe, regs, bucket_of, i * RING + LEAD)
                for s in range(STEPS):
                    take_q(i, s + 1, buckets)
                    spread(i, s)
                    turn(i, s + EARLY)

        @block.vector
        def _(dve):
            for s in (dve_onehot, dve_product, dve_score, dve_upper, dve_halves, dve_most):
                nc.vector.sem_inc(s, AHEAD)
            nc.vector.memset(most[:, :, :], -FAR).then_inc(cleared, 1)
            nc.vector.memset(scores[:, ET:ETX, :], 0.0).then_inc(cleared, 1)
            dve.wait_ge(cleared, 2)

            def onehots(i, s):
                done(dve, pe_turned, i, s, 2)
                make_onehot(nc, consts, onehot[:, s % 2, :, :], local_of, i * RING + s * STEP, STEP, dve_onehot)

            def multiply(i, s):
                done(dve, pe_q, i, s)
                for g in range(STEP):
                    dve.wait_ge(gathered[s * STEP + g], i * 16 + 16)
                done(dve, dve_score, i, s, 1)
                nc.vector.tensor_tensor(product[:, :, :].rearrange("p g d -> p (g d)"), ps_q[s % 2][:, :],
                                        rows[:, s * STEP:(s + 1) * STEP, :].rearrange("p g d -> p (g d)"),
                                        ALU.mult).then_inc(dve_product, 1)

            def sum_up(i, s):
                done(dve, dve_product, i, s)
                done(dve, act_kept, i, s, 2)
                nc.vector.tensor_reduce(score[:, s % 2, :, :], product[:, :, :].rearrange("p g (h c) -> p g h c", h=HEADS),
                                        AX, ALU.add).then_inc(dve_score, 1)

            def upper_half(i, s):
                done(dve, dve_score, i, s)
                done(dve, pe_all, i, s, 2)
                nc.vector.tensor_copy(halves[:, s % 2, 0, :],
                                      score[:, s % 2, :, :].rearrange("p g h -> p (g h)")).then_inc(dve_upper, 1)

            def lower_half(i, s):
                done(dve, dve_upper, i, s)
                nc.vector.tensor_tensor(halves[:, s % 2, 1, :], score[:, s % 2, :, :].rearrange("p g h -> p (g h)"),
                                        halves[:, s % 2, 0, :], ALU.subtract).then_inc(dve_halves, 1)

            def find_most(i, s):
                u = s % 2
                done(dve, pe_all, i, s)
                nc.vector.tensor_reduce(tile_most[:, u, :, :], ps_all[u][:, :, :].rearrange("p g (h e) -> p g h e", h=HEADS),
                                        AX, ALU.max).then_inc(dve_most, 1)

            def merge(i, s, g, buckets):
                if g == 0:
                    done(dve, dve_most, i, s)
                cur = flat(most[:, at(buckets[LEAD + s * STEP + g]), :])
                dve.wait_ge(dve_merged, i * RING + (s * STEP + g + RING))
                nc.vector.tensor_tensor(cur, cur, tile_most[:, s % 2, g, :], ALU.max).then_inc(dve_merged, 1)

            regs = bucket_registers(dve, "dve_score")

            def round_of(i, first=False):
                buckets = load_buckets(dve, regs, bucket_of, i * RING)
                for s in range(STEPS):
                    merging = s > 1 or not first
                    multiply(i, s)
                    if merging:
                        merge(i, s - 2, 0, buckets)
                    sum_up(i, s)
                    if merging:
                        merge(i, s - 2, 1, buckets)
                    upper_half(i, s)
                    onehots(i, s + EARLY)
                    lower_half(i, s)
                    if s > 0 or not first:
                        find_most(i, s - 1)
            nc.vector.sem_inc(dve_merged, RING)
            for s in range(EARLY):
                onehots(0, s)
            round_of(0, first=True)
            with dve.Fori(1, ET // RING) as i:
                round_of(i)
            last = ET // RING - 1
            buckets = load_buckets(dve, regs, bucket_of, last * RING)
            find_most(last, STEPS - 1)
            for s in (STEPS - 2, STEPS - 1):
                for g in range(STEP):
                    merge(last, s, g, buckets)


def attend(nc, consts, v_table, edges, total, scores, most2):
    local_of, other_of, bucket_of = edges
    with ExitStack() as ctx:
        sc = Scope(nc, ctx, "attend")
        rows = sc.sb("rows", [P, RING, D])
        index = sc.sb("index", [P, RING], I32)
        onehot = sc.sb("onehot", [P, SLOTS, STEP, P])
        turned = sc.sb("turned", [P, 2, STEP, P], BF16)
        less = sc.sb("less", [P, 2, STEP, HEADS])
        message = sc.sb("message", [P, 2, STEP, AW])
        ps_turn = [sc.ps(f"turn{u}", [P, BANK]) for u in range(2)]
        ps_most = [sc.ps(f"most{u}", [P, BANK]) for u in range(2)]
        ps_sum = [[sc.ps(f"sum{u}{g}", [P, BANK]) for g in range(STEP)] for u in range(2)]
        gathered = [sc.sem(f"gathered{r}") for r in range(RING)]
        indexed, begun, cleared, each_added = sc.sem("indexed"), sc.sem("begun"), sc.sem("cleared"), sc.sem("each_added")
        dve_onehot, pe_turned, act_turned, pe_most = (sc.sem(s) for s in ("dve_onehot", "pe_turned", "act_turned", "pe_most"))
        dve_less, act_exp, dve_message, pe_summed = (sc.sem(s) for s in ("dve_less", "act_exp", "dve_message", "pe_summed"))
        block = ctx.enter_context(nc.Block())

        @block.gpsimd
        def _(pool):
            gather_rows(nc, pool, v_table, rows, index, indexed, begun, gathered)

        @block.scalar
        def _(act):
            for s in (act_turned, act_exp):
                nc.scalar.sem_inc(s, AHEAD)
            for s in range(STEPS):
                copy_index(nc, index, other_of, s * STEP, s, indexed)

            def turn(i, s):
                u = s % 2
                done(act, pe_turned, i, s)
                done(act, pe_most, i, s, 2)
                nc.scalar.activation(turned[:, u, :, :].rearrange("p g e -> p (g e)"), ps_turn[u][:, 0:STEP * P],
                                     ACT.Copy).then_inc(act_turned, 1)

            def exponential(i, s):
                u = s % 2
                done(act, dve_less, i, s)
                done(act, pe_summed, i, s, 2)
                nc.scalar.activation(message[:, u, :, D:AW], less[:, u, :, :], ACT.Exp).then_inc(act_exp, 1)
            turn(0, 0)
            turn(0, 1)
            exponential(0, 0)
            with act.Fori(0, ET // RING) as i:
                for s in range(STEPS):
                    exponential(i, s + 1)
                    turn(i, s + 2)
                    done(act, dve_message, i, s)
                    copy_index(nc, index, other_of, i * RING + (s * STEP + RING), s, indexed)

        @block.tensor
        def _(pe):
            for s in (pe_turned, pe_most, pe_summed):
                nc.tensor.sem_inc(s, AHEAD)

            regs = bucket_registers(pe, "pe_attend")

            def turn(i, s):
                u = s % 2
                done(pe, dve_onehot, i, s)
                done(pe, act_turned, i, s, 2)
                for g in range(STEP):
                    tr = nc.tensor.transpose(ps_turn[u][:, g * P:(g + 1) * P], onehot[:, s % SLOTS, g, :],
                                             consts["ident"][:, :])
                tr.then_inc(pe_turned, 1)

            def take_most(i, s, buckets):
                u = s % 2
                done(pe, act_turned, i, s)
                done(pe, dve_less, i, s, 2)
                for g in range(STEP):
                    b = buckets[s * STEP + g]
                    for part in range(2):
                        mm = nc.tensor.matmul(ps_most[u][:, g * HEADS:(g + 1) * HEADS], turned[:, u, g, :],
                                              most2[:, at(b), part * HEADS:(part + 1) * HEADS].rearrange("p o d -> p (o d)"),
                                              start=(part == 0), stop=(part == 1))
                mm.then_inc(pe_most, 1)

            def sum_up(i, s):
                u = s % 2
                done(pe, dve_message, i, s)
                pe.wait_ge(each_added, i * RING + ((s - 1) * STEP + AHEAD * STEP))
                for g in range(STEP):
                    mm = nc.tensor.matmul(ps_sum[u][g][:, 0:AW], onehot[:, s % SLOTS, g, :], message[:, u, g, :], start=True,
                                          stop=True)
                mm.then_inc(pe_summed, 1)

            for s in range(EARLY):
                turn(0, s)
            buckets = load_buckets(pe, regs, bucket_of, LEAD)
            take_most(0, 0, buckets)
            take_most(0, 1, buckets)
            with pe.Fori(0, ET // RING) as i:
                buckets = load_buckets(pe, regs, bucket_of, i * RING + LEAD)
                for s in range(STEPS):
                    sum_up(i, s)
                    take_most(i, s + 2, buckets)
                    turn(i, s + EARLY)

        @block.vector
        def _(dve):
            for s in (dve_onehot, dve_less, dve_message):
                nc.vector.sem_inc(s, AHEAD)
            nc.vector.sem_inc(each_added, AHEAD * STEP)
            nc.vector.memset(total[:, :, :], 0.0).then_inc(cleared, 1)
            dve.wait_ge(cleared, 1)

            def onehots(i, s):
                done(dve, pe_summed, i, s, SLOTS)
                make_onehot(nc, consts, onehot[:, s % SLOTS, :, :], local_of, i * RING + s * STEP, STEP, dve_onehot)

            def subtract_most(i, s):
                u = s % 2
                done(dve, pe_most, i, s)
                done(dve, act_exp, i, s, 2)
                nc.vector.tensor_tensor(less[:, u, :, :], scores[:, at(i * RING + s * STEP, STEP), :],
                                        ps_most[u][:, 0:STEP * HEADS].rearrange("p (g h) -> p g h", g=STEP),
                                        ALU.subtract).then_inc(dve_less, 1)

            def weigh(i, s):
                u = s % 2
                done(dve, act_exp, i, s)
                for g in range(STEP):
                    dve.wait_ge(gathered[s * STEP + g], i * 16 + 16)
                nc.vector.tensor_tensor(message[:, u, :, 0:D].rearrange("p g (h c) -> p g h c", h=HEADS),
                                        rows[:, s * STEP:(s + 1) * STEP, :].rearrange("p g (h c) -> p g h c", h=HEADS),
                                        message[:, u, :, D:AW, None].to_broadcast([P, STEP, HEADS, C]),
                                        ALU.mult).then_inc(dve_message, 1)

            regs = bucket_registers(dve, "dve_attend")

            def round_of(i, first=False):
                buckets = load_buckets(dve, regs, bucket_of, i * RING)
                for s in range(STEPS):
                    adding = s > 0 or not first
                    weigh(i, s)
                    subtract_most(i, s + 1)
                    if adding:
                        add_sum(nc, dve, total, ps_sum[(s - 1) % 2], buckets, i, s - 1, 0, AW, pe_summed, each_added)
                    onehots(i, s + EARLY)
                    if adding:
                        add_sum(nc, dve, total, ps_sum[(s - 1) % 2], buckets, i, s - 1, 1, AW, pe_summed, each_added)
            for s in range(EARLY):
                onehots(0, s)
            subtract_most(0, 0)
            round_of(0, first=True)
            with dve.Fori(1, ET // RING) as i:
                round_of(i)
            buckets = load_buckets(dve, regs, bucket_of, ET - RING)
            for g in range(STEP):
                add_sum(nc, dve, total, ps_sum[(STEPS - 1) % 2], buckets, ET // RING - 1, STEPS - 1, g, AW, pe_summed,
                        each_added)


def add_sum(nc, dve, total, ps, buckets, i, s, g, width, pe_summed, each_added):
    if g == 0:
        done(dve, pe_summed, i, s)
    cur = flat(total[:, at(buckets[LEAD + s * STEP + g]), 0:width])
    dve.wait_ge(each_added, i * RING + (s * STEP + g + AHEAD * STEP))
    nc.vector.tensor_tensor(cur, cur, ps[g][:, 0:width], ALU.add).then_inc(each_added, 1)


def edge_sums(nc, tag, consts, table, edges, total):
    local_of, other_of, bucket_of = edges
    with ExitStack() as ctx:
        sc = Scope(nc, ctx, tag)
        rows = sc.sb("rows", [P, RING, D + 1])
        index = sc.sb("index", [P, RING], I32)
        onehot = sc.sb("onehot", [P, 2, STEP, P])
        ps_sum = [[sc.ps(f"sum{u}{g}", [P, 512]) for g in range(STEP)] for u in range(2)]
        gathered = [sc.sem(f"gathered{r}") for r in range(RING)]
        indexed, begun, cleared, each_added = sc.sem("indexed"), sc.sem("begun"), sc.sem("cleared"), sc.sem("each_added")
        dve_onehot, pe_summed = sc.sem("dve_onehot"), sc.sem("pe_summed")
        block = ctx.enter_context(nc.Block())

        @block.gpsimd
        def _(pool):
            gather_rows(nc, pool, table, rows, index, indexed, begun, gathered)

        @block.scalar
        def _(act):
            for s in range(STEPS):
                copy_index(nc, index, other_of, s * STEP, s, indexed)
            with act.Fori(0, ET // RING) as i:
                for s in range(STEPS):
                    done(act, pe_summed, i, s)
                    copy_index(nc, index, other_of, i * RING + (s * STEP + RING), s, indexed)

        @block.tensor
        def _(pe):
            nc.tensor.sem_inc(pe_summed, AHEAD)
            pe.wait_ge(cleared, 2)
            with pe.Fori(0, ET // RING) as i:
                for s in range(STEPS):
                    u = s % 2
                    done(pe, dve_onehot, i, s)
                    pe.wait_ge(each_added, i * RING + ((s - 1) * STEP + AHEAD * STEP))
                    for g in range(STEP):
                        r = s * STEP + g
                        pe.wait_ge(gathered[r], i * 16 + 16)
                        mm = nc.tensor.matmul(ps_sum[u][g][:, 0:D + 1], onehot[:, u, g, :], rows[:, r, :], start=True, stop=True)
                    mm.then_inc(pe_summed, 1)

        @block.vector
        def _(dve):
            nc.vector.sem_inc(dve_onehot, AHEAD)
            nc.vector.sem_inc(each_added, AHEAD * STEP)
            nc.vector.memset(total[:, :, :], 0.0).then_inc(cleared, 1)
            nc.vector.memset(rows[:, :, D:D + 1], 1.0).then_inc(cleared, 1)
            dve.wait_ge(cleared, 2)

            def onehots(i, s):
                done(dve, pe_summed, i, s, 2)
                make_onehot(nc, consts, onehot[:, s % 2, :, :], local_of, i * RING + s * STEP, STEP, dve_onehot)
            regs = bucket_registers(dve, f"dve_{tag}")
            onehots(0, 0)
            with dve.Fori(0, ET // RING) as i:
                buckets = load_buckets(dve, regs, bucket_of, i * RING)
                for s in range(STEPS):
                    onehots(i, s + 1)
                    for g in range(STEP):
                        add_sum(nc, dve, total, ps_sum[s % 2], buckets, i, s, g, D + 1, pe_summed, each_added)


def join_attention(nc, total, skip, X):
    with ExitStack() as ctx:
        sc = Scope(nc, ctx, "join")
        none = sc.sb("none", [P, NT, HEADS])
        chain = sc.sem("chain")
        block = ctx.enter_context(nc.Block())

        @block.vector
        def _(dve):
            then = chained(dve, chain)
            den = total[:, :, D:AW]
            then(nc.vector.tensor_scalar(none[:, :, :], den, 0.0, None, ALU.is_equal))
            then(nc.vector.tensor_tensor(none[:, :, :], none[:, :, :], den, ALU.add))
            then(nc.vector.reciprocal(none[:, :, :], none[:, :, :]))
            for h in range(HEADS):
                part = total[:, :, h * C:(h + 1) * C]
                then(nc.vector.tensor_tensor(part, part, none[:, :, h:h + 1].to_broadcast([P, NT, C]), ALU.mult))
            then(nc.vector.tensor_tensor(skip[:, :, :], skip[:, :, :], total[:, :, 0:D], ALU.add))
            then(nc.vector.tensor_tensor(X[:, :, :], X[:, :, :], skip[:, :, :], ALU.add))


def divide_by_count(nc, tag, total, table=None, bias=None, slope=None, residual=None, dest=None, add_to=None):
    with ExitStack() as ctx:
        sc = Scope(nc, ctx, tag)
        inv = sc.sb("inv", [P, NT])
        some = sc.sb("some", [P, NT])
        b_row = sc.sb("b_row", [P, D])
        a = sc.sb("a", [P, 1])
        low = sc.sb("low", [P, NT, D]) if dest is not None or add_to is not None else None
        loaded, chain, divided, stored = sc.sem("loaded"), sc.sem("chain"), sc.sem("divided"), sc.sem("stored")
        block = ctx.enter_context(nc.Block())

        @block.sync
        def _(sp):
            if table is not None:
                sp.wait_ge(divided, 1)
                sp.dma_start(table.rearrange("(b p) d -> p b d", p=P), total[:, :, 0:D]).then_inc(stored, 16)
                sp.wait_ge(stored, 16)
            else:
                sp.dma_start(b_row[:, :], row(bias)).then_inc(loaded, 16)
                sp.dma_start(a[:, :], row(slope, 1)).then_inc(loaded, 16)

        @block.vector
        def _(dve):
            then = chained(dve, chain)
            count = total[:, :, D]
            then(nc.vector.tensor_scalar(inv[:, :], count, 1.0, None, ALU.max))
            then(nc.vector.reciprocal(inv[:, :], inv[:, :]))
            then(nc.vector.tensor_scalar(some[:, :], count, 1.0, None, ALU.min))
            then(nc.vector.tensor_tensor(inv[:, :], inv[:, :], some[:, :], ALU.mult))
            body = total[:, :, 0:D]
            then(nc.vector.tensor_tensor(body, body, inv[:, :, None].to_broadcast([P, NT, D]), ALU.mult))
            if table is not None:
                nc.vector.sem_inc(divided, 1)
                return
            dve.wait_ge(loaded, 32)
            then(nc.vector.tensor_tensor(body, body, b_row[:, None, :].to_broadcast([P, NT, D]), ALU.add))
            if residual is not None:
                then(nc.vector.tensor_tensor(body, body, residual[:, :, :], ALU.add))
            then(nc.vector.tensor_scalar(low[:, :, :], body, 0.0, a[:, 0:1], ALU.min, ALU.mult))
            if dest is not None:
                then(nc.vector.scalar_tensor_tensor(out=dest[:, :, :], in0=body, scalar=0.0, in1=low[:, :, :],
                                                    op0=ALU.max, op1=ALU.add))
            else:
                then(nc.vector.scalar_tensor_tensor(out=body, in0=body, scalar=0.0, in1=low[:, :, :],
                                                    op0=ALU.max, op1=ALU.add))
                then(nc.vector.tensor_tensor(add_to[:, :, :], add_to[:, :, :], body, ALU.add))


def top_two(nc, sc, then, consts, probs, T):
    found = []
    left = probs
    for n in range(2):
        best = sc[f"best{n}"]
        first = sc[f"first{n}"]
        one = sc[f"one{n}"]
        wide = [P, T, EXPERTS]
        names = consts["iota_e"][:, None, :].to_broadcast(wide)
        then(nc.vector.tensor_reduce(best[:, :], left[:, :, :], AX, ALU.max))
        then(nc.vector.tensor_tensor(one[:, :, :], left[:, :, :], best[:, :, None].to_broadcast(wide), ALU.is_equal))
        then(nc.vector.tensor_tensor(one[:, :, :], one[:, :, :], names, ALU.mult))
        then(nc.vector.tensor_reduce(first[:, :], one[:, :, :], AX, ALU.min))
        then(nc.vector.tensor_tensor(one[:, :, :], first[:, :, None].to_broadcast(wide), names, ALU.is_equal))
        if n == 0:
            then(nc.vector.scalar_tensor_tensor(out=sc["left"][:, :, :], in0=one[:, :, :], scalar=-4.0, in1=probs[:, :, :],
                                                op0=ALU.mult, op1=ALU.add))
            left = sc["left"]
        found.append((best, first, one))
    return found


def top_buffers(sc, T):
    out = {"left": sc.sb("left", [P, T, EXPERTS])}
    for n in range(2):
        out[f"best{n}"] = sc.sb(f"best{n}", [P, T])
        out[f"first{n}"] = sc.sb(f"first{n}", [P, T])
        out[f"one{n}"] = sc.sb(f"one{n}", [P, T, EXPERTS])
    return out


def softmax_steps(nc, dve, then, peak, sums, x, T, exp_asked, exp_done, n):
    shape = [P, T, x.shape[2]]
    then(nc.vector.tensor_reduce(peak[:, :], x[:, :, :], AX, ALU.max))
    nc.vector.tensor_tensor(x[:, :, :], x[:, :, :], peak[:, :, None].to_broadcast(shape), ALU.subtract).then_inc(exp_asked, 1)
    dve.wait_ge(exp_done, n)
    then(nc.vector.tensor_reduce(sums[:, :], x[:, :, :], AX, ALU.add))
    then(nc.vector.reciprocal(sums[:, :], sums[:, :]))
    then(nc.vector.tensor_tensor(x[:, :, :], x[:, :, :], sums[:, :, None].to_broadcast(shape), ALU.mult))


def route_all(nc, consts, U, Wr, br, chosen, gate):
    capacity = float(math.ceil(N * 1.25 / EXPERTS))
    with ExitStack() as ctx:
        sc = Scope(nc, ctx, "route")
        wr = sc.sb("wr", [P, D, EXPERTS])
        wide = sc.sb("wide", [P, D, EXPERTS])
        br_row = sc.sb("br_row", [P, 1, EXPERTS])
        mean = sc.sb("mean", [P, D])
        rw = sc.sb("rw", [P, 1, EXPERTS])
        load = sc.sb("load", [P, 1, EXPERTS])
        over = sc.sb("over", [P, 1, EXPERTS])
        two = sc.sb("two", [P, 1, 2])
        peak, sums = sc.sb("peak", [P, 1]), sc.sb("sums", [P, 1])
        tops = top_buffers(sc, 1)
        total = sc.ps("total", [P, D])
        loaded, chain, summed = sc.sem("loaded"), sc.sem("chain"), sc.sem("summed")
        exp_asked, exp_done = sc.sem("exp_asked"), sc.sem("exp_done")
        block = ctx.enter_context(nc.Block())

        @block.sync
        def _(sp):
            sp.dma_start(wr[:, :, :].rearrange("p d e -> p (d e)"), row(Wr.rearrange("d e -> (d e)"), D * EXPERTS)).then_inc(loaded, 16)
            sp.dma_start(br_row[:, 0, :], row(br, EXPERTS)).then_inc(loaded, 16)

        @block.tensor
        def _(pe):
            nc.tensor.matmul(total[:, :], consts["real"][:, :], U[:, NT - 1, :], start=True, stop=False)
            for t in range(NT - 1):
                mm = nc.tensor.matmul(total[:, :], consts["ones"][:, :], U[:, t, :], start=False, stop=(t == NT - 2))
            mm.then_inc(summed, 1)

        @block.scalar
        def _(act):
            for n, x in enumerate((rw, rw, two)):
                act.wait_ge(exp_asked, n + 1)
                nc.scalar.activation(x[:, :, :], x[:, :, :], ACT.Exp).then_inc(exp_done, 1)

        @block.vector
        def _(dve):
            then = chained(dve, chain)
            dve.wait_ge(loaded, 32)
            dve.wait_ge(summed, 1)
            then(nc.vector.tensor_scalar(mean[:, :], total[:, :], 1.0 / N, None, ALU.mult))
            then(nc.vector.tensor_tensor(wide[:, :, :], wr[:, :, :], mean[:, :, None].to_broadcast([P, D, EXPERTS]), ALU.mult))
            then(nc.vector.tensor_reduce(rw[:, 0, :], wide[:, :, :].rearrange("p d e -> p e d"), AX, ALU.add))
            then(nc.vector.tensor_tensor(rw[:, :, :], rw[:, :, :], br_row[:, :, :], ALU.add))
            softmax_steps(nc, dve, then, peak, sums, rw, 1, exp_asked, exp_done, 1)
            then(nc.vector.tensor_scalar(load[:, :, :], rw[:, :, :], float(N), None, ALU.mult))
            then(nc.vector.tensor_scalar(over[:, :, :], load[:, :, :], capacity, None, ALU.max))
            then(nc.vector.reciprocal(over[:, :, :], over[:, :, :]))
            then(nc.vector.scalar_tensor_tensor(out=rw[:, :, :], in0=over[:, :, :], scalar=capacity, in1=rw[:, :, :],
                                                op0=ALU.mult, op1=ALU.mult))
            softmax_steps(nc, dve, then, peak, sums, rw, 1, exp_asked, exp_done, 2)
            found = top_two(nc, tops, then, consts, rw, 1)
            for n, (best, first, one) in enumerate(found):
                then(nc.vector.tensor_copy(two[:, 0, n:n + 1], best[:, :]))
                then(nc.vector.tensor_scalar(chosen[:, n:n + 1], first[0:1, :], float(EXPERTS), None, ALU.add))
            softmax_steps(nc, dve, then, peak, sums, two, 1, exp_asked, exp_done, 3)
            then(nc.vector.tensor_copy(gate[:, :], two[:, 0, :]))


def route_each(nc, consts, logits, br, gate):
    with ExitStack() as ctx:
        sc = Scope(nc, ctx, "each")
        br_row = sc.sb("br_row", [P, EXPERTS])
        peak, sums = sc.sb("peak", [P, NT]), sc.sb("sums", [P, NT])
        tops = top_buffers(sc, NT)
        loaded, chain, exp_asked, exp_done = sc.sem("loaded"), sc.sem("chain"), sc.sem("exp_asked"), sc.sem("exp_done")
        block = ctx.enter_context(nc.Block())
        wide = [P, NT, EXPERTS]

        @block.sync
        def _(sp):
            sp.dma_start(br_row[:, :], row(br, EXPERTS)).then_inc(loaded, 16)

        @block.scalar
        def _(act):
            act.wait_ge(exp_asked, 1)
            nc.scalar.activation(logits[:, :, :], logits[:, :, :], ACT.Exp).then_inc(exp_done, 1)

        @block.vector
        def _(dve):
            then = chained(dve, chain)
            dve.wait_ge(loaded, 16)
            then(nc.vector.tensor_tensor(logits[:, :, :], logits[:, :, :], br_row[:, None, :].to_broadcast(wide), ALU.add))
            softmax_steps(nc, dve, then, peak, sums, logits, NT, exp_asked, exp_done, 1)
            (p1, _, one1), (p2, _, one2) = top_two(nc, tops, then, consts, logits, NT)
            then(nc.vector.tensor_tensor(sums[:, :], p1[:, :], p2[:, :], ALU.add))
            then(nc.vector.reciprocal(sums[:, :], sums[:, :]))
            for p, one in ((p1, one1), (p2, one2)):
                then(nc.vector.tensor_tensor(p[:, :], p[:, :], sums[:, :], ALU.mult))
                then(nc.vector.tensor_tensor(one[:, :, :], one[:, :, :], p[:, :, None].to_broadcast(wide), ALU.mult))
            then(nc.vector.tensor_tensor(gate[:, :, :], one1[:, :, :], one2[:, :, :], ALU.add))


def feed_forward(nc, tag, uT, acc, F, experts, params, gate, chosen=None, affine=None):
    W1, b1, W2, b2 = params
    J = F // P
    slots = min(2, experts)
    half = GW // 2
    with ExitStack() as ctx:
        sc = Scope(nc, ctx, tag)
        w1 = [sc.sb(f"w1_{s}", [P, KD, F]) for s in range(slots)]
        w2 = [sc.sb(f"w2_{s}", [P, J, D]) for s in range(slots)]
        b1c = [sc.sb(f"b1_{s}", [P, J]) for s in range(slots)]
        b2r = [sc.sb(f"b2_{s}", [P, D]) for s in range(slots)]
        gc = [sc.sb(f"gc_{s}", [P, KD]) for s in range(slots)]
        bc = [sc.sb(f"bc_{s}", [P, KD]) for s in range(slots)]
        xe = sc.sb("xe", [P, KD, GW])
        hid = sc.sb("hid", [P, J, GW])
        part = sc.sb("part", [P, 2, D])
        ps_h = [sc.ps(f"h{u}", [P, 2, 512]) for u in range(2)]
        ps_y = [sc.ps(f"y{u}", [P, D]) for u in range(2)]
        loaded = [sc.sem(f"loaded{s}") for s in range(slots)]
        weights_used, pool_x, pe_h, act_h = (sc.sem(s) for s in ("weights_used", "pool_x", "pe_h", "act_h"))
        pe_y, dve_part, dve_acc = (sc.sem(s) for s in ("pe_y", "dve_part", "dve_acc"))
        loads = 4 + (2 if affine else 0)
        xs = KD * (2 if affine else 1)
        started = sc.sem("started")
        block = ctx.enter_context(nc.Block())

        def each(eng, body, before=None, after=None):
            def pair(ep):
                for s in range(slots):
                    if before:
                        before(s, ep)
                    with eng.Fori(0, GROUPS) as g:
                        body(s, ep * slots + s, g, (ep * slots + s) * GROUPS + g)
                    if after:
                        after(s, ep)
            if experts > slots:
                with eng.Fori(0, experts // slots) as ep:
                    pair(ep)
            else:
                pair(0)

        @block.sync
        def _(sp):
            def load(s, ep):
                e = ep * slots + s
                if chosen is not None:
                    e = sp.value_load(chosen[0:1, s:s + 1], min_val=0, max_val=EXPERTS - 1)
                sp.wait_ge(weights_used, e + 1) if chosen is None else None
                lot = [(w1[s][:, :, :], W1[at(e), :, :].rearrange("o (k p) f -> p (o k) f", p=P)),
                       (w2[s][:, :, :], W2[at(e), :, :].rearrange("o (j p) d -> p (o j) d", p=P)),
                       (b1c[s][:, :], b1[at(e), :].rearrange("o (j p) -> p (o j)", p=P)),
                       (b2r[s][:, :], b2[at(e), :].to_broadcast([P, D]))]
                if affine:
                    lot += [(gc[s][:, :], affine[0][at(e), :].rearrange("o (k p) -> p (o k)", p=P)),
                            (bc[s][:, :], affine[1][at(e), :].rearrange("o (k p) -> p (o k)", p=P))]
                for tile, dram in lot:
                    sp.dma_start(tile, dram, allow_slow_non_contiguous=True).then_inc(loaded[s], 16)

            if experts > slots:
                with sp.Fori(0, experts // slots) as ep:
                    for s in range(slots):
                        load(s, ep)
            else:
                for s in range(slots):
                    load(s, 0)

        @block.gpsimd
        def _(pool):
            def body(s, e, g, step):
                pool.wait_ge(pe_h, step * J + 2)
                for k in range(KD):
                    u = uT[:, k, at(g * GW, GW)]
                    nc.gpsimd.tensor_copy(xe[:, k, :], u).then_inc(pool_x, 1)
                if affine:
                    pool.wait_ge(pool_x, step * xs + KD)
                    nc.gpsimd.sem_inc(started, 1)
                    for k in range(KD):
                        nc.gpsimd.tensor_scalar(xe[:, k, :], xe[:, k, :], gc[s][:, k:k + 1], bc[s][:, k:k + 1], ALU.mult,
                                                ALU.add).then_inc(pool_x, 1)

            def before(s, ep):
                pool.wait_ge(loaded[s], ep * (16 * loads) + 16 * loads)
                nc.gpsimd.sem_inc(started, 1)
            each(pool, body, before)

        @block.tensor
        def _(pe):
            nc.tensor.sem_inc(pe_h, 2)

            def before(s, ep):
                pe.wait_ge(loaded[s], ep * (16 * loads) + 16 * loads)
                nc.tensor.sem_inc(started, 1)

            def body(s, e, g, step):
                pe.wait_ge(pool_x, step * xs + xs)
                for j in range(J):
                    pe.wait_ge(act_h, step * J + (j + 1))
                    for a in range(2):
                        for k in range(KD):
                            mm = nc.tensor.matmul(ps_h[j % 2][:, a, 0:half], w1[s][:, k, j * P:(j + 1) * P],
                                                  xe[:, k, a * half:(a + 1) * half], start=(k == 0), stop=(k == KD - 1))
                    mm.then_inc(pe_h, 1)
                pe.wait_ge(act_h, step * J + (J + 2))
                for v in range(GT):
                    pe.wait_ge(dve_part, step * GT + (v + 1 if v == 0 else v))
                    for j in range(J):
                        mm = nc.tensor.matmul(ps_y[v % 2][:, :], hid[:, j, v * P:(v + 1) * P], w2[s][:, j, :],
                                              start=(j == 0), stop=(j == J - 1))
                    mm.then_inc(pe_y, 1)

            each(pe, body, before)

        @block.scalar
        def _(act):
            nc.scalar.sem_inc(act_h, 2)

            def before(s, ep):
                act.wait_ge(loaded[s], ep * (16 * loads) + 16 * loads)
                nc.scalar.sem_inc(started, 1)

            def body(s, e, g, step):
                for j in range(J):
                    act.wait_ge(pe_h, step * J + (j + 3))
                    nc.scalar.activation(hid[:, j, :].rearrange("p (a n) -> p a n", a=2), ps_h[j % 2][:, :, 0:half], ACT.Gelu,
                                         bias=b1c[s][:, j:j + 1]).then_inc(act_h, 1)
            each(act, body, before)

        @block.vector
        def _(dve):
            nc.vector.sem_inc(dve_part, 1)
            nc.vector.sem_inc(dve_acc, 2)
            nc.vector.sem_inc(weights_used, slots)

            def before(s, ep):
                dve.wait_ge(loaded[s], ep * (16 * loads) + 16 * loads)
                nc.vector.sem_inc(started, 1)

            def body(s, e, g, step):
                for v in range(GT):
                    dve.wait_ge(pe_y, step * GT + (v + 1))
                    dve.wait_ge(dve_acc, step * GT + (v + 2))
                    nc.vector.tensor_tensor(part[:, v % 2, :], ps_y[v % 2][:, :], b2r[s][:, :], ALU.add).then_inc(dve_part, 1)
                    dve.wait_ge(dve_part, step * GT + (v + 2))
                    cur = flat(acc[:, at(g * GT + v), :])
                    nc.vector.scalar_tensor_tensor(out=cur, in0=part[:, v % 2, :], scalar=gate(g * GT + v, e, s), in1=cur,
                                                   op0=ALU.mult, op1=ALU.add).then_inc(dve_acc, 1)

            def after(s, ep):
                dve.wait_ge(dve_acc, (ep * slots + (s + 1)) * (GROUPS * GT) + 2)
                nc.vector.sem_inc(weights_used, 1)
            each(dve, body, before, after)


def program(nc, x, src, dst, ln1_w, ln1_b, ln2_w, ln2_b, wq, bq, wk, bk, wv, bv, wskip, bskip, w1, b1, w2, b2,
            fWr, fbr, fW1, fb1, fW2, fb2, gamma, beta, hW1, hb1, hW2, hb2, slope,
            mWr, mbr, ln_g, ln_b, mW1, mb1, mW2, mb2, out):
    tables = [nc.dram_tensor(f"table{n}", (NT * P, D), F32, kind="Internal").ap() for n in range(6)]
    with ExitStack() as ctx:
        keep = Scope(nc, ctx, "keep")
        c = constants(nc, keep)

        def edge_lists(name):
            return (keep.sb(f"{name}_local", [P, ETX]), keep.sb(f"{name}_other", [P, ETX], I32),
                    keep.sb(f"{name}_bucket", [1, LEAD + ETX + LEAD], I32))
        by_dst, by_src = edge_lists("dst"), edge_lists("src")
        sort_edges(nc, "sort_dst", dst, src, c, by_dst[0], by_dst[1], by_dst[2])
        sort_edges(nc, "sort_src", src, dst, c, by_src[0], by_src[1], by_src[2])

        X = keep.sb("X", [P, NT, D])
        U = keep.sb("U", [P, NT, D])
        load_nodes(nc, x, X)

        layer_norm(nc, "ln_x0", X, U)
        with ExitStack() as part:
            loc = Scope(nc, part, "att")
            Q3 = loc.sb("Q3", [P, NT, 3 * D], BF16)
            with ExitStack() as inner:
                kv = Scope(nc, inner, "kv")
                H, K, V = kv.sb("H", [P, NT, D]), kv.sb("K", [P, NT, D]), kv.sb("V", [P, NT, D])
                layer_norm(nc, "ln_1", U, H, ln1_w, ln1_b)

                q, rest = kv.sb("q", [P, 2, D]), kv.sb("rest", [P, 2, D])

                def handle(u, t, ps, biases, then, settle):
                    then(nc.vector.tensor_tensor(q[:, u, :], ps[:, 0:D], biases[:, 0:D], ALU.add))
                    for n, dest in enumerate((K, V)):
                        then(nc.vector.tensor_tensor(flat(dest[:, at(t), :]), ps[:, (n + 1) * D:(n + 2) * D],
                                                     biases[:, (n + 1) * D:(n + 2) * D], ALU.add))
                    cur = flat(U[:, at(t), :])
                    then(nc.vector.tensor_tensor(cur, cur, ps[:, 3 * D:4 * D], ALU.add))
                    part = [flat(Q3[:, at(t), n * D:(n + 1) * D]) for n in range(3)]
                    settle()
                    then(nc.vector.tensor_scalar(q[:, u, :], q[:, u, :], C ** -0.5, None, ALU.mult))
                    settle()
                    then(nc.vector.tensor_copy(part[0], q[:, u, :]))
                    settle()
                    then(nc.vector.tensor_tensor(rest[:, u, :], q[:, u, :], part[0], ALU.subtract))
                    settle()
                    then(nc.vector.tensor_copy(part[1], rest[:, u, :]))
                    settle()
                    then(nc.vector.tensor_tensor(part[2], rest[:, u, :], part[1], ALU.subtract))
                add_row(nc, "skip_bias", U, bskip)
                project(nc, "qkv", c, H, [(wq, 0), (wk, D), (wv, 2 * D), (wskip, 3 * D)], [(bq, 0), (bk, D), (bv, 2 * D)],
                        4 * D, 9, handle, [(tables[0], K), (tables[1], V)])
            scores = loc.sb("scores", [P, ETX, HEADS])
            most = loc.sb("most", [P, NT, HEADS])
            most2 = loc.sb("most2", [P, NT, 2 * HEADS], BF16)
            attention_scores(nc, c, tables[0], Q3, by_dst, scores, most)

            def split_most(r, then):
                then(nc.vector.tensor_copy(most2[:, :, 0:HEADS], most[:, :, :]))
                then(nc.vector.tensor_tensor(most2[:, :, HEADS:], most[:, :, :], most2[:, :, 0:HEADS], ALU.subtract))
            small_phase(nc, "split_most", None, split_most)
            total = loc.sb("total", [P, NT, AW])
            attend(nc, c, tables[1], by_dst, total, scores, most2)
            join_attention(nc, total, U, X)
        one_expert = (w1.rearrange("(o d) f -> o d f", o=1), b1.rearrange("(o f) -> o f", o=1),
                      w2.rearrange("(o f) d -> o f d", o=1), b2.rearrange("(o d) -> o d", o=1))
        with ExitStack() as part:
            loc = Scope(nc, part, "ff1")
            H, uT = loc.sb("H", [P, NT, D]), loc.sb("uT", [P, KD, NT * P])
            layer_norm(nc, "ln_2", U, H, ln2_w, ln2_b)
            turn_nodes(nc, "turn_1", c, H, uT)
            feed_forward(nc, "ffn_1", uT, X, 2 * D, 1, one_expert, lambda t, e, s: c["ones"][:, 0:1])

        with ExitStack() as part:
            loc = Scope(nc, part, "ff2")
            uT = loc.sb("uT", [P, KD, NT * P])
            chosen, gate = loc.sb("chosen", [1, 2], I32), loc.sb("gate", [P, 2])
            layer_norm(nc, "ln_x1", X, U)
            route_all(nc, c, U, fWr, fbr, chosen, gate)
            turn_nodes(nc, "turn_2", c, U, uT)
            feed_forward(nc, "ffn_2", uT, U, 2 * D, 2, (fW1, fb1, fW2, fb2), lambda t, e, s: gate[:, s:s + 1], chosen=chosen)
            layer_norm(nc, "ln_3", U, U, gamma, beta, add_to=X)

        with ExitStack() as part:
            loc = Scope(nc, part, "hyper")
            H, total = loc.sb("H", [P, NT, D]), loc.sb("total", [P, NT, AW])
            layer_norm(nc, "ln_x2", X, U)

            def handle(u, t, ps, biases, then, settle):
                then(nc.vector.tensor_copy(flat(H[:, at(t), :]), ps[:, :]))
            project(nc, "conv_1", c, U, [(hW1, 0)], [], D, 1, handle, [(tables[2], H)])
            edge_sums(nc, "to_dst_1", c, tables[2], by_dst, total)
            divide_by_count(nc, "mean_1", total, table=tables[3])
            edge_sums(nc, "to_src_1", c, tables[3], by_src, total)
            divide_by_count(nc, "act_1", total, bias=hb1, slope=slope, dest=H)
            project(nc, "conv_2", c, H, [(hW2, 0)], [], D, 1, handle, [(tables[4], H)])
            edge_sums(nc, "to_dst_2", c, tables[4], by_dst, total)
            divide_by_count(nc, "mean_2", total, table=tables[5])
            edge_sums(nc, "to_src_2", c, tables[5], by_src, total)
            divide_by_count(nc, "act_2", total, bias=hb2, slope=slope, residual=U, add_to=X)

        with ExitStack() as part:
            loc = Scope(nc, part, "moe")
            uT = loc.sb("uT", [P, KD, NT * P])
            gate = loc.sb("gate", [P, NT, EXPERTS])
            logits = loc.sb("logits", [P, NT, EXPERTS])
            layer_norm(nc, "ln_x3", X, U)

            def handle(u, t, ps, biases, then, settle):
                then(nc.vector.tensor_copy(flat(logits[:, at(t), :]), ps[:, :]))
            project(nc, "logits", c, U, [(mWr, 0)], [], EXPERTS, 1, handle, [])
            route_each(nc, c, logits, mbr, gate)
            layer_norm(nc, "ln_4", U, U)
            turn_nodes(nc, "turn_3", c, U, uT)
            gates = gate[:, :, :].rearrange("p t e -> p (t e)")
            feed_forward(nc, "ffn_3", uT, X, 4 * D, EXPERTS, (mW1, mb1, mW2, mb2),
                         lambda t, e, s: gates[:, at(t * EXPERTS + e)], affine=(ln_g, ln_b))
        store_nodes(nc, X, out)


_INS = ["x", "src", "dst", "L0_gnn_ln1_w", "L0_gnn_ln1_b", "L0_gnn_ln2_w", "L0_gnn_ln2_b", "L0_gnn_wq", "L0_gnn_bq",
        "L0_gnn_wk", "L0_gnn_bk", "L0_gnn_wv", "L0_gnn_bv", "L0_gnn_wskip", "L0_gnn_bskip", "L0_gnn_w1", "L0_gnn_b1",
        "L0_gnn_w2", "L0_gnn_b2", "L0_ffn_Wr", "L0_ffn_br", "L0_ffn_W1", "L0_ffn_b1", "L0_ffn_W2", "L0_ffn_b2",
        "L0_ffn_gamma", "L0_ffn_beta", "L1_gnn_W1", "L1_gnn_b1", "L1_gnn_W2", "L1_gnn_b2", "L1_gnn_a", "L1_ffn_Wr",
        "L1_ffn_br", "L1_ffn_ln_g", "L1_ffn_ln_b", "L1_ffn_W1", "L1_ffn_b1", "L1_ffn_W2", "L1_ffn_b2"]


def kernel(**inputs):
    import numpy as _np
    import concourse.bacc as _bacc
    from concourse import mybir as _mybir
    from concourse.bass_utils import run_bass_kernel_spmd as _run

    nc = _bacc.Bacc("TRN2", target_bir_lowering=False, num_devices=1)
    arrays, args = {}, []
    for name in _INS:
        a = _np.ascontiguousarray(inputs[name])
        arrays[f"in_{name}_dram"] = a
        args.append(nc.dram_tensor(f"in_{name}_dram", a.shape, _mybir.dt.from_np(a.dtype), kind="ExternalInput").ap())
    args.append(nc.dram_tensor("out_0_dram", (N, D), F32, kind="ExternalOutput").ap())
    program(nc, *args)
    r = _run(nc, [arrays], core_ids=[0])
    return r.results[0]["out_0_dram"]
```

```python
from contextlib import ExitStack
import math
import concourse.bass as bass
from concourse import mybir

F32 = mybir.dt.float32
F16 = mybir.dt.float16
BF16 = mybir.dt.bfloat16
I32 = mybir.dt.int32
ALU = mybir.AluOpType
ACT = mybir.ActivationFunctionType
AX = mybir.AxisListType.X
P = 128
N = 3125
D = 256
KD = D // P
E = 53125
HEADS = 4
C = D // HEADS
NT = (N + P - 1) // P
TAIL = N - (NT - 1) * P
EC = (E + P - 1) // P
RING = 8
ET = ((E + NT * (P - 1)) // P + RING) // RING * RING
EXPERTS = 8
EPS = 1e-5
FAR = 1e30
GT = 5
GROUPS = NT // GT
GW = GT * P
BT = 256
BATCHES = (2 * N + EXPERTS * (BT - 1)) // BT
WSLOTS = 4
ETX = ET + RING
BANK = 512
TCOLS = (ETX + P - 1) // P
COLS = 4
AW = D + HEADS


def at(i, n=1):
    return bass.ds(i, n)


def flat(ap):
    return ap.rearrange("p o d -> p (o d)")


class Scope:
    def __init__(self, nc, ctx, tag):
        self.nc, self.ctx, self.tag = nc, ctx, tag
        self.sems = []
        ctx.callback(self.end)

    def end(self):
        if self.sems:
            self.nc.clear_and_free_semaphores(self.sems)
            self.nc.all_engine_barrier()

    def sb(self, name, shape, dt=F32):
        return self.ctx.enter_context(self.nc.sbuf_tensor(f"{name}_{self.tag}", shape, dt))

    def ps(self, name, shape, dt=F32):
        return self.ctx.enter_context(self.nc.psum_tensor(f"{name}_{self.tag}", shape, dt))

    def sem(self, name):
        self.sems.append(self.nc.alloc_semaphore(f"{name}_{self.tag}"))
        return self.sems[-1]


def chained(dve, sem):
    step = [0]

    def then(ins, settle=True):
        step[0] += 1
        ins.then_inc(sem, 1)
        if settle:
            dve.wait_ge(sem, step[0])
    return then


def row(dram, n=D):
    return dram.rearrange("(o d) -> o d", o=1).to_broadcast([P, n])


def constants(nc, sc):
    c = {"iota_t": sc.sb("iota_t", [P, ET], F16), "iota_l": sc.sb("iota_l", [P, P], F16),
         "iota_lf": sc.sb("iota_lf", [P, P]), "iota_b": sc.sb("iota_b", [P, NT]), "iota_tf": sc.sb("iota_tf", [1, ETX]),
         "iota_e": sc.sb("iota_e", [P, EXPERTS]), "spare": sc.sb("spare", [P, 2]), "tile_no": sc.sb("tile_no", [P, TCOLS]),
         "below": sc.sb("below", [P, P]), "ones": sc.sb("ones", [P, P]),
         "real": sc.sb("real", [P, P]), "ident": sc.sb("ident", [P, P]), "ident_b": sc.sb("ident_b", [P, P], BF16),
         "ones_b": sc.sb("ones_b", [P, P], BF16)}
    with ExitStack() as inner:
        filled = Scope(nc, inner, "const").sem("filled")
        block = inner.enter_context(nc.Block())

        @block.gpsimd
        def _(pool):
            for name, n in (("iota_t", ET), ("iota_l", P), ("iota_lf", P), ("iota_b", NT), ("iota_tf", ETX)):
                nc.gpsimd.iota(c[name][:, :], [[1, n]], base=0, channel_multiplier=0, allow_small_or_imprecise_dtypes=True)
            nc.gpsimd.iota(c["iota_e"][:, :], [[1, EXPERTS]], base=-EXPERTS, channel_multiplier=0,
                           allow_small_or_imprecise_dtypes=True)
            nc.gpsimd.iota(c["spare"][:, :], [[P, 2]], base=BATCHES * BT + 1, channel_multiplier=1,
                           allow_small_or_imprecise_dtypes=True)
            nc.gpsimd.iota(c["tile_no"][:, :], [[P, TCOLS]], base=0, channel_multiplier=1,
                           allow_small_or_imprecise_dtypes=True)
            nc.gpsimd.memset(c["ones_b"][:, :], 1.0).then_inc(filled, 1)
            nc.gpsimd.memset(c["ones"][:, :], 1.0).then_inc(filled, 1)
            pool.wait_ge(filled, 2)
            nc.gpsimd.affine_select(out=c["below"][:, :], in_=c["ones"][:, :], compare_op=ALU.is_gt, fill=0.0, base=0,
                                    pattern=[[1, P]], channel_multiplier=-1)
            nc.gpsimd.affine_select(out=c["real"][:, :], in_=c["ones"][:, :], compare_op=ALU.is_gt, fill=0.0, base=TAIL,
                                    pattern=[[0, P]], channel_multiplier=-1)
            for name, ones in (("ident", "ones"), ("ident_b", "ones_b")):
                nc.gpsimd.affine_select(out=c[name][:, :], in_=c[ones][:, :], compare_op=ALU.is_equal, fill=0.0, base=0,
                                        pattern=[[1, P]], channel_multiplier=-1)
    return c


def load_nodes(nc, x, X):
    with ExitStack() as ctx:
        sc = Scope(nc, ctx, "load")
        cleared, loaded = sc.sem("cleared"), sc.sem("loaded")
        block = ctx.enter_context(nc.Block())

        @block.vector
        def _(dve):
            nc.vector.memset(X[:, NT - 1, :], 0.0).then_inc(cleared, 1)

        @block.sync
        def _(sp):
            sp.dma_start(X[:, 0:NT - 1, :], x[0:(NT - 1) * P, :].rearrange("(b p) d -> p b d", p=P)).then_inc(loaded, 16)
            sp.wait_ge(cleared, 1)
            sp.dma_start(X[0:TAIL, NT - 1, :], x[(NT - 1) * P:N, :]).then_inc(loaded, 16)
            sp.wait_ge(loaded, 32)


def places(sc):
    p = {name: sc.sb(name, [P, EC]) for name in ("tile_f", "lane_f")}
    p["pay"] = sc.sb("pay", [P, 2, EC])
    p["less_pay"] = sc.sb("less_pay", [P, 2, EC])
    p["less_lane"] = sc.sb("less_lane", [P, EC + COLS])
    return p


def rank_edges(nc, tag, key, other, consts, place, edges, cleared=None):
    local_of, other_of, bucket_of = edges
    tile_f, lane_f, pay, less_pay, less_lane = (place[n] for n in ("tile_f", "lane_f", "pay", "less_pay", "less_lane"))
    with ExitStack() as ctx:
        sc = Scope(nc, ctx, tag)
        key_i = sc.sb("key_i", [P, EC], I32)
        oth_i = sc.sb("oth_i", [P, EC], I32)
        tmp_i = sc.sb("tmp_i", [P, EC], I32)
        bucket_f = sc.sb("bucket_f", [P, EC])
        member = sc.sb("member", [P, NT, EC])
        running = sc.sb("running", [P, NT, EC])
        zero = sc.sb("zero", [P, 1])
        count = sc.sb("count", [P, NT])
        upto = sc.sb("upto", [P, NT])
        ti = sc.sb("ti", [P, NT], I32)
        tf = sc.sb("tf", [P, NT])
        first = sc.sb("first", [P, NT])
        offset = sc.sb("offset", [P, NT])
        pos_f = sc.sb("pos_f", [P, EC])
        begun = sc.sb("begun", [P, TCOLS, NT])
        begun_sum = sc.sb("begun_sum", [P, TCOLS])
        zeros = sc.sb("zeros", [P, 8 * D]) if cleared is not None else None
        ps_before = sc.ps("before", [P, BANK])
        ps_total = sc.ps("total", [P, BANK])
        ps_bucket = sc.ps("bucket", [1, TCOLS * P])
        loaded, padded, chain = sc.sem("loaded"), sc.sem("padded"), sc.sem("chain")
        counted, summed = sc.sem("counted"), sc.sem("summed")
        ranked, turned_row = sc.sem("ranked"), sc.sem("turned_row")
        zeros_made, zeroed = sc.sem("zeros_made"), sc.sem("zeroed")
        full = E // EC
        block = ctx.enter_context(nc.Block())

        @block.sync
        def _(sp):
            sp.wait_ge(padded, 2)
            for dram, tile in ((key, key_i), (other, oth_i)):
                sp.dma_start(tile[0:full, :], dram[0:full * EC].rearrange("(p j) -> p j", j=EC)).then_inc(loaded, 16)
                sp.dma_start(tile[full:full + 1, 0:E - full * EC],
                             dram[full * EC:E].rearrange("(p j) -> p j", p=1)).then_inc(loaded, 16)
            if cleared is not None:
                sp.wait_ge(zeros_made, 1)
                pieces = BATCHES * BT // (8 * P)
                table = cleared[0:BATCHES * BT, :].rearrange("(n p r) d -> n p (r d)", p=P, r=8)
                for n in range(pieces):
                    sp.dma_start(table[n, :, :], zeros[:, :]).then_inc(zeroed, 16)
                sp.wait_ge(zeroed, 16 * pieces)

        @block.gpsimd
        def _(pool):
            if cleared is not None:
                nc.gpsimd.memset(zeros[:, :], 0.0).then_inc(zeros_made, 1)

        @block.vector
        def _(dve):
            then = chained(dve, chain)
            nc.vector.memset(key_i[:, :], NT * P).then_inc(padded, 1)
            nc.vector.memset(oth_i[:, :], 0).then_inc(padded, 1)
            nc.vector.memset(zero[:, :], 0.0)
            nc.vector.memset(other_of[:, ET:ETX], 0)
            nc.vector.memset(local_of[:, ET:ETX], -1.0)
            nc.vector.memset(bucket_of[:, :], 0)
            then(nc.vector.memset(less_lane[:, :], 0.0))
            dve.wait_ge(loaded, 64)
            then(nc.vector.tensor_scalar(tmp_i[:, :], key_i[:, :], 7, None, ALU.arith_shift_right))
            then(nc.vector.tensor_copy(bucket_f[:, :], tmp_i[:, :]))
            then(nc.vector.tensor_scalar(tmp_i[:, :], key_i[:, :], P - 1, None, ALU.bitwise_and))
            then(nc.vector.tensor_scalar(pay[:, 0, :], tmp_i[:, :], 8.0, 8.0, ALU.mult, ALU.add))
            then(nc.vector.tensor_scalar(tmp_i[:, :], oth_i[:, :], 9, None, ALU.arith_shift_right))
            then(nc.vector.tensor_tensor(pay[:, 0, :], pay[:, 0, :], tmp_i[:, :], ALU.add))
            then(nc.vector.tensor_scalar(tmp_i[:, :], oth_i[:, :], 511, None, ALU.bitwise_and))
            then(nc.vector.tensor_copy(pay[:, 1, :], tmp_i[:, :]))
            then(nc.vector.tensor_scalar(less_pay[:, :, :], pay[:, :, :], -1.0, None, ALU.mult))
            then(nc.vector.tensor_tensor(member[:, :, :], bucket_f[:, None, :].to_broadcast([P, NT, EC]),
                                         consts["iota_b"][:, :, None].to_broadcast([P, NT, EC]), ALU.is_equal))
            then(nc.vector.tensor_tensor_scan(running[:, :, :].rearrange("p b j -> p (b j)"),
                                              member[:, :, :].rearrange("p b j -> p (b j)"),
                                              zero[:, 0:1].to_broadcast([P, NT * EC]), 0.0, ALU.add, ALU.add))
            then(nc.vector.tensor_copy(upto[:, :], running[:, :, EC - 1]))
            then(nc.vector.tensor_copy(count[:, 0:1], upto[:, 0:1]))
            nc.vector.tensor_tensor(count[:, 1:NT], upto[:, 1:NT], upto[:, 0:NT - 1], ALU.subtract).then_inc(counted, 1)
            dve.wait_ge(summed, 1)
            then(nc.vector.tensor_scalar(ti[:, :], ps_total[:, 0:NT], float(P - 1), None, ALU.add))
            then(nc.vector.tensor_scalar(ti[:, :], ti[:, :], 7, None, ALU.arith_shift_right))
            then(nc.vector.tensor_copy(tf[:, :], ti[:, :]))
            then(nc.vector.tensor_tensor_scan(first[:, :], tf[:, :], zero[:, 0:1].to_broadcast([P, NT]), 0.0,
                                              ALU.add, ALU.add))
            then(nc.vector.tensor_tensor(first[:, :], first[:, :], tf[:, :], ALU.subtract))
            then(nc.vector.scalar_tensor_tensor(out=offset[:, :], in0=first[:, :], scalar=float(P), in1=ps_before[:, 0:NT],
                                                op0=ALU.mult, op1=ALU.add))
            then(nc.vector.tensor_tensor(offset[:, 1:NT], offset[:, 1:NT], upto[:, 0:NT - 1], ALU.subtract))
            for b in range(NT):
                then(nc.vector.scalar_tensor_tensor(out=running[:, b, :], in0=running[:, b, :], scalar=offset[:, b:b + 1],
                                                    in1=member[:, b, :], op0=ALU.add, op1=ALU.mult), settle=b == NT - 1)
            then(nc.vector.tensor_reduce(pos_f[:, :], running[:, :, :].rearrange("p b j -> p j b"), AX, ALU.add))
            then(nc.vector.tensor_scalar(key_i[:, :], pos_f[:, :], -1.0, None, ALU.add))
            then(nc.vector.tensor_scalar(tmp_i[:, :], key_i[:, :], 7, None, ALU.arith_shift_right))
            then(nc.vector.tensor_copy(tile_f[:, :], tmp_i[:, :]))
            then(nc.vector.tensor_scalar(tmp_i[:, :], key_i[:, :], P - 1, None, ALU.bitwise_and))
            then(nc.vector.tensor_copy(lane_f[:, :], tmp_i[:, :]))
            then(nc.vector.tensor_scalar(less_lane[:, 0:EC], lane_f[:, :], -1.0, None, ALU.mult))
            then(nc.vector.tensor_tensor(begun[:, :, :], consts["tile_no"][:, :, None].to_broadcast([P, TCOLS, NT]),
                                         first[:, None, :].to_broadcast([P, TCOLS, NT]), ALU.is_ge))
            nc.vector.tensor_reduce(begun_sum[:, :], begun[:, :, :], AX, ALU.add).then_inc(ranked, 1)
            dve.wait_ge(turned_row, 1)
            then(nc.vector.tensor_scalar(bucket_of[:, LEAD:LEAD + ETX], ps_bucket[:, 0:ETX], -1.0, None, ALU.add))

        @block.tensor
        def _(pe):
            pe.wait_ge(counted, 1)
            nc.tensor.matmul(ps_before[:, 0:NT], consts["below"][:, :], count[:, :], start=True, stop=True)
            nc.tensor.matmul(ps_total[:, 0:NT], consts["ones"][:, :], count[:, :], start=True,
                             stop=True).then_inc(summed, 1)
            pe.wait_ge(ranked, 1)
            for n in range(TCOLS):
                mm = nc.tensor.matmul(ps_bucket[:, n * P:(n + 1) * P], begun_sum[:, n:n + 1], consts["ident"][:, :],
                                      start=True, stop=True)
            mm.then_inc(turned_row, 1)


def placement(nc, sc, consts, place, edges, per):
    assert EC % per == 0 and per % 8 == 0
    in_tile = sc.sb("in_tile", [P, COLS, ET], F16)
    in_lane = sc.sb("in_lane", [P, COLS, 2, P], F16)
    distance = sc.sb("distance", [P, 4, P], F16)
    zl, zr = sc.sb("zl", [P, P], F16), sc.sb("zr", [P, ET], F16)
    upper_i, part_i = sc.sb("upper_i", [P, ET], I32), sc.sb("part_i", [P, ET], I32)
    ps = [sc.ps(f"sorted{k}", [P, BANK]) for k in range(2)]
    cleared = sc.sem("sorted_cleared")
    merge_chain = sc.sem("merge_chain")
    dve_tile, dve_lanes, act_distance, act_lanes, onehots_used = (sc.sem(n) for n in (
        "dve_tile", "dve_lanes", "act_distance", "act_lanes", "onehots_used"))

    def vector_start():
        nc.vector.sem_inc(onehots_used, COLS)
        nc.vector.memset(zl[:, :], 0.0)
        nc.vector.memset(zr[:, :], 0.0).then_inc(cleared, 1)

    def vector_column(dve, i, n):
        u = n % COLS
        j = i * per + n
        dve.wait_ge(onehots_used, i * per + (n + 1))
        nc.vector.tensor_scalar(in_tile[:, u, :], consts["iota_t"][:, :], place["tile_f"][:, at(j)], None,
                                ALU.is_equal).then_inc(dve_tile, 1)
        if n % 2 == 0:
            for k in range(2):
                nc.vector.tensor_scalar(in_lane[:, u, k, :], consts["iota_l"][:, :], place["lane_f"][:, at(j)],
                                        place["pay"][:, k, at(j)], ALU.is_equal, ALU.mult).then_inc(dve_lanes, 1)

    def vector_end(dve):
        local_of, other_of, _ = edges
        then = chained(dve, merge_chain)
        dve.wait_ge(onehots_used, EC + COLS)
        then(nc.vector.tensor_copy(upper_i[:, :], ps[0][:, 0:ET]))
        then(nc.vector.tensor_scalar(part_i[:, :], upper_i[:, :], 3, None, ALU.arith_shift_right))
        then(nc.vector.tensor_scalar(local_of[:, 0:ET], part_i[:, :], -1.0, None, ALU.add))
        then(nc.vector.tensor_scalar(part_i[:, :], upper_i[:, :], 7, None, ALU.bitwise_and))
        then(nc.vector.scalar_tensor_tensor(out=other_of[:, 0:ET], in0=part_i[:, :], scalar=512.0, in1=ps[1][:, 0:ET],
                                            op0=ALU.mult, op1=ALU.add))

    def measure(j, n):
        nc.scalar.activation(distance[:, n // 2 % 4, :], consts["iota_l"][:, :], ACT.Abs,
                                  bias=place["less_lane"][:, at(j)]).then_inc(act_distance, 1)

    def scalar_start():
        nc.scalar.sem_inc(act_lanes, 8)
        measure(1, 1)

    def scalar_column(act, i, n):
        j = i * per + n
        act.wait_ge(act_lanes, i * per + (n + 3))
        measure(i * per + (n + 2), n + 2)
        act.wait_ge(act_distance, i * (per // 2) + (n // 2 + 1))
        act.wait_ge(onehots_used, i * per + (n + 1))
        for k in range(2):
            nc.scalar.activation(in_lane[:, n % COLS, k, :], distance[:, n // 2 % 4, :], ACT.Relu,
                                 scale=place["less_pay"][:, k, at(j)], bias=place["pay"][:, k, at(j)]).then_inc(act_lanes, 1)

    def tensor_start(pe):
        pe.wait_ge(cleared, 1)
        for k in range(2):
            nc.tensor.matmul(ps[k][:, 0:ET], zl[:, :], zr[:, :], start=True, stop=False,
                                  skip_group_check=True)

    def tensor_column(pe, i, n):
        u = n % COLS
        pe.wait_ge(dve_tile, i * per + (n + 1))
        if n % 2 == 0:
            pe.wait_ge(dve_lanes, i * per + (n + 2))
        else:
            pe.wait_ge(act_lanes, i * per + (n + 9))
        for k in range(2):
            mm = nc.tensor.matmul(ps[k][:, 0:ET], in_lane[:, u, k, :], in_tile[:, u, :],
                                       start=False, stop=False, skip_group_check=True)
        mm.then_inc(onehots_used, 1)

    return {"vector_start": vector_start, "vector_column": vector_column, "vector_end": vector_end,
            "scalar_start": scalar_start, "scalar_column": scalar_column,
            "tensor_start": tensor_start, "tensor_column": tensor_column}


def place_edges(nc, tag, consts, place, edges):
    with ExitStack() as ctx:
        sc = Scope(nc, ctx, tag)
        per = 8
        sort = placement(nc, sc, consts, place, edges, per)
        block = ctx.enter_context(nc.Block())

        @block.vector
        def _(dve):
            sort["vector_start"]()
            with dve.Fori(0, EC // per) as i:
                for n in range(per):
                    sort["vector_column"](dve, i, n)
            sort["vector_end"](dve)

        @block.scalar
        def _(act):
            sort["scalar_start"]()
            with act.Fori(0, EC // per) as i:
                for n in range(1, per, 2):
                    sort["scalar_column"](act, i, n)

        @block.tensor
        def _(pe):
            sort["tensor_start"](pe)
            with pe.Fori(0, EC // per) as i:
                for n in range(per):
                    sort["tensor_column"](pe, i, n)


def layer_norm(nc, tag, src, dst, gamma=None, beta=None, add_to=None):
    with ExitStack() as ctx:
        sc = Scope(nc, ctx, tag)
        stats = sc.sb("stats", [P, NT, 6])
        moments = sc.sb("moments", [P, NT, 2])
        rstd = sc.sb("rstd", [P, NT])
        eps = sc.sb("eps", [P, 1])
        g_row = sc.sb("g_row", [P, D])
        b_row = sc.sb("b_row", [P, D])
        loaded, chain, deviated = sc.sem("loaded"), sc.sem("chain"), sc.sem("deviated")
        stats_done, aggregated, scaled = sc.sem("stats_done"), sc.sem("aggregated"), sc.sem("scaled")
        block = ctx.enter_context(nc.Block())

        @block.sync
        def _(sp):
            if gamma is not None:
                sp.dma_start(g_row[:, :], row(gamma)).then_inc(loaded, 16)
                sp.dma_start(b_row[:, :], row(beta)).then_inc(loaded, 16)

        @block.scalar
        def _(act):
            act.wait_ge(aggregated, NT + 1)
            nc.scalar.activation(rstd[:, :], moments[:, :, 1], ACT.Sqrt, bias=eps[:, 0:1]).then_inc(deviated, 1)

        @block.vector
        def _(dve):
            nc.vector.memset(eps[:, :], EPS).then_inc(aggregated, 1)
            with dve.Fori(0, GROUPS) as g:
                for v in range(GT):
                    t = g * GT + v
                    nc.vector.bn_stats(flat(stats[:, at(t), :]), flat(src[:, at(t), :])).then_inc(stats_done, 1)
            dve.wait_ge(stats_done, NT)
            for t in range(NT):
                nc.vector.bn_aggr(moments[:, t, :], stats[:, t, :]).then_inc(aggregated, 1)
            then = chained(dve, chain)
            dve.wait_ge(deviated, 1)
            then(nc.vector.reciprocal(rstd[:, :], rstd[:, :]))
            with dve.Fori(0, GROUPS) as g:
                for v in range(GT):
                    t = g * GT + v
                    nc.vector.tensor_scalar(flat(dst[:, at(t), :]), flat(src[:, at(t), :]),
                                            flat(moments[:, at(t), 0:1]), rstd[:, at(t)],
                                            ALU.subtract, ALU.mult).then_inc(scaled, 1)
            dve.wait_ge(scaled, NT)
            if gamma is not None:
                dve.wait_ge(loaded, 32)
                then(nc.vector.tensor_tensor(dst[:, :, :], dst[:, :, :], g_row[:, None, :].to_broadcast([P, NT, D]), ALU.mult))
                then(nc.vector.tensor_tensor(dst[:, :, :], dst[:, :, :], b_row[:, None, :].to_broadcast([P, NT, D]), ALU.add))
            if add_to is not None:
                then(nc.vector.tensor_tensor(add_to[:, :, :], add_to[:, :, :], dst[:, :, :], ALU.add))


def in_pairs(eng, body):
    with eng.Fori(0, NT // 2) as i:
        body(i * 2, 2)
    if NT % 2:
        body(NT - 1, 1)


def pairs_ahead(eng, lead, first, second):
    pairs = NT // 2
    for n in range(lead):
        for u in range(2):
            first(n * 2, u)
    with eng.Fori(0, pairs - lead) as i:
        for u in range(2):
            first(i * 2 + 2 * lead, u)
        for u in range(2):
            second(i * 2, u)
    for n in range(pairs - lead, pairs):
        if n == pairs - lead and NT % 2:
            first(NT - 1, 0)
        for u in range(2):
            second(n * 2, u)
    if NT % 2:
        second(NT - 1, 0)


def small_phase(nc, tag, row_dram, work):
    with ExitStack() as ctx:
        sc = Scope(nc, ctx, tag)
        r = sc.sb("r", [P, D])
        loaded, chain = sc.sem("loaded"), sc.sem("chain")
        block = ctx.enter_context(nc.Block())

        @block.sync
        def _(sp):
            if row_dram is not None:
                sp.dma_start(r[:, :], row(row_dram)).then_inc(loaded, 16)

        @block.vector
        def _(dve):
            if row_dram is not None:
                dve.wait_ge(loaded, 16)
            work(r, chained(dve, chain))


def project(nc, tag, consts, source, weights, bias_rows, width, steps, handle, stores):
    with ExitStack() as ctx:
        sc = Scope(nc, ctx, tag)
        placed = sc.sb("placed", [P, 2, D])
        turned = sc.sb("turned", [P, 2, D])
        W = sc.sb("W", [P, KD, width])
        biases = sc.sb("biases", [P, width])
        ps_turn = [sc.ps(f"turn{u}", [P, D]) for u in range(2)]
        out = [sc.ps(f"out{u}", [P, max(width, 512) if width > 256 else width]) for u in range(2)]
        loaded, stored = sc.sem("loaded"), sc.sem("stored")
        dve_placed, pe_turned, act_turned = sc.sem("dve_placed"), sc.sem("pe_turned"), sc.sem("act_turned")
        pe_projected, dve_handled = sc.sem("pe_projected"), sc.sem("dve_handled")
        block = ctx.enter_context(nc.Block())

        @block.sync
        def _(sp):
            for dram, c0 in weights:
                sp.dma_start(W[:, :, c0:c0 + dram.shape[1]], dram.rearrange("(k p) n -> p k n", p=P)).then_inc(loaded, 16)
            for dram, c0 in bias_rows:
                sp.dma_start(biases[:, c0:c0 + dram.shape[0]], row(dram, dram.shape[0])).then_inc(loaded, 16)
            if stores:
                with sp.Fori(0, GROUPS) as g:
                    sp.wait_ge(dve_handled, g * (GT * steps) + (GT + 2) * steps)
                    for table, buf in stores:
                        sp.dma_start(table[at(g * GW, GW), :].rearrange("(b p) d -> p b d", p=P),
                                     buf[:, at(g * GT, GT), :]).then_inc(stored, 16)
                sp.wait_ge(stored, 16 * len(stores) * GROUPS)

        @block.tensor
        def _(pe):
            nc.tensor.sem_inc(pe_turned, 4)
            nc.tensor.sem_inc(pe_projected, 2)
            pe.wait_ge(loaded, 16 * (len(weights) + len(bias_rows)))

            def turn(t0, u):
                pe.wait_ge(dve_placed, t0 + (u + 1))
                pe.wait_ge(act_turned, t0 + (u + 1))
                for k in range(KD):
                    nc.tensor.transpose(ps_turn[u][:, k * P:(k + 1) * P], placed[:, u, k * P:(k + 1) * P],
                                        consts["ident"][:, :]).then_inc(pe_turned, 1)

            def multiply(t0, u):
                pe.wait_ge(act_turned, t0 + (u + 3))
                pe.wait_ge(dve_handled, t0 * steps + (u + 1) * steps)
                for c0 in range(0, width, 512):
                    w = min(512, width - c0)
                    for k in range(KD):
                        mm = nc.tensor.matmul(out[u][:, c0:c0 + w], turned[:, u, k * P:(k + 1) * P],
                                              W[:, k, c0:c0 + w], start=(k == 0), stop=(k == KD - 1))
                mm.then_inc(pe_projected, 1)
            pairs_ahead(pe, 1, turn, multiply)

        @block.scalar
        def _(act):
            nc.scalar.sem_inc(act_turned, 2)

            def body(t0, n):
                for u in range(n):
                    act.wait_ge(pe_turned, t0 * 2 + (u + 3) * 2)
                    act.wait_ge(pe_projected, t0 + (u + 1))
                    nc.scalar.activation(turned[:, u, :], ps_turn[u][:, :], ACT.Copy).then_inc(act_turned, 1)
            in_pairs(act, body)

        @block.vector
        def _(dve):
            nc.vector.sem_inc(dve_handled, 2 * steps)

            def place(t0, u):
                dve.wait_ge(pe_turned, t0 * 2 + (u + 1) * 2)
                nc.vector.tensor_copy(placed[:, u, :], flat(source[:, at(t0 + u), :])).then_inc(dve_placed, 1)

            def handle_tile(t0, u):
                dve.wait_ge(pe_projected, t0 + (u + 3))
                made = [0]

                def then(ins):
                    made[0] += 1
                    ins.then_inc(dve_handled, 1)

                def settle():
                    dve.wait_ge(dve_handled, t0 * steps + ((u + 2) * steps + made[0]))
                handle(u, t0 + u, out[u], biases, then, settle)
            pairs_ahead(dve, 2, place, handle_tile)


def turn_nodes(nc, tag, consts, source, dest):
    with ExitStack() as ctx:
        sc = Scope(nc, ctx, tag)
        placed = sc.sb("placed", [P, 2, D])
        ps_turn = [sc.ps(f"turn{u}", [P, D]) for u in range(2)]
        dve_placed, pe_turned, act_turned = sc.sem("dve_placed"), sc.sem("pe_turned"), sc.sem("act_turned")
        block = ctx.enter_context(nc.Block())

        @block.vector
        def _(dve):
            def body(t0, n):
                for u in range(n):
                    dve.wait_ge(pe_turned, t0 * 2 + (u + 1) * 2)
                    nc.vector.tensor_copy(placed[:, u, :], flat(source[:, at(t0 + u), :])).then_inc(dve_placed, 1)
            in_pairs(dve, body)

        @block.tensor
        def _(pe):
            nc.tensor.sem_inc(pe_turned, 4)

            def body(t0, n):
                for u in range(n):
                    pe.wait_ge(dve_placed, t0 + (u + 1))
                    pe.wait_ge(act_turned, t0 + (u + 1))
                    for k in range(KD):
                        nc.tensor.transpose(ps_turn[u][:, k * P:(k + 1) * P], placed[:, u, k * P:(k + 1) * P],
                                            consts["ident"][:, :]).then_inc(pe_turned, 1)
            in_pairs(pe, body)

        @block.scalar
        def _(act):
            nc.scalar.sem_inc(act_turned, 2)

            def body(t0, n):
                for u in range(n):
                    act.wait_ge(pe_turned, t0 * 2 + (u + 3) * 2)
                    nc.scalar.activation(dest[:, :, at((t0 + u) * P, P)], ps_turn[u][:, :].rearrange("p (k n) -> p k n", k=KD),
                                         ACT.Copy).then_inc(act_turned, 1)
            in_pairs(act, body)


STEP = 2
STEPS = RING // STEP
AHEAD = 4
EARLY = 3
SLOTS = 4


LEAD = 6
BATCH = 14


def bucket_registers(eng, name):
    return [eng.alloc_register(f"{name}{n}") for n in range(BATCH)]


def load_buckets(eng, regs, bucket_of, start):
    eng.load(regs, bucket_of[0:1, at(start, BATCH)])
    return [eng.snap(r, min_val=0, max_val=NT - 1) for r in regs]


def done(eng, sem, i, s, lag=0):
    eng.wait_ge(sem, i * STEPS + (s + 1 + AHEAD - lag))


def gather_rows(nc, pool, table, rows, index, indexed, begun, gathered):
    with pool.Fori(0, ET // RING) as i:
        for r in range(RING):
            if r % STEP == 0:
                pool.wait_ge(indexed, i * STEPS + (r // STEP + 1))
                nc.gpsimd.sem_inc(begun, 1)
            pool.indirect_dma_start(rows[:, r, 0:D], None, table,
                                    bass.IndirectOffsetOnAxis(ap=index[:, r:r + 1], axis=0)).then_inc(gathered[r], 16)


def copy_index(nc, index, other_of, t, s, indexed):
    nc.scalar.activation(index[:, s * STEP:(s + 1) * STEP], other_of[:, at(t, STEP)], ACT.Copy).then_inc(indexed, 1)


def make_onehot(nc, consts, onehot, local_of, t, n, made):
    shape = [P, n, P]
    nc.vector.tensor_tensor(onehot, consts["iota_lf"][:, None, :].to_broadcast(shape),
                            local_of[:, at(t, n), None].to_broadcast(shape), ALU.is_equal).then_inc(made, 1)


def attention_scores(nc, consts, k_table, Q3, edges, scores, most):
    local_of, other_of, bucket_of = edges
    with ExitStack() as ctx:
        sc = Scope(nc, ctx, "score")
        rows = sc.sb("rows", [P, RING, D])
        index = sc.sb("index", [P, RING], I32)
        onehot = sc.sb("onehot", [P, 2, STEP, P])
        distance = sc.sb("distance", [P, STEP, P])
        turned = sc.sb("turned", [P, SLOTS, STEP, P], BF16)
        away = sc.sb("away", [P, SLOTS, STEP, P], BF16)
        product = sc.sb("product", [P, STEP, D])
        score = sc.sb("score", [P, 2, STEP, HEADS])
        halves = sc.sb("halves", [P, 2, 2, STEP * HEADS], BF16)
        tile_most = sc.sb("tile_most", [P, 2, STEP, HEADS])
        ps_turn = [sc.ps(f"turn{u}", [P, STEP * P]) for u in range(2)]
        ps_q = [sc.ps(f"q{u}", [P, STEP * D]) for u in range(2)]
        ps_all = [sc.ps(f"all{u}", [P, STEP, HEADS * P]) for u in range(2)]
        gathered = [sc.sem(f"gathered{r}") for r in range(RING)]
        indexed, begun, cleared = sc.sem("indexed"), sc.sem("begun"), sc.sem("cleared")
        act_distance, act_onehot, pe_turned, act_turned, act_away = (sc.sem(s) for s in (
            "act_distance", "act_onehot", "pe_turned", "act_turned", "act_away"))
        pe_q, dve_product, dve_score, act_kept = (sc.sem(s) for s in ("pe_q", "dve_product", "dve_score", "act_kept"))
        act_upper, dve_halves, pe_all, dve_most, dve_merged = (sc.sem(s) for s in (
            "act_upper", "dve_halves", "pe_all", "dve_most", "dve_merged"))
        block = ctx.enter_context(nc.Block())

        @block.gpsimd
        def _(pool):
            gather_rows(nc, pool, k_table, rows, index, indexed, begun, gathered)

        @block.scalar
        def _(act):
            for s in (act_distance, act_onehot, act_turned, act_away, act_kept, act_upper):
                nc.scalar.sem_inc(s, AHEAD)
            for s in range(STEPS):
                copy_index(nc, index, other_of, s * STEP, s, indexed)

            def turn(i, s):
                u, v = s % 2, s % SLOTS
                done(act, pe_turned, i, s)
                done(act, pe_q, i, s, SLOTS)
                nc.scalar.activation(turned[:, v, :, :].rearrange("p g e -> p (g e)"), ps_turn[u][:, :],
                                     ACT.Copy).then_inc(act_turned, 1)
                done(act, pe_all, i, s, SLOTS)
                nc.scalar.activation(away[:, v, :, :].rearrange("p g e -> p (g e)"), ps_turn[u][:, :], ACT.Copy, bias=-FAR,
                                     scale=FAR).then_inc(act_away, 1)

            def measure(i, s):
                done(act, act_onehot, i, s, 1)
                for g in range(STEP):
                    ins = nc.scalar.activation(distance[:, g, :], consts["iota_lf"][:, :], ACT.Abs, scale=-1.0,
                                               bias=local_of[:, at(i * RING + (s * STEP + g))])
                ins.then_inc(act_distance, 1)

            def onehots(i, s):
                done(act, act_distance, i, s)
                done(act, pe_turned, i, s, 2)
                nc.scalar.activation(onehot[:, s % 2, :, :], distance[:, :, :], ACT.Relu, scale=-1.0,
                                     bias=consts["ones"][:, 0:1]).then_inc(act_onehot, 1)
            for s in range(EARLY):
                measure(0, s)
                onehots(0, s)
                turn(0, s)
            measure(0, EARLY)
            onehots(0, EARLY)
            with act.Fori(0, ET // RING) as i:
                for s in range(STEPS):
                    measure(i, s + EARLY + 1)
                    done(act, dve_product, i, s)
                    copy_index(nc, index, other_of, i * RING + (s * STEP + RING), s, indexed)
                    done(act, dve_score, i, s)
                    done(act, pe_all, i, s, 2)
                    nc.scalar.activation(halves[:, s % 2, 0, :], score[:, s % 2, :, :].rearrange("p g h -> p (g h)"),
                                         ACT.Copy).then_inc(act_upper, 1)
                    nc.scalar.activation(scores[:, at(i * RING + s * STEP, STEP), :], score[:, s % 2, :, :],
                                         ACT.Copy).then_inc(act_kept, 1)
                    turn(i, s + EARLY)
                    onehots(i, s + EARLY + 1)

        @block.tensor
        def _(pe):
            for s in (pe_turned, pe_q, pe_all):
                nc.tensor.sem_inc(s, AHEAD)

            def turn(i, s):
                u = s % 2
                done(pe, act_onehot, i, s)
                done(pe, act_away, i, s, 2)
                for g in range(STEP):
                    tr = nc.tensor.transpose(ps_turn[u][:, g * P:(g + 1) * P], onehot[:, u, g, :], consts["ident"][:, :])
                tr.then_inc(pe_turned, 1)

            regs = bucket_registers(pe, "pe_score")

            def take_q(i, s, buckets):
                u = s % 2
                done(pe, act_turned, i, s)
                done(pe, dve_product, i, s, 2)
                for g in range(STEP):
                    b = buckets[s * STEP + g]
                    for part in range(3):
                        mm = nc.tensor.matmul(ps_q[u][:, g * D:(g + 1) * D], turned[:, s % SLOTS, g, :],
                                              Q3[:, at(b), part * D:(part + 1) * D].rearrange("p o d -> p (o d)"),
                                              start=(part == 0), stop=(part == 2))
                mm.then_inc(pe_q, 1)

            def spread(i, s):
                u = s % 2
                done(pe, act_away, i, s)
                done(pe, dve_halves, i, s)
                done(pe, dve_most, i, s, 2)
                for g in range(STEP):
                    nc.tensor.matmul(ps_all[u][:, g, :].rearrange("p (h e) -> p h e", h=HEADS), consts["ident_b"][:, :],
                                     away[:, s % SLOTS, g, None, :].to_broadcast([P, HEADS, P]), start=True, stop=False,
                                     skip_group_check=True)
                    for h in range(HEADS):
                        for part in range(2):
                            c = g * HEADS + h
                            mm = nc.tensor.matmul(ps_all[u][:, g, h * P:(h + 1) * P],
                                                  halves[:, u, part, c:c + 1].to_broadcast([P, P]), consts["ident_b"][:, :],
                                                  start=False, stop=(h == HEADS - 1 and part == 1), skip_group_check=True)
                mm.then_inc(pe_all, 1)
            for s in range(EARLY):
                turn(0, s)
            take_q(0, 0, load_buckets(pe, regs, bucket_of, LEAD))

            def round_of(i, first=False):
                buckets = load_buckets(pe, regs, bucket_of, i * RING + LEAD)
                for s in range(STEPS):
                    take_q(i, s + 1, buckets)
                    turn(i, s + EARLY)
                    if s > 0 or not first:
                        spread(i, s - 1)
            round_of(0, first=True)
            with pe.Fori(1, ET // RING) as i:
                round_of(i)
            spread(ET // RING - 1, STEPS - 1)

        @block.vector
        def _(dve):
            for s in (dve_product, dve_score, dve_halves, dve_most):
                nc.vector.sem_inc(s, AHEAD)
            nc.vector.memset(most[:, :, :], -FAR).then_inc(cleared, 1)
            nc.vector.memset(scores[:, ET:ETX, :], 0.0).then_inc(cleared, 1)
            dve.wait_ge(cleared, 2)

            def multiply(i, s):
                done(dve, pe_q, i, s)
                for g in range(STEP):
                    dve.wait_ge(gathered[s * STEP + g], i * 16 + 16)
                done(dve, dve_score, i, s, 1)
                nc.vector.tensor_tensor(product[:, :, :].rearrange("p g d -> p (g d)"), ps_q[s % 2][:, :],
                                        rows[:, s * STEP:(s + 1) * STEP, :].rearrange("p g d -> p (g d)"),
                                        ALU.mult).then_inc(dve_product, 1)

            def sum_up(i, s):
                done(dve, dve_product, i, s)
                done(dve, act_kept, i, s, 2)
                done(dve, dve_halves, i, s, 2)
                nc.vector.tensor_reduce(score[:, s % 2, :, :], product[:, :, :].rearrange("p g (h c) -> p g h c", h=HEADS),
                                        AX, ALU.add).then_inc(dve_score, 1)

            def lower_half(i, s):
                done(dve, act_upper, i, s)
                nc.vector.tensor_tensor(halves[:, s % 2, 1, :], score[:, s % 2, :, :].rearrange("p g h -> p (g h)"),
                                        halves[:, s % 2, 0, :], ALU.subtract).then_inc(dve_halves, 1)

            def find_most(i, s):
                u = s % 2
                done(dve, pe_all, i, s)
                nc.vector.tensor_reduce(tile_most[:, u, :, :], ps_all[u][:, :, :].rearrange("p g (h e) -> p g h e", h=HEADS),
                                        AX, ALU.max).then_inc(dve_most, 1)

            def merge(i, s, g, buckets):
                if g == 0:
                    done(dve, dve_most, i, s)
                cur = flat(most[:, at(buckets[LEAD + s * STEP + g]), :])
                dve.wait_ge(dve_merged, i * RING + (s * STEP + g + RING))
                nc.vector.tensor_tensor(cur, cur, tile_most[:, s % 2, g, :], ALU.max).then_inc(dve_merged, 1)

            regs = bucket_registers(dve, "dve_score")

            def round_of(i, first=False):
                buckets = load_buckets(dve, regs, bucket_of, i * RING)
                for s in range(STEPS):
                    multiply(i, s)
                    if s > 0 or not first:
                        lower_half(i, s - 1)
                    if s > 2 or not first:
                        merge(i, s - 3, 0, buckets)
                    sum_up(i, s)
                    if s > 2 or not first:
                        merge(i, s - 3, 1, buckets)
                    if s > 1 or not first:
                        find_most(i, s - 2)
            nc.vector.sem_inc(dve_merged, RING)
            round_of(0, first=True)
            with dve.Fori(1, ET // RING) as i:
                round_of(i)
            last = ET // RING - 1
            buckets = load_buckets(dve, regs, bucket_of, last * RING)
            lower_half(last, STEPS - 1)
            for s in (STEPS - 3, STEPS - 2, STEPS - 1):
                if s > STEPS - 3:
                    find_most(last, s)
                for g in range(STEP):
                    merge(last, s, g, buckets)


def attend(nc, consts, v_table, edges, total, scores, most2):
    local_of, other_of, bucket_of = edges
    with ExitStack() as ctx:
        sc = Scope(nc, ctx, "attend")
        rows = sc.sb("rows", [P, RING, D])
        index = sc.sb("index", [P, RING], I32)
        onehot = sc.sb("onehot", [P, SLOTS, STEP, P])
        turned = sc.sb("turned", [P, 2, STEP, P], BF16)
        less = sc.sb("less", [P, 2, STEP, HEADS])
        message = sc.sb("message", [P, 2, STEP, AW])
        ps_turn = [sc.ps(f"turn{u}", [P, BANK]) for u in range(2)]
        ps_most = [sc.ps(f"most{u}", [P, BANK]) for u in range(2)]
        ps_sum = [[sc.ps(f"sum{u}{g}", [P, BANK]) for g in range(STEP)] for u in range(2)]
        gathered = [sc.sem(f"gathered{r}") for r in range(RING)]
        indexed, begun, cleared, each_added = sc.sem("indexed"), sc.sem("begun"), sc.sem("cleared"), sc.sem("each_added")
        dve_onehot, pe_turned, act_turned, pe_most = (sc.sem(s) for s in ("dve_onehot", "pe_turned", "act_turned", "pe_most"))
        dve_less, act_exp, dve_message, pe_summed = (sc.sem(s) for s in ("dve_less", "act_exp", "dve_message", "pe_summed"))
        block = ctx.enter_context(nc.Block())

        @block.gpsimd
        def _(pool):
            gather_rows(nc, pool, v_table, rows, index, indexed, begun, gathered)

        @block.scalar
        def _(act):
            for s in (act_turned, act_exp):
                nc.scalar.sem_inc(s, AHEAD)
            for s in range(STEPS):
                copy_index(nc, index, other_of, s * STEP, s, indexed)

            def turn(i, s):
                u = s % 2
                done(act, pe_turned, i, s)
                done(act, pe_most, i, s, 2)
                nc.scalar.activation(turned[:, u, :, :].rearrange("p g e -> p (g e)"), ps_turn[u][:, 0:STEP * P],
                                     ACT.Copy).then_inc(act_turned, 1)

            def exponential(i, s):
                u = s % 2
                done(act, dve_less, i, s)
                done(act, pe_summed, i, s, 2)
                nc.scalar.activation(message[:, u, :, D:AW], less[:, u, :, :], ACT.Exp).then_inc(act_exp, 1)
            turn(0, 0)
            turn(0, 1)
            exponential(0, 0)
            with act.Fori(0, ET // RING) as i:
                for s in range(STEPS):
                    exponential(i, s + 1)
                    turn(i, s + 2)
                    done(act, dve_message, i, s)
                    copy_index(nc, index, other_of, i * RING + (s * STEP + RING), s, indexed)

        @block.tensor
        def _(pe):
            for s in (pe_turned, pe_most, pe_summed):
                nc.tensor.sem_inc(s, AHEAD)

            regs = bucket_registers(pe, "pe_attend")

            def turn(i, s):
                u = s % 2
                done(pe, dve_onehot, i, s)
                done(pe, act_turned, i, s, 2)
                for g in range(STEP):
                    tr = nc.tensor.transpose(ps_turn[u][:, g * P:(g + 1) * P], onehot[:, s % SLOTS, g, :],
                                             consts["ident"][:, :])
                tr.then_inc(pe_turned, 1)

            def take_most(i, s, buckets):
                u = s % 2
                done(pe, act_turned, i, s)
                done(pe, dve_less, i, s, 2)
                for g in range(STEP):
                    b = buckets[s * STEP + g]
                    for part in range(2):
                        mm = nc.tensor.matmul(ps_most[u][:, g * HEADS:(g + 1) * HEADS], turned[:, u, g, :],
                                              most2[:, at(b), part * HEADS:(part + 1) * HEADS].rearrange("p o d -> p (o d)"),
                                              start=(part == 0), stop=(part == 1))
                mm.then_inc(pe_most, 1)

            def sum_up(i, s):
                u = s % 2
                done(pe, dve_message, i, s)
                pe.wait_ge(each_added, i * RING + ((s - 1) * STEP + AHEAD * STEP))
                for g in range(STEP):
                    mm = nc.tensor.matmul(ps_sum[u][g][:, 0:AW], onehot[:, s % SLOTS, g, :], message[:, u, g, :], start=True,
                                          stop=True)
                mm.then_inc(pe_summed, 1)

            for s in range(EARLY):
                turn(0, s)
            buckets = load_buckets(pe, regs, bucket_of, LEAD)
            take_most(0, 0, buckets)
            take_most(0, 1, buckets)
            with pe.Fori(0, ET // RING) as i:
                buckets = load_buckets(pe, regs, bucket_of, i * RING + LEAD)
                for s in range(STEPS):
                    sum_up(i, s)
                    take_most(i, s + 2, buckets)
                    turn(i, s + EARLY)

        @block.vector
        def _(dve):
            for s in (dve_onehot, dve_less, dve_message):
                nc.vector.sem_inc(s, AHEAD)
            nc.vector.sem_inc(each_added, AHEAD * STEP)
            nc.vector.memset(total[:, :, :], 0.0).then_inc(cleared, 1)
            dve.wait_ge(cleared, 1)

            def onehots(i, s):
                done(dve, pe_summed, i, s, SLOTS)
                make_onehot(nc, consts, onehot[:, s % SLOTS, :, :], local_of, i * RING + s * STEP, STEP, dve_onehot)

            def subtract_most(i, s):
                u = s % 2
                done(dve, pe_most, i, s)
                done(dve, act_exp, i, s, 2)
                nc.vector.tensor_tensor(less[:, u, :, :], scores[:, at(i * RING + s * STEP, STEP), :],
                                        ps_most[u][:, 0:STEP * HEADS].rearrange("p (g h) -> p g h", g=STEP),
                                        ALU.subtract).then_inc(dve_less, 1)

            def weigh(i, s):
                u = s % 2
                done(dve, act_exp, i, s)
                for g in range(STEP):
                    dve.wait_ge(gathered[s * STEP + g], i * 16 + 16)
                nc.vector.tensor_tensor(message[:, u, :, 0:D].rearrange("p g (h c) -> p g h c", h=HEADS),
                                        rows[:, s * STEP:(s + 1) * STEP, :].rearrange("p g (h c) -> p g h c", h=HEADS),
                                        message[:, u, :, D:AW, None].to_broadcast([P, STEP, HEADS, C]),
                                        ALU.mult).then_inc(dve_message, 1)

            regs = bucket_registers(dve, "dve_attend")

            def round_of(i, first=False):
                buckets = load_buckets(dve, regs, bucket_of, i * RING)
                for s in range(STEPS):
                    adding = s > 0 or not first
                    weigh(i, s)
                    subtract_most(i, s + 1)
                    if adding:
                        add_sum(nc, dve, total, ps_sum[(s - 1) % 2], buckets, i, s - 1, 0, AW, pe_summed, each_added)
                    onehots(i, s + EARLY)
                    if adding:
                        add_sum(nc, dve, total, ps_sum[(s - 1) % 2], buckets, i, s - 1, 1, AW, pe_summed, each_added)
            for s in range(EARLY):
                onehots(0, s)
            subtract_most(0, 0)
            round_of(0, first=True)
            with dve.Fori(1, ET // RING) as i:
                round_of(i)
            buckets = load_buckets(dve, regs, bucket_of, ET - RING)
            for g in range(STEP):
                add_sum(nc, dve, total, ps_sum[(STEPS - 1) % 2], buckets, ET // RING - 1, STEPS - 1, g, AW, pe_summed,
                        each_added)


def add_sum(nc, dve, total, ps, buckets, i, s, g, width, pe_summed, each_added):
    if g == 0:
        done(dve, pe_summed, i, s)
    cur = flat(total[:, at(buckets[LEAD + s * STEP + g]), 0:width])
    dve.wait_ge(each_added, i * RING + (s * STEP + g + AHEAD * STEP))
    nc.vector.tensor_tensor(cur, cur, ps[g][:, 0:width], ALU.add).then_inc(each_added, 1)


def edge_sums(nc, tag, consts, table, edges, total, place=None, sorting=None):
    local_of, other_of, bucket_of = edges
    with ExitStack() as ctx:
        sc = Scope(nc, ctx, tag)
        rows = sc.sb("rows", [P, RING, D + 1])
        index = sc.sb("index", [P, RING], I32)
        onehot = sc.sb("onehot", [P, SLOTS, STEP, P])
        ps_sum = [[sc.ps(f"sum{u}{g}", [P, 512]) for g in range(STEP)] for u in range(2)]
        gathered = [sc.sem(f"gathered{r}") for r in range(RING)]
        indexed, begun, cleared, each_added = sc.sem("indexed"), sc.sem("begun"), sc.sem("cleared"), sc.sem("each_added")
        dve_onehot, pe_summed = sc.sem("dve_onehot"), sc.sem("pe_summed")
        rounds = ET // RING
        sort = placement(nc, sc, consts, place, sorting, RING) if place is not None else None
        sorted_at = EC // RING if sort else rounds
        assert sorted_at <= rounds

        def each_round(eng, work, start=0):
            with eng.Fori(start, sorted_at) as i:
                work(i, STEP if sort else 0)
            if sorted_at < rounds:
                with eng.Fori(sorted_at, rounds) as i:
                    work(i, 0)
        block = ctx.enter_context(nc.Block())

        @block.gpsimd
        def _(pool):
            gather_rows(nc, pool, table, rows, index, indexed, begun, gathered)

        @block.scalar
        def _(act):
            for s in range(STEPS):
                copy_index(nc, index, other_of, s * STEP, s, indexed)
            if sort:
                sort["scalar_start"]()

            def work(i, columns):
                for s in range(STEPS):
                    for n in range(s * columns + 1, (s + 1) * columns, 2):
                        sort["scalar_column"](act, i, n)
                    done(act, pe_summed, i, s)
                    copy_index(nc, index, other_of, i * RING + (s * STEP + RING), s, indexed)
            each_round(act, work)

        @block.tensor
        def _(pe):
            nc.tensor.sem_inc(pe_summed, AHEAD)
            pe.wait_ge(cleared, 2)
            if sort:
                sort["tensor_start"](pe)

            def work(i, columns):
                for s in range(STEPS):
                    u = s % 2
                    done(pe, dve_onehot, i, s)
                    pe.wait_ge(each_added, i * RING + ((s - 1) * STEP + AHEAD * STEP))
                    for g in range(STEP):
                        r = s * STEP + g
                        pe.wait_ge(gathered[r], i * 16 + 16)
                        mm = nc.tensor.matmul(ps_sum[u][g][:, 0:D + 1], onehot[:, s % SLOTS, g, :], rows[:, r, :], start=True, stop=True)
                    mm.then_inc(pe_summed, 1)
                    for n in range(s * columns, (s + 1) * columns):
                        sort["tensor_column"](pe, i, n)
            each_round(pe, work)

        @block.vector
        def _(dve):
            nc.vector.sem_inc(dve_onehot, AHEAD)
            nc.vector.sem_inc(each_added, AHEAD * STEP)
            nc.vector.memset(total[:, :, :], 0.0).then_inc(cleared, 1)
            nc.vector.memset(rows[:, :, D:D + 1], 1.0).then_inc(cleared, 1)
            dve.wait_ge(cleared, 2)

            def onehots(i, s):
                done(dve, pe_summed, i, s, SLOTS)
                make_onehot(nc, consts, onehot[:, s % SLOTS, :, :], local_of, i * RING + s * STEP, STEP, dve_onehot)
            regs = bucket_registers(dve, f"dve_{tag}")

            def add(buckets, i, s, g):
                add_sum(nc, dve, total, ps_sum[s % 2], buckets, i, s, g, D + 1, pe_summed, each_added)

            def work(i, columns, first=False):
                buckets = load_buckets(dve, regs, bucket_of, i * RING)
                for s in range(STEPS):
                    onehots(i, s + 2)
                    for g in range(STEP):
                        if s > 0 or not first:
                            add(buckets, i, s - 1, g)
                        if columns:
                            sort["vector_column"](dve, i, s * columns + g)
            for s in range(2):
                onehots(0, s)
            if sort:
                sort["vector_start"]()
            work(0, STEP if sort else 0, first=True)
            each_round(dve, work, start=1)
            buckets = load_buckets(dve, regs, bucket_of, ET - RING)
            for g in range(STEP):
                add(buckets, rounds - 1, STEPS - 1, g)
            if sort:
                sort["vector_end"](dve)


def join_attention(nc, total, skip, X):
    with ExitStack() as ctx:
        sc = Scope(nc, ctx, "join")
        none = sc.sb("none", [P, NT, HEADS])
        chain = sc.sem("chain")
        block = ctx.enter_context(nc.Block())

        @block.vector
        def _(dve):
            then = chained(dve, chain)
            den = total[:, :, D:AW]
            then(nc.vector.tensor_scalar(none[:, :, :], den, 0.0, None, ALU.is_equal))
            then(nc.vector.tensor_tensor(none[:, :, :], none[:, :, :], den, ALU.add))
            then(nc.vector.reciprocal(none[:, :, :], none[:, :, :]))
            for h in range(HEADS):
                part = total[:, :, h * C:(h + 1) * C]
                then(nc.vector.tensor_tensor(part, part, none[:, :, h:h + 1].to_broadcast([P, NT, C]), ALU.mult))
            then(nc.vector.tensor_tensor(skip[:, :, :], skip[:, :, :], total[:, :, 0:D], ALU.add))
            then(nc.vector.tensor_tensor(X[:, :, :], X[:, :, :], skip[:, :, :], ALU.add))


def divide_by_count(nc, tag, total, table=None, bias=None, slope=None, residual=None, dest=None, add_to=None):
    with ExitStack() as ctx:
        sc = Scope(nc, ctx, tag)
        inv = sc.sb("inv", [P, NT])
        some = sc.sb("some", [P, NT])
        b_row = sc.sb("b_row", [P, D])
        a = sc.sb("a", [P, 1])
        low = sc.sb("low", [P, NT, D]) if dest is not None or add_to is not None else None
        loaded, chain, divided, stored = sc.sem("loaded"), sc.sem("chain"), sc.sem("divided"), sc.sem("stored")
        block = ctx.enter_context(nc.Block())

        @block.sync
        def _(sp):
            if table is not None:
                for g in range(GROUPS):
                    sp.wait_ge(divided, g + 1)
                    sp.dma_start(table[g * GW:(g + 1) * GW, :].rearrange("(b p) d -> p b d", p=P),
                                 total[:, g * GT:(g + 1) * GT, 0:D]).then_inc(stored, 16)
                sp.wait_ge(stored, 16 * GROUPS)
            else:
                sp.dma_start(b_row[:, :], row(bias)).then_inc(loaded, 16)
                sp.dma_start(a[:, :], row(slope, 1)).then_inc(loaded, 16)

        @block.vector
        def _(dve):
            then = chained(dve, chain)
            count = total[:, :, D]
            then(nc.vector.tensor_scalar(inv[:, :], count, 1.0, None, ALU.max))
            then(nc.vector.reciprocal(inv[:, :], inv[:, :]))
            then(nc.vector.tensor_scalar(some[:, :], count, 1.0, None, ALU.min))
            then(nc.vector.tensor_tensor(inv[:, :], inv[:, :], some[:, :], ALU.mult))
            if table is not None:
                for g in range(GROUPS):
                    part = total[:, g * GT:(g + 1) * GT, 0:D]
                    nc.vector.tensor_tensor(part, part, inv[:, g * GT:(g + 1) * GT, None].to_broadcast([P, GT, D]),
                                            ALU.mult).then_inc(divided, 1)
                return
            body = total[:, :, 0:D]
            then(nc.vector.tensor_tensor(body, body, inv[:, :, None].to_broadcast([P, NT, D]), ALU.mult))
            dve.wait_ge(loaded, 32)
            then(nc.vector.tensor_tensor(body, body, b_row[:, None, :].to_broadcast([P, NT, D]), ALU.add))
            if residual is not None:
                then(nc.vector.tensor_tensor(body, body, residual[:, :, :], ALU.add))
            then(nc.vector.tensor_scalar(low[:, :, :], body, 0.0, a[:, 0:1], ALU.min, ALU.mult))
            if dest is not None:
                then(nc.vector.scalar_tensor_tensor(out=dest[:, :, :], in0=body, scalar=0.0, in1=low[:, :, :],
                                                    op0=ALU.max, op1=ALU.add))
            else:
                then(nc.vector.scalar_tensor_tensor(out=body, in0=body, scalar=0.0, in1=low[:, :, :],
                                                    op0=ALU.max, op1=ALU.add))
                then(nc.vector.tensor_tensor(add_to[:, :, :], add_to[:, :, :], body, ALU.add))


def top_two(nc, sc, then, consts, probs, T):
    found = []
    left = probs
    for n in range(2):
        best = sc[f"best{n}"]
        first = sc[f"first{n}"]
        one = sc[f"one{n}"]
        wide = [P, T, EXPERTS]
        names = consts["iota_e"][:, None, :].to_broadcast(wide)
        then(nc.vector.tensor_reduce(best[:, :], left[:, :, :], AX, ALU.max))
        then(nc.vector.tensor_tensor(one[:, :, :], left[:, :, :], best[:, :, None].to_broadcast(wide), ALU.is_equal))
        then(nc.vector.tensor_tensor(one[:, :, :], one[:, :, :], names, ALU.mult))
        then(nc.vector.tensor_reduce(first[:, :], one[:, :, :], AX, ALU.min))
        then(nc.vector.tensor_tensor(one[:, :, :], first[:, :, None].to_broadcast(wide), names, ALU.is_equal))
        if n == 0:
            then(nc.vector.scalar_tensor_tensor(out=sc["left"][:, :, :], in0=one[:, :, :], scalar=-4.0, in1=probs[:, :, :],
                                                op0=ALU.mult, op1=ALU.add))
            left = sc["left"]
        found.append((best, first, one))
    return found


def top_buffers(sc, T):
    out = {"left": sc.sb("left", [P, T, EXPERTS])}
    for n in range(2):
        out[f"best{n}"] = sc.sb(f"best{n}", [P, T])
        out[f"first{n}"] = sc.sb(f"first{n}", [P, T])
        out[f"one{n}"] = sc.sb(f"one{n}", [P, T, EXPERTS])
    return out


def softmax_steps(nc, dve, then, peak, sums, x, T, exp_asked, exp_done, n):
    shape = [P, T, x.shape[2]]
    then(nc.vector.tensor_reduce(peak[:, :], x[:, :, :], AX, ALU.max))
    nc.vector.tensor_tensor(x[:, :, :], x[:, :, :], peak[:, :, None].to_broadcast(shape), ALU.subtract).then_inc(exp_asked, 1)
    dve.wait_ge(exp_done, n)
    then(nc.vector.tensor_reduce(sums[:, :], x[:, :, :], AX, ALU.add))
    then(nc.vector.reciprocal(sums[:, :], sums[:, :]))
    then(nc.vector.tensor_tensor(x[:, :, :], x[:, :, :], sums[:, :, None].to_broadcast(shape), ALU.mult))


def route_all(nc, consts, U, Wr, br, chosen, gate):
    capacity = float(math.ceil(N * 1.25 / EXPERTS))
    with ExitStack() as ctx:
        sc = Scope(nc, ctx, "route")
        wr = sc.sb("wr", [P, D, EXPERTS])
        wide = sc.sb("wide", [P, D, EXPERTS])
        br_row = sc.sb("br_row", [P, 1, EXPERTS])
        mean = sc.sb("mean", [P, D])
        rw = sc.sb("rw", [P, 1, EXPERTS])
        load = sc.sb("load", [P, 1, EXPERTS])
        over = sc.sb("over", [P, 1, EXPERTS])
        two = sc.sb("two", [P, 1, 2])
        peak, sums = sc.sb("peak", [P, 1]), sc.sb("sums", [P, 1])
        tops = top_buffers(sc, 1)
        total = sc.ps("total", [P, D])
        loaded, chain, summed = sc.sem("loaded"), sc.sem("chain"), sc.sem("summed")
        exp_asked, exp_done = sc.sem("exp_asked"), sc.sem("exp_done")
        block = ctx.enter_context(nc.Block())

        @block.sync
        def _(sp):
            sp.dma_start(wr[:, :, :].rearrange("p d e -> p (d e)"), row(Wr.rearrange("d e -> (d e)"), D * EXPERTS)).then_inc(loaded, 16)
            sp.dma_start(br_row[:, 0, :], row(br, EXPERTS)).then_inc(loaded, 16)

        @block.tensor
        def _(pe):
            nc.tensor.matmul(total[:, :], consts["real"][:, :], U[:, NT - 1, :], start=True, stop=False)
            for t in range(NT - 1):
                mm = nc.tensor.matmul(total[:, :], consts["ones"][:, :], U[:, t, :], start=False, stop=(t == NT - 2))
            mm.then_inc(summed, 1)

        @block.scalar
        def _(act):
            for n, x in enumerate((rw, rw, two)):
                act.wait_ge(exp_asked, n + 1)
                nc.scalar.activation(x[:, :, :], x[:, :, :], ACT.Exp).then_inc(exp_done, 1)

        @block.vector
        def _(dve):
            then = chained(dve, chain)
            dve.wait_ge(loaded, 32)
            dve.wait_ge(summed, 1)
            then(nc.vector.tensor_scalar(mean[:, :], total[:, :], 1.0 / N, None, ALU.mult))
            then(nc.vector.tensor_tensor(wide[:, :, :], wr[:, :, :], mean[:, :, None].to_broadcast([P, D, EXPERTS]), ALU.mult))
            then(nc.vector.tensor_reduce(rw[:, 0, :], wide[:, :, :].rearrange("p d e -> p e d"), AX, ALU.add))
            then(nc.vector.tensor_tensor(rw[:, :, :], rw[:, :, :], br_row[:, :, :], ALU.add))
            softmax_steps(nc, dve, then, peak, sums, rw, 1, exp_asked, exp_done, 1)
            then(nc.vector.tensor_scalar(load[:, :, :], rw[:, :, :], float(N), None, ALU.mult))
            then(nc.vector.tensor_scalar(over[:, :, :], load[:, :, :], capacity, None, ALU.max))
            then(nc.vector.reciprocal(over[:, :, :], over[:, :, :]))
            then(nc.vector.scalar_tensor_tensor(out=rw[:, :, :], in0=over[:, :, :], scalar=capacity, in1=rw[:, :, :],
                                                op0=ALU.mult, op1=ALU.mult))
            softmax_steps(nc, dve, then, peak, sums, rw, 1, exp_asked, exp_done, 2)
            found = top_two(nc, tops, then, consts, rw, 1)
            for n, (best, first, one) in enumerate(found):
                then(nc.vector.tensor_copy(two[:, 0, n:n + 1], best[:, :]))
                then(nc.vector.tensor_scalar(chosen[:, n:n + 1], first[0:1, :], float(EXPERTS), None, ALU.add))
            softmax_steps(nc, dve, then, peak, sums, two, 1, exp_asked, exp_done, 3)
            then(nc.vector.tensor_copy(gate[:, :], two[:, 0, :]))


def route_each(nc, consts, logits, br, gate, put, get, expert_of):
    with ExitStack() as ctx:
        sc = Scope(nc, ctx, "each")
        br_row = sc.sb("br_row", [P, EXPERTS])
        peak, sums = sc.sb("peak", [P, NT]), sc.sb("sums", [P, NT])
        tops = top_buffers(sc, NT)
        member = sc.sb("member", [P, EXPERTS, NT])
        running = sc.sb("running", [P, EXPERTS, NT])
        zero = sc.sb("zero", [P, 1])
        upto, count = sc.sb("upto", [P, EXPERTS]), sc.sb("count", [P, EXPERTS])
        batches_i, batches = sc.sb("batches_i", [P, EXPERTS], I32), sc.sb("batches", [P, EXPERTS])
        first, offset = sc.sb("first", [P, EXPERTS]), sc.sb("offset", [P, EXPERTS])
        place, missing = sc.sb("place", [P, NT]), sc.sb("missing", [P, NT])
        begun, begun_sum = sc.sb("begun", [1, BATCHES, EXPERTS]), sc.sb("begun_sum", [1, BATCHES])
        ps_before, ps_total = sc.ps("before", [P, BANK]), sc.ps("total", [P, BANK])
        loaded, chain, exp_asked, exp_done = sc.sem("loaded"), sc.sem("chain"), sc.sem("exp_asked"), sc.sem("exp_done")
        counted, summed = sc.sem("counted"), sc.sem("summed")
        block = ctx.enter_context(nc.Block())
        wide = [P, NT, EXPERTS]

        @block.sync
        def _(sp):
            sp.dma_start(br_row[:, :], row(br, EXPERTS)).then_inc(loaded, 16)

        @block.scalar
        def _(act):
            act.wait_ge(exp_asked, 1)
            nc.scalar.activation(logits[:, :, :], logits[:, :, :], ACT.Exp).then_inc(exp_done, 1)

        @block.tensor
        def _(pe):
            pe.wait_ge(counted, 1)
            nc.tensor.matmul(ps_before[:, 0:EXPERTS], consts["below"][:, :], count[:, :], start=True, stop=True)
            nc.tensor.matmul(ps_total[:, 0:EXPERTS], consts["ones"][:, :], count[:, :], start=True,
                             stop=True).then_inc(summed, 1)

        @block.vector
        def _(dve):
            then = chained(dve, chain)
            nc.vector.memset(zero[:, :], 0.0)
            dve.wait_ge(loaded, 16)
            then(nc.vector.tensor_tensor(logits[:, :, :], logits[:, :, :], br_row[:, None, :].to_broadcast(wide), ALU.add))
            softmax_steps(nc, dve, then, peak, sums, logits, NT, exp_asked, exp_done, 1)
            found = top_two(nc, tops, then, consts, logits, NT)
            then(nc.vector.tensor_tensor(sums[:, :], found[0][0][:, :], found[1][0][:, :], ALU.add))
            then(nc.vector.reciprocal(sums[:, :], sums[:, :]))
            for k, (prob, _, one) in enumerate(found):
                nc.vector.tensor_tensor(gate[:, :, k], prob[:, :], sums[:, :], ALU.mult)
                last = one[:, NT - 1, :]
                then(nc.vector.tensor_tensor(last, last, consts["real"][:, 0:EXPERTS], ALU.mult))
            ones = [one[:, :, :].rearrange("p t e -> p e t") for _, _, one in found]
            then(nc.vector.tensor_tensor(member[:, :, :], ones[0], ones[1], ALU.add))
            then(nc.vector.tensor_tensor_scan(running[:, :, :].rearrange("p e t -> p (e t)"),
                                              member[:, :, :].rearrange("p e t -> p (e t)"),
                                              zero[:, 0:1].to_broadcast([P, EXPERTS * NT]), 0.0, ALU.add, ALU.add))
            then(nc.vector.tensor_copy(upto[:, :], running[:, :, NT - 1]))
            then(nc.vector.tensor_copy(count[:, 0:1], upto[:, 0:1]))
            nc.vector.tensor_tensor(count[:, 1:], upto[:, 1:], upto[:, 0:EXPERTS - 1], ALU.subtract).then_inc(counted, 1)
            dve.wait_ge(summed, 1)
            then(nc.vector.tensor_scalar(batches_i[:, :], ps_total[:, 0:EXPERTS], float(BT - 1), None, ALU.add))
            then(nc.vector.tensor_scalar(batches_i[:, :], batches_i[:, :], BT.bit_length() - 1, None, ALU.arith_shift_right))
            then(nc.vector.tensor_copy(batches[:, :], batches_i[:, :]))
            then(nc.vector.tensor_tensor_scan(first[:, :], batches[:, :], zero[:, 0:1].to_broadcast([P, EXPERTS]), 0.0,
                                              ALU.add, ALU.add))
            then(nc.vector.tensor_tensor(first[:, :], first[:, :], batches[:, :], ALU.subtract))
            then(nc.vector.scalar_tensor_tensor(out=offset[:, :], in0=first[:, :], scalar=float(BT),
                                                in1=ps_before[:, 0:EXPERTS], op0=ALU.mult, op1=ALU.add))
            then(nc.vector.tensor_tensor(offset[:, 1:], offset[:, 1:], upto[:, 0:EXPERTS - 1], ALU.subtract))
            then(nc.vector.tensor_tensor(running[:, :, :], running[:, :, :],
                                         offset[:, :, None].to_broadcast([P, EXPERTS, NT]), ALU.add))
            for k in range(2):
                then(nc.vector.tensor_tensor(member[:, :, :], running[:, :, :], ones[k], ALU.mult))
                then(nc.vector.tensor_reduce(place[:, :], member[:, :, :].rearrange("p e t -> p t e"), AX, ALU.add))
                then(nc.vector.tensor_scalar(missing[:, :], place[:, :], 0.0, consts["spare"][:, k:k + 1], ALU.is_equal,
                                             ALU.mult))
                then(nc.vector.tensor_tensor(missing[:, :], missing[:, :], place[:, :], ALU.add))
                then(nc.vector.tensor_scalar(put[:, :, k], missing[:, :], -1.0, None, ALU.add))
                then(nc.vector.tensor_scalar(get[:, :, k], place[:, :], -1.0, 0.0, ALU.add, ALU.max))
            then(nc.vector.tensor_tensor(begun[:, :, :],
                                         consts["iota_tf"][0:1, 0:BATCHES, None].to_broadcast([1, BATCHES, EXPERTS]),
                                         first[0:1, None, :].to_broadcast([1, BATCHES, EXPERTS]), ALU.is_ge))
            then(nc.vector.tensor_reduce(begun_sum[:, :], begun[:, :, :], AX, ALU.add))
            then(nc.vector.tensor_scalar(expert_of[:, :], begun_sum[:, :], -1.0, None, ALU.add))


def run_experts(nc, consts, U, put, expert_of, params, affine, batch_in, batch_out):
    W1, b1, W2, b2 = params
    F = W1.shape[2]
    J = F // P
    V = BT // P
    with ExitStack() as ctx:
        sc = Scope(nc, ctx, "experts")
        slots = range(WSLOTS)
        w1 = [sc.sb(f"w1_{s}", [P, KD, F]) for s in slots]
        w2 = [sc.sb(f"w2_{s}", [P, J, D]) for s in slots]
        b1c = [sc.sb(f"b1c{s}", [P, J]) for s in slots]
        b2r = [sc.sb(f"b2r{s}", [P, D]) for s in slots]
        gc = [sc.sb(f"gc{s}", [P, KD]) for s in slots]
        bc = [sc.sb(f"bc{s}", [P, KD]) for s in slots]
        x = [sc.sb(f"x{s}", [P, V, D]) for s in slots]
        y = [sc.sb(f"out{s}", [P, V, D]) for s in slots]
        xe = sc.sb("xe", [P, 2, KD, BT])
        hid = sc.sb("hid", [P, J, BT])
        ps_turn = [sc.ps(f"turn{u}", [P, KD * BT]) for u in range(2)]
        ps_h = [sc.ps(f"h{u}", [P, BANK]) for u in range(2)]
        ps_y = [sc.ps(f"y{u}", [P, BANK]) for u in range(2)]
        loads = 6
        loaded = [sc.sem(f"loaded{s}") for s in slots]
        x_loaded = [sc.sem(f"x_loaded{s}") for s in slots]
        stored = [sc.sem(f"stored{s}") for s in slots]
        scattered = sc.sem("scattered")
        pe_turned, dve_xe, pe_h, act_h, pe_y, dve_y = (sc.sem(n) for n in (
            "pe_turned", "dve_xe", "pe_h", "act_h", "pe_y", "dve_y"))
        block = ctx.enter_context(nc.Block())
        rounds = BATCHES // WSLOTS

        def each(eng, body):
            for s in slots:
                body(0, s, True, False)
            with eng.Fori(1, rounds - 1) as i:
                for s in slots:
                    body(i, s, False, False)
            for s in slots:
                body(rounds - 1, s, False, s == WSLOTS - 1)

        def rows_of(table, n):
            return table[at(n * BT, BT), :].rearrange("(v p) d -> p v d", p=P)

        @block.sync
        def _(sp):
            def load_weights(i, s):
                e = sp.value_load(expert_of[0:1, at(i * WSLOTS + s)], min_val=0, max_val=EXPERTS - 1)
                for tile, dram in ((w1[s][:, :, :], W1[at(e), :, :].rearrange("o (k p) f -> p (o k) f", p=P)),
                                   (w2[s][:, :, :], W2[at(e), :, :].rearrange("o (j p) d -> p (o j) d", p=P)),
                                   (b1c[s][:, :], b1[at(e), :].rearrange("o (j p) -> p (o j)", p=P)),
                                   (b2r[s][:, :], b2[at(e), :].to_broadcast([P, D])),
                                   (gc[s][:, :], affine[0][at(e), :].rearrange("o (k p) -> p (o k)", p=P)),
                                   (bc[s][:, :], affine[1][at(e), :].rearrange("o (k p) -> p (o k)", p=P))):
                    sp.dma_start(tile, dram, allow_slow_non_contiguous=True).then_inc(loaded[s], 16)
            for s in slots:
                load_weights(0, s)
            sp.wait_ge(scattered, 16 * 2 * NT)
            for s in slots:
                sp.dma_start(x[s][:, :, :], rows_of(batch_in, s)).then_inc(x_loaded[s], 16)
            with sp.Fori(1, rounds) as i:
                for s in slots:
                    sp.wait_ge(dve_y, i * (WSLOTS * V) + ((s + 1 - WSLOTS) * V + V))
                    load_weights(i, s)
                    sp.dma_start(x[s][:, :, :], rows_of(batch_in, i * WSLOTS + s)).then_inc(x_loaded[s], 16)

        @block.gpsimd
        def _(pool):
            for t in range(NT):
                for k in range(2):
                    pool.indirect_dma_start(batch_in, bass.IndirectOffsetOnAxis(ap=put[:, t, k:k + 1], axis=0),
                                            U[:, t, :], None).then_inc(scattered, 16)

            def body(i, s, first, last):
                n = i * WSLOTS + s
                pool.wait_ge(dve_y, i * (WSLOTS * V) + ((s + 1) * V + V))
                pool.dma_start(rows_of(batch_out, n), y[s][:, :, :]).then_inc(stored[s], 16)
            each(pool, body)
            for s in slots:
                pool.wait_ge(stored[s], 16 * rounds)

        @block.tensor
        def _(pe):
            def turn(i, s):
                u = s % 2
                pe.wait_ge(x_loaded[s], i * 16 + 16)
                pe.wait_ge(dve_xe, i * (WSLOTS * KD) + (s + 1) * KD)
                for k in range(KD):
                    for v in range(V):
                        tr = nc.tensor.transpose(ps_turn[u][:, k * BT + v * P:k * BT + (v + 1) * P],
                                                 x[s][:, v, k * P:(k + 1) * P], consts["ident"][:, :])
                tr.then_inc(pe_turned, 1)

            def body(i, s, first, last):
                u = s % 2
                pe.wait_ge(loaded[s], i * (16 * loads) + 16 * loads)
                pe.wait_ge(dve_xe, i * (WSLOTS * KD) + (s + 3) * KD)
                for j in range(J):
                    pe.wait_ge(act_h, i * (WSLOTS * J) + (s * J + j + 1))
                    for k in range(KD):
                        mm = nc.tensor.matmul(ps_h[j % 2][:, 0:BT], w1[s][:, k, j * P:(j + 1) * P], xe[:, u, k, :],
                                              start=(k == 0), stop=(k == KD - 1))
                    mm.then_inc(pe_h, 1)
                if s < WSLOTS - 1:
                    turn(i, s + 1)
                elif not last:
                    turn(i + 1, 0)
                pe.wait_ge(act_h, i * (WSLOTS * J) + ((s + 1) * J + 2))
                for v in range(V):
                    pe.wait_ge(dve_y, i * (WSLOTS * V) + (s * V + v + 1))
                    for j in range(J):
                        mm = nc.tensor.matmul(ps_y[v][:, 0:D], hid[:, j, v * P:(v + 1) * P], w2[s][:, j, :],
                                              start=(j == 0), stop=(j == J - 1))
                    mm.then_inc(pe_y, 1)
            turn(0, 0)
            each(pe, body)

        @block.scalar
        def _(act):
            nc.scalar.sem_inc(act_h, 2)

            def body(i, s, first, last):
                act.wait_ge(loaded[s], i * (16 * loads) + 16 * loads)
                for j in range(J):
                    act.wait_ge(pe_h, i * (WSLOTS * J) + (s * J + j + 1))
                    nc.scalar.activation(hid[:, j, :], ps_h[j % 2][:, 0:BT], ACT.Gelu, bias=b1c[s][:, j:j + 1]).then_inc(act_h, 1)
            each(act, body)

        @block.vector
        def _(dve):
            nc.vector.sem_inc(dve_xe, 2 * KD)
            nc.vector.sem_inc(dve_y, V)

            def scale_shift(i, s):
                dve.wait_ge(loaded[s], i * (16 * loads) + 16 * loads)
                dve.wait_ge(pe_turned, i * WSLOTS + (s + 1))
                for k in range(KD):
                    nc.vector.tensor_scalar(xe[:, s % 2, k, :], ps_turn[s % 2][:, k * BT:(k + 1) * BT], gc[s][:, k:k + 1],
                                            bc[s][:, k:k + 1], ALU.mult, ALU.add).then_inc(dve_xe, 1)

            def body(i, s, first, last):
                if s < WSLOTS - 1:
                    scale_shift(i, s + 1)
                elif not last:
                    scale_shift(i + 1, 0)
                if not first:
                    dve.wait_ge(stored[s], i * 16)
                for v in range(V):
                    dve.wait_ge(pe_y, i * (WSLOTS * V) + (s * V + v + 1))
                    nc.vector.tensor_tensor(y[s][:, v, :], ps_y[v][:, 0:D], b2r[s][:, :], ALU.add).then_inc(dve_y, 1)
            scale_shift(0, 0)
            each(dve, body)


def join_experts(nc, batch_out, get, gate, X, out):
    with ExitStack() as ctx:
        sc = Scope(nc, ctx, "join_experts")
        rows = sc.sb("rows", [P, NT, 2, D])
        gathered = [sc.sem(f"gathered{g}") for g in range(GROUPS)]
        chain, joined, stored = sc.sem("chain"), sc.sem("joined"), sc.sem("stored")
        block = ctx.enter_context(nc.Block())

        @block.gpsimd
        def _(pool):
            for t in range(NT):
                for k in range(2):
                    pool.indirect_dma_start(rows[:, t, k, :], None, batch_out,
                                            bass.IndirectOffsetOnAxis(ap=get[:, t, k:k + 1], axis=0)).then_inc(
                                                gathered[t // GT], 16)

        @block.vector
        def _(dve):
            then = chained(dve, chain)
            for g in range(GROUPS):
                dve.wait_ge(gathered[g], 16 * 2 * GT)
                lot = rows[:, g * GT:(g + 1) * GT, :, :]
                cur = X[:, g * GT:(g + 1) * GT, :]
                then(nc.vector.tensor_tensor(lot, lot, gate[:, g * GT:(g + 1) * GT, :, None].to_broadcast([P, GT, 2, D]),
                                             ALU.mult))
                then(nc.vector.tensor_tensor(cur, cur, lot[:, :, 0, :], ALU.add))
                nc.vector.tensor_tensor(cur, cur, lot[:, :, 1, :], ALU.add).then_inc(joined, 1)

        @block.sync
        def _(sp):
            for g in range(GROUPS):
                sp.wait_ge(joined, g + 1)
                full = GT if g < GROUPS - 1 else GT - 1
                b0 = g * GT
                sp.dma_start(out[b0 * P:(b0 + full) * P, :].rearrange("(b p) d -> p b d", p=P),
                             X[:, b0:b0 + full, :]).then_inc(stored, 16)
            sp.dma_start(out[(NT - 1) * P:N, :], X[0:TAIL, NT - 1, :]).then_inc(stored, 16)
            sp.wait_ge(stored, 16 * (GROUPS + 1))


def feed_forward(nc, tag, uT, acc, F, experts, params, gate, chosen=None, affine=None):
    W1, b1, W2, b2 = params
    J = F // P
    slots = min(2, experts)
    half = GW // 2
    with ExitStack() as ctx:
        sc = Scope(nc, ctx, tag)
        w1 = [sc.sb(f"w1_{s}", [P, KD, F]) for s in range(slots)]
        w2 = [sc.sb(f"w2_{s}", [P, J, D]) for s in range(slots)]
        b1c = [sc.sb(f"b1_{s}", [P, J]) for s in range(slots)]
        b2r = [sc.sb(f"b2_{s}", [P, D]) for s in range(slots)]
        gc = [sc.sb(f"gc_{s}", [P, KD]) for s in range(slots)]
        bc = [sc.sb(f"bc_{s}", [P, KD]) for s in range(slots)]
        xe = sc.sb("xe", [P, KD, GW])
        hid = sc.sb("hid", [P, J, GW])
        part = sc.sb("part", [P, 2, D])
        ps_h = [sc.ps(f"h{u}", [P, 2, 512]) for u in range(2)]
        ps_y = [sc.ps(f"y{u}", [P, D]) for u in range(2)]
        loaded = [sc.sem(f"loaded{s}") for s in range(slots)]
        weights_used, pool_x, pe_h, act_h = (sc.sem(s) for s in ("weights_used", "pool_x", "pe_h", "act_h"))
        pe_y, dve_part, dve_acc = (sc.sem(s) for s in ("pe_y", "dve_part", "dve_acc"))
        loads = 4 + (2 if affine else 0)
        xs = KD * (2 if affine else 1)
        started = sc.sem("started")
        block = ctx.enter_context(nc.Block())

        def each(eng, body, before=None, after=None):
            def pair(ep):
                for s in range(slots):
                    if before:
                        before(s, ep)
                    with eng.Fori(0, GROUPS) as g:
                        body(s, ep * slots + s, g, (ep * slots + s) * GROUPS + g)
                    if after:
                        after(s, ep)
            if experts > slots:
                with eng.Fori(0, experts // slots) as ep:
                    pair(ep)
            else:
                pair(0)

        @block.sync
        def _(sp):
            def load(s, ep):
                e = ep * slots + s
                if chosen is not None:
                    e = sp.value_load(chosen[0:1, s:s + 1], min_val=0, max_val=EXPERTS - 1)
                sp.wait_ge(weights_used, e + 1) if chosen is None else None
                lot = [(w1[s][:, :, :], W1[at(e), :, :].rearrange("o (k p) f -> p (o k) f", p=P)),
                       (w2[s][:, :, :], W2[at(e), :, :].rearrange("o (j p) d -> p (o j) d", p=P)),
                       (b1c[s][:, :], b1[at(e), :].rearrange("o (j p) -> p (o j)", p=P)),
                       (b2r[s][:, :], b2[at(e), :].to_broadcast([P, D]))]
                if affine:
                    lot += [(gc[s][:, :], affine[0][at(e), :].rearrange("o (k p) -> p (o k)", p=P)),
                            (bc[s][:, :], affine[1][at(e), :].rearrange("o (k p) -> p (o k)", p=P))]
                for tile, dram in lot:
                    sp.dma_start(tile, dram, allow_slow_non_contiguous=True).then_inc(loaded[s], 16)

            if experts > slots:
                with sp.Fori(0, experts // slots) as ep:
                    for s in range(slots):
                        load(s, ep)
            else:
                for s in range(slots):
                    load(s, 0)

        @block.gpsimd
        def _(pool):
            def body(s, e, g, step):
                pool.wait_ge(pe_h, step * J + 2)
                for k in range(KD):
                    u = uT[:, k, at(g * GW, GW)]
                    nc.gpsimd.tensor_copy(xe[:, k, :], u).then_inc(pool_x, 1)
                if affine:
                    pool.wait_ge(pool_x, step * xs + KD)
                    nc.gpsimd.sem_inc(started, 1)
                    for k in range(KD):
                        nc.gpsimd.tensor_scalar(xe[:, k, :], xe[:, k, :], gc[s][:, k:k + 1], bc[s][:, k:k + 1], ALU.mult,
                                                ALU.add).then_inc(pool_x, 1)

            def before(s, ep):
                pool.wait_ge(loaded[s], ep * (16 * loads) + 16 * loads)
                nc.gpsimd.sem_inc(started, 1)
            each(pool, body, before)

        @block.tensor
        def _(pe):
            nc.tensor.sem_inc(pe_h, 2)

            def before(s, ep):
                pe.wait_ge(loaded[s], ep * (16 * loads) + 16 * loads)
                nc.tensor.sem_inc(started, 1)

            def body(s, e, g, step):
                pe.wait_ge(pool_x, step * xs + xs)
                for j in range(J):
                    pe.wait_ge(act_h, step * J + (j + 1))
                    for a in range(2):
                        for k in range(KD):
                            mm = nc.tensor.matmul(ps_h[j % 2][:, a, 0:half], w1[s][:, k, j * P:(j + 1) * P],
                                                  xe[:, k, a * half:(a + 1) * half], start=(k == 0), stop=(k == KD - 1))
                    mm.then_inc(pe_h, 1)
                pe.wait_ge(act_h, step * J + (J + 2))
                for v in range(GT):
                    pe.wait_ge(dve_part, step * GT + (v + 1 if v == 0 else v))
                    for j in range(J):
                        mm = nc.tensor.matmul(ps_y[v % 2][:, :], hid[:, j, v * P:(v + 1) * P], w2[s][:, j, :],
                                              start=(j == 0), stop=(j == J - 1))
                    mm.then_inc(pe_y, 1)

            each(pe, body, before)

        @block.scalar
        def _(act):
            nc.scalar.sem_inc(act_h, 2)

            def before(s, ep):
                act.wait_ge(loaded[s], ep * (16 * loads) + 16 * loads)
                nc.scalar.sem_inc(started, 1)

            def body(s, e, g, step):
                for j in range(J):
                    act.wait_ge(pe_h, step * J + (j + 3))
                    nc.scalar.activation(hid[:, j, :].rearrange("p (a n) -> p a n", a=2), ps_h[j % 2][:, :, 0:half], ACT.Gelu,
                                         bias=b1c[s][:, j:j + 1]).then_inc(act_h, 1)
            each(act, body, before)

        @block.vector
        def _(dve):
            nc.vector.sem_inc(dve_part, 1)
            nc.vector.sem_inc(dve_acc, 2)
            nc.vector.sem_inc(weights_used, slots)

            def before(s, ep):
                dve.wait_ge(loaded[s], ep * (16 * loads) + 16 * loads)
                nc.vector.sem_inc(started, 1)

            def body(s, e, g, step):
                for v in range(GT):
                    dve.wait_ge(pe_y, step * GT + (v + 1))
                    dve.wait_ge(dve_acc, step * GT + (v + 2))
                    nc.vector.tensor_tensor(part[:, v % 2, :], ps_y[v % 2][:, :], b2r[s][:, :], ALU.add).then_inc(dve_part, 1)
                    dve.wait_ge(dve_part, step * GT + (v + 2))
                    cur = flat(acc[:, at(g * GT + v), :])
                    nc.vector.scalar_tensor_tensor(out=cur, in0=part[:, v % 2, :], scalar=gate(g * GT + v, e, s), in1=cur,
                                                   op0=ALU.mult, op1=ALU.add).then_inc(dve_acc, 1)

            def after(s, ep):
                dve.wait_ge(dve_acc, (ep * slots + (s + 1)) * (GROUPS * GT) + 2)
                nc.vector.sem_inc(weights_used, 1)
            each(dve, body, before, after)


def program(nc, x, src, dst, ln1_w, ln1_b, ln2_w, ln2_b, wq, bq, wk, bk, wv, bv, wskip, bskip, w1, b1, w2, b2,
            fWr, fbr, fW1, fb1, fW2, fb2, gamma, beta, hW1, hb1, hW2, hb2, slope,
            mWr, mbr, ln_g, ln_b, mW1, mb1, mW2, mb2, out):
    tables = [nc.dram_tensor(f"table{n}", (NT * P, D), F32, kind="Internal").ap() for n in range(6)]
    batch_in = nc.dram_tensor("batch_in", (BATCHES * BT + 2 * P, D), F32, kind="Internal").ap()
    batch_out = nc.dram_tensor("batch_out", (BATCHES * BT, D), F32, kind="Internal").ap()
    with ExitStack() as ctx:
        keep = Scope(nc, ctx, "keep")
        c = constants(nc, keep)

        def edge_lists(name):
            return (keep.sb(f"{name}_local", [P, ETX]), keep.sb(f"{name}_other", [P, ETX], I32),
                    keep.sb(f"{name}_bucket", [1, LEAD + ETX + LEAD], I32))
        by_dst, by_src = edge_lists("dst"), edge_lists("src")
        with ExitStack() as part:
            place = places(Scope(nc, part, "dst"))
            rank_edges(nc, "rank_dst", dst, src, c, place, by_dst, cleared=batch_in)
            place_edges(nc, "place_dst", c, place, by_dst)

        X = keep.sb("X", [P, NT, D])
        U = keep.sb("U", [P, NT, D])
        load_nodes(nc, x, X)

        layer_norm(nc, "ln_x0", X, U)
        with ExitStack() as part:
            loc = Scope(nc, part, "att")
            Q3 = loc.sb("Q3", [P, NT, 3 * D], BF16)
            with ExitStack() as inner:
                kv = Scope(nc, inner, "kv")
                H, K, V = kv.sb("H", [P, NT, D]), kv.sb("K", [P, NT, D]), kv.sb("V", [P, NT, D])
                layer_norm(nc, "ln_1", U, H, ln1_w, ln1_b)

                q, rest = kv.sb("q", [P, 2, D]), kv.sb("rest", [P, 2, D])

                def handle(u, t, ps, biases, then, settle):
                    then(nc.vector.tensor_tensor(q[:, u, :], ps[:, 0:D], biases[:, 0:D], ALU.add))
                    for n, dest in enumerate((K, V)):
                        then(nc.vector.tensor_tensor(flat(dest[:, at(t), :]), ps[:, (n + 1) * D:(n + 2) * D],
                                                     biases[:, (n + 1) * D:(n + 2) * D], ALU.add))
                    cur = flat(U[:, at(t), :])
                    then(nc.vector.tensor_tensor(cur, cur, biases[:, 3 * D:4 * D], ALU.add))
                    part = [flat(Q3[:, at(t), n * D:(n + 1) * D]) for n in range(3)]
                    settle()
                    then(nc.vector.tensor_tensor(cur, cur, ps[:, 3 * D:4 * D], ALU.add))
                    then(nc.vector.tensor_scalar(q[:, u, :], q[:, u, :], C ** -0.5, None, ALU.mult))
                    settle()
                    then(nc.vector.tensor_copy(part[0], q[:, u, :]))
                    settle()
                    then(nc.vector.tensor_tensor(rest[:, u, :], q[:, u, :], part[0], ALU.subtract))
                    settle()
                    then(nc.vector.tensor_copy(part[1], rest[:, u, :]))
                    settle()
                    then(nc.vector.tensor_tensor(part[2], rest[:, u, :], part[1], ALU.subtract))
                project(nc, "qkv", c, H, [(wq, 0), (wk, D), (wv, 2 * D), (wskip, 3 * D)], [(bq, 0), (bk, D), (bv, 2 * D), (bskip, 3 * D)],
                        4 * D, 10, handle, [(tables[0], K), (tables[1], V)])
            scores = loc.sb("scores", [P, ETX, HEADS])
            most = loc.sb("most", [P, NT, HEADS])
            most2 = loc.sb("most2", [P, NT, 2 * HEADS], BF16)
            attention_scores(nc, c, tables[0], Q3, by_dst, scores, most)

            def split_most(r, then):
                then(nc.vector.tensor_copy(most2[:, :, 0:HEADS], most[:, :, :]))
                then(nc.vector.tensor_tensor(most2[:, :, HEADS:], most[:, :, :], most2[:, :, 0:HEADS], ALU.subtract))
            small_phase(nc, "split_most", None, split_most)
            total = loc.sb("total", [P, NT, AW])
            attend(nc, c, tables[1], by_dst, total, scores, most2)
            join_attention(nc, total, U, X)
        one_expert = (w1.rearrange("(o d) f -> o d f", o=1), b1.rearrange("(o f) -> o f", o=1),
                      w2.rearrange("(o f) d -> o f d", o=1), b2.rearrange("(o d) -> o d", o=1))
        with ExitStack() as part:
            loc = Scope(nc, part, "ff1")
            H, uT = loc.sb("H", [P, NT, D]), loc.sb("uT", [P, KD, NT * P])
            layer_norm(nc, "ln_2", U, H, ln2_w, ln2_b)
            turn_nodes(nc, "turn_1", c, H, uT)
            feed_forward(nc, "ffn_1", uT, X, 2 * D, 1, one_expert, lambda t, e, s: c["ones"][:, 0:1])

        with ExitStack() as part:
            loc = Scope(nc, part, "ff2")
            uT = loc.sb("uT", [P, KD, NT * P])
            chosen, gate = loc.sb("chosen", [1, 2], I32), loc.sb("gate", [P, 2])
            layer_norm(nc, "ln_x1", X, U)
            route_all(nc, c, U, fWr, fbr, chosen, gate)
            turn_nodes(nc, "turn_2", c, U, uT)
            feed_forward(nc, "ffn_2", uT, U, 2 * D, 2, (fW1, fb1, fW2, fb2), lambda t, e, s: gate[:, s:s + 1], chosen=chosen)
            layer_norm(nc, "ln_3", U, U, gamma, beta, add_to=X)

        with ExitStack() as part:
            loc = Scope(nc, part, "hyper")
            place = places(loc)
            rank_edges(nc, "rank_src", src, dst, c, place, by_src)
            H, total = loc.sb("H", [P, NT, D]), loc.sb("total", [P, NT, AW])
            layer_norm(nc, "ln_x2", X, U)

            def handle(u, t, ps, biases, then, settle):
                then(nc.vector.tensor_copy(flat(H[:, at(t), :]), ps[:, :]))
            project(nc, "conv_1", c, U, [(hW1, 0)], [], D, 1, handle, [(tables[2], H)])
            edge_sums(nc, "to_dst_1", c, tables[2], by_dst, total, place=place, sorting=by_src)
            divide_by_count(nc, "mean_1", total, table=tables[3])
            edge_sums(nc, "to_src_1", c, tables[3], by_src, total)
            divide_by_count(nc, "act_1", total, bias=hb1, slope=slope, dest=H)
            project(nc, "conv_2", c, H, [(hW2, 0)], [], D, 1, handle, [(tables[4], H)])
            edge_sums(nc, "to_dst_2", c, tables[4], by_dst, total)
            divide_by_count(nc, "mean_2", total, table=tables[5])
            edge_sums(nc, "to_src_2", c, tables[5], by_src, total)
            divide_by_count(nc, "act_2", total, bias=hb2, slope=slope, residual=U, add_to=X)

        with ExitStack() as part:
            loc = Scope(nc, part, "moe")
            gate = loc.sb("gate", [P, NT, 2])
            logits = loc.sb("logits", [P, NT, EXPERTS])
            put, get = loc.sb("put", [P, NT, 2], I32), loc.sb("get", [P, NT, 2], I32)
            expert_of = loc.sb("expert_of", [1, BATCHES], I32)
            layer_norm(nc, "ln_x3", X, U)

            def handle(u, t, ps, biases, then, settle):
                then(nc.vector.tensor_copy(flat(logits[:, at(t), :]), ps[:, :]))
            project(nc, "logits", c, U, [(mWr, 0)], [], EXPERTS, 1, handle, [])
            route_each(nc, c, logits, mbr, gate, put, get, expert_of)
            layer_norm(nc, "ln_4", U, U)
            run_experts(nc, c, U, put, expert_of, (mW1, mb1, mW2, mb2), (ln_g, ln_b), batch_in, batch_out)
            join_experts(nc, batch_out, get, gate, X, out)


_INS = ["x", "src", "dst", "L0_gnn_ln1_w", "L0_gnn_ln1_b", "L0_gnn_ln2_w", "L0_gnn_ln2_b", "L0_gnn_wq", "L0_gnn_bq",
        "L0_gnn_wk", "L0_gnn_bk", "L0_gnn_wv", "L0_gnn_bv", "L0_gnn_wskip", "L0_gnn_bskip", "L0_gnn_w1", "L0_gnn_b1",
        "L0_gnn_w2", "L0_gnn_b2", "L0_ffn_Wr", "L0_ffn_br", "L0_ffn_W1", "L0_ffn_b1", "L0_ffn_W2", "L0_ffn_b2",
        "L0_ffn_gamma", "L0_ffn_beta", "L1_gnn_W1", "L1_gnn_b1", "L1_gnn_W2", "L1_gnn_b2", "L1_gnn_a", "L1_ffn_Wr",
        "L1_ffn_br", "L1_ffn_ln_g", "L1_ffn_ln_b", "L1_ffn_W1", "L1_ffn_b1", "L1_ffn_W2", "L1_ffn_b2"]


def kernel(**inputs):
    import numpy as _np
    import concourse.bacc as _bacc
    from concourse import mybir as _mybir
    from concourse.bass_utils import run_bass_kernel_spmd as _run

    nc = _bacc.Bacc("TRN2", target_bir_lowering=False, num_devices=1)
    arrays, args = {}, []
    for name in _INS:
        a = _np.ascontiguousarray(inputs[name])
        arrays[f"in_{name}_dram"] = a
        args.append(nc.dram_tensor(f"in_{name}_dram", a.shape, _mybir.dt.from_np(a.dtype), kind="ExternalInput").ap())
    args.append(nc.dram_tensor("out_0_dram", (N, D), F32, kind="ExternalOutput").ap())
    program(nc, *args)
    r = _run(nc, [arrays], core_ids=[0])
    return r.results[0]["out_0_dram"]
```
